# Optimizing a Trainium2 kernel written in Bass

```python
import numpy as np
import jax
import jax.numpy as jnp

def _softmax(x, axis=-1):
    return jax.nn.softmax(x, axis=axis)

def _gelu(x):
    return jax.nn.gelu(x, approximate=True)

def _silu(x):
    return jax.nn.silu(x)

def _sigmoid(x):
    return jax.nn.sigmoid(x)

def _layernorm(x, axis=-1, eps=1e-05):
    m = jnp.mean(x, axis=axis, keepdims=True)
    v = jnp.var(x, axis=axis, keepdims=True)
    return (x - m) / jnp.sqrt(v + eps)

def _scatter_add(tgt, idx, src, axis=0):
    return tgt.at[idx].add(src)

def _segment_sum(src, seg, n):
    return jax.ops.segment_sum(src, seg, n)
kernel_name = 'mk_gnn_ffn_d2_gnn_r8_5d7cdc'

def setup_inputs(seed: int=0):
    np.random.seed(seed)
    _w = jnp.asarray

    def _rec_inputs():
        import jax
        import jax.numpy as jnp
        _gk = jax.random.key(seed)
        x = -0.0002117 + 1 * jax.random.normal(jax.random.fold_in(_gk, 1), (1250, 1024), jnp.float32)
        _s = jax.random.randint(jax.random.fold_in(_gk, 2), (10000,), 0, 1250, jnp.int32)
        _d = jax.random.randint(jax.random.fold_in(_gk, 3), (10000,), 0, 1250, jnp.int32)
        _loop = jnp.arange(1250, dtype=jnp.int32)
        src = jnp.concatenate([_s, _d, _loop])
        dst = jnp.concatenate([_d, _s, _loop])
        _o = jnp.argsort(dst, stable=True)
        src = src[_o]
        dst = dst[_o]
        return (x, src, dst)
    x, src, dst = _rec_inputs()

    def _L0_gnn_setup():
        import jax, jax.numpy as jnp
        import numpy as np
        N_NODES = 3125
        N_EDGES = 50000
        D = 1024

        def _sage_layer(h, edge_src, edge_dst, deg_inv, W_self, W_neigh, b):
            msg = h[edge_src]
            agg = jax.ops.segment_sum(msg, edge_dst, num_segments=h.shape[0])
            mean = agg * deg_inv[:, None]
            return h @ W_self + mean @ W_neigh + b
        key = jax.random.key(seed)
        ks = jax.random.split(key, 8)
        s = 1.0 / np.sqrt(D)
        return {'x': jax.random.normal(ks[0], (N_NODES, D), dtype=jnp.float32), 'edge_src': jax.random.randint(ks[1], (N_EDGES,), 0, N_NODES, dtype=jnp.int32), 'edge_dst': jax.random.randint(ks[2], (N_EDGES,), 0, N_NODES, dtype=jnp.int32), 'W_self0': jax.random.normal(ks[3], (D, D), dtype=jnp.float32) * s, 'W_neigh0': jax.random.normal(ks[4], (D, D), dtype=jnp.float32) * s, 'b0': jnp.zeros((D,), dtype=jnp.float32), 'W_self1': jax.random.normal(ks[5], (D, D), dtype=jnp.float32) * s, 'W_neigh1': jax.random.normal(ks[6], (D, D), dtype=jnp.float32) * s, 'b1': jnp.zeros((D,), dtype=jnp.float32)}
    _L0_gnn_all = _L0_gnn_setup()
    _L0_gnn_in = {k: v for k, v in _L0_gnn_all.items() if k in ('W_self0', 'W_neigh0', 'b0', 'W_self1', 'W_neigh1', 'b1')}
    del _L0_gnn_all

    def _L0_ffn_setup():
        import jax, jax.numpy as jnp
        import numpy as np
        OUT_FEATURES = 512
        IN_FEATURES = 512

        def _unfold_tt(G1, G2):
            W = jnp.einsum('abcd,cefg->abefdg', G1, G2)
            return W.reshape(OUT_FEATURES, IN_FEATURES)
        key = jax.random.key(seed)
        ks = jax.random.split(key, 5)
        std = np.sqrt(2.0 / IN_FEATURES).astype(np.float32)
        x = jax.random.normal(ks[0], (8, 512, 2 * IN_FEATURES), dtype=jnp.float32)
        G1_R = jax.random.uniform(ks[1], (1, 32, 4, 32), jnp.float32, -std, std)
        G2_R = jax.random.uniform(ks[2], (4, 16, 1, 16), jnp.float32, -std, std)
        G1_I = jax.random.uniform(ks[3], (1, 32, 4, 32), jnp.float32, -std, std)
        G2_I = jax.random.uniform(ks[4], (4, 16, 1, 16), jnp.float32, -std, std)
        bias_real = jnp.zeros((OUT_FEATURES,), jnp.float32)
        bias_imag = jnp.zeros((OUT_FEATURES,), jnp.float32)
        return {'x': x, 'G1_R': G1_R, 'G2_R': G2_R, 'G1_I': G1_I, 'G2_I': G2_I, 'bias_real': bias_real, 'bias_imag': bias_imag}
    _L0_ffn_all = _L0_ffn_setup()
    _L0_ffn_in = {k: v for k, v in _L0_ffn_all.items() if k in ('G1_R', 'G2_R', 'G1_I', 'G2_I', 'bias_real', 'bias_imag')}
    del _L0_ffn_all

    def _L1_gnn_setup():
        import jax, jax.numpy as jnp
        import numpy as np
        NEG_SLOPE = 0.1
        EPS = 1e-05
        key = jax.random.key(seed)
        k1, k2, k3, k4, k5 = jax.random.split(key, 5)
        N, E, DIN, DOUT = (1250, 20000, 1024, 1024)
        x = jax.random.normal(k1, (N, DIN), dtype=jnp.float32)
        W = jax.random.normal(k2, (DIN, DOUT), dtype=jnp.float32) * 0.02
        a = jax.random.normal(k3, (1, 2 * DOUT), dtype=jnp.float32) * 0.02
        src = jax.random.randint(k4, (E,), 0, N, dtype=jnp.int64)
        dst = jax.random.randint(k5, (E,), 0, N, dtype=jnp.int64)
        return {'x': x, 'W': W, 'a': a, 'src': src, 'dst': dst}
    _L1_gnn_all = _L1_gnn_setup()
    _L1_gnn_in = {k: v for k, v in _L1_gnn_all.items() if k in ('W', 'a')}
    del _L1_gnn_all

    def _L1_ffn_setup():
        import jax, jax.numpy as jnp
        import numpy as np
        DIM = 1024
        HID = 352
        E = 8
        TOP_K = 2
        EPS = 1e-06

        def _rmsnorm(x, w):
            var = jnp.mean(jnp.square(x), axis=-1, keepdims=True)
            return x * jax.lax.rsqrt(var + EPS) * w
        key = jax.random.key(seed)
        ks = jax.random.split(key, 5)
        x = jax.random.normal(ks[0], (4, 256, DIM), dtype=jnp.float32)
        norm_weight = jnp.ones((DIM,), dtype=jnp.float32)
        router_weight = jax.random.normal(ks[1], (E, DIM), dtype=jnp.float32) * 0.02
        gate_up_weight = jax.random.normal(ks[2], (E, 2 * HID, DIM), dtype=jnp.float32) * (0.02 / np.sqrt(E))
        down_weight = jax.random.normal(ks[3], (E, DIM, HID), dtype=jnp.float32) * (0.02 / np.sqrt(E))
        residual_alpha = jnp.float32(1.0)
        return {'x': x, 'norm_weight': norm_weight, 'router_weight': router_weight, 'gate_up_weight': gate_up_weight, 'down_weight': down_weight, 'residual_alpha': residual_alpha}
    _L1_ffn_all = _L1_ffn_setup()
    _L1_ffn_in = {k: v for k, v in _L1_ffn_all.items() if k in ('norm_weight', 'router_weight', 'gate_up_weight', 'down_weight', 'residual_alpha')}
    del _L1_ffn_all
    return {'x': x, 'src': src, 'dst': dst, 'L0_gnn_W_self0': _L0_gnn_in['W_self0'], 'L0_gnn_W_neigh0': _L0_gnn_in['W_neigh0'], 'L0_gnn_b0': _L0_gnn_in['b0'], 'L0_gnn_W_self1': _L0_gnn_in['W_self1'], 'L0_gnn_W_neigh1': _L0_gnn_in['W_neigh1'], 'L0_gnn_b1': _L0_gnn_in['b1'], 'L0_ffn_G1_R': _L0_ffn_in['G1_R'], 'L0_ffn_G2_R': _L0_ffn_in['G2_R'], 'L0_ffn_G1_I': _L0_ffn_in['G1_I'], 'L0_ffn_G2_I': _L0_ffn_in['G2_I'], 'L0_ffn_bias_real': _L0_ffn_in['bias_real'], 'L0_ffn_bias_imag': _L0_ffn_in['bias_imag'], 'L1_gnn_W': _L1_gnn_in['W'], 'L1_gnn_a': _L1_gnn_in['a'], 'L1_ffn_norm_weight': _L1_ffn_in['norm_weight'], 'L1_ffn_router_weight': _L1_ffn_in['router_weight'], 'L1_ffn_gate_up_weight': _L1_ffn_in['gate_up_weight'], 'L1_ffn_down_weight': _L1_ffn_in['down_weight'], 'L1_ffn_residual_alpha': _L1_ffn_in['residual_alpha']}

def reference(x, src, dst, L0_gnn_W_self0, L0_gnn_W_neigh0, L0_gnn_b0, L0_gnn_W_self1, L0_gnn_W_neigh1, L0_gnn_b1, L0_ffn_G1_R, L0_ffn_G2_R, L0_ffn_G1_I, L0_ffn_G2_I, L0_ffn_bias_real, L0_ffn_bias_imag, L1_gnn_W, L1_gnn_a, L1_ffn_norm_weight, L1_ffn_router_weight, L1_ffn_gate_up_weight, L1_ffn_down_weight, L1_ffn_residual_alpha):
    import jax
    import jax.numpy as jnp

    def _L0_gnn_ref(x, edge_src, edge_dst, W_self0, W_neigh0, b0, W_self1, W_neigh1, b1):
        import jax, jax.numpy as jnp
        import numpy as np
        N_NODES = 3125
        N_EDGES = 50000
        D = 1024

        def _sage_layer(h, edge_src, edge_dst, deg_inv, W_self, W_neigh, b):
            msg = h[edge_src]
            agg = jax.ops.segment_sum(msg, edge_dst, num_segments=h.shape[0])
            mean = agg * deg_inv[:, None]
            return h @ W_self + mean @ W_neigh + b
        N = x.shape[0]
        deg = jax.ops.segment_sum(jnp.ones_like(edge_dst, dtype=x.dtype), edge_dst, num_segments=N)
        deg_inv = 1.0 / jnp.maximum(deg, 1.0)
        h = jax.nn.relu(_sage_layer(x, edge_src, edge_dst, deg_inv, W_self0, W_neigh0, b0))
        out = _sage_layer(h, edge_src, edge_dst, deg_inv, W_self1, W_neigh1, b1)
        return out

    def _L0_ffn_ref(x, G1_R, G2_R, G1_I, G2_I, bias_real, bias_imag):
        import jax, jax.numpy as jnp
        import numpy as np
        OUT_FEATURES = 512
        IN_FEATURES = 512

        def _unfold_tt(G1, G2):
            W = jnp.einsum('abcd,cefg->abefdg', G1, G2)
            return W.reshape(OUT_FEATURES, IN_FEATURES)
        W_real = _unfold_tt(G1_R, G2_R)
        W_imag = _unfold_tt(G1_I, G2_I)
        x_real, x_imag = jnp.split(x, 2, axis=-1)
        out_real = x_real @ W_real.T - x_imag @ W_imag.T + bias_real
        out_imag = x_real @ W_imag.T + x_imag @ W_real.T + bias_imag
        return jnp.concatenate([out_real, out_imag], axis=-1)

    def _L1_gnn_ref(x, W, a, src, dst):
        import jax, jax.numpy as jnp
        import numpy as np
        NEG_SLOPE = 0.1
        EPS = 1e-05
        N = x.shape[0]
        d = W.shape[1]
        h = x @ W
        a_l, a_r = (a[0, :d], a[0, d:])
        al = h @ a_l
        ar = h @ a_r
        e = jnp.exp(-jax.nn.leaky_relu(al[src] + ar[dst], negative_slope=NEG_SLOPE))
        rowsum = jax.ops.segment_sum(e, src, num_segments=N)
        h_prime = jax.ops.segment_sum(e[:, None] * h[dst], src, num_segments=N)
        h_prime = h_prime / (rowsum[:, None] + EPS)
        return jax.nn.elu(h_prime)

    def _L1_ffn_ref(x, norm_weight, router_weight, gate_up_weight, down_weight, residual_alpha):
        import jax, jax.numpy as jnp
        import numpy as np
        DIM = 1024
        HID = 352
        E = 8
        TOP_K = 2
        EPS = 1e-06

        def _rmsnorm(x, w):
            var = jnp.mean(jnp.square(x), axis=-1, keepdims=True)
            return x * jax.lax.rsqrt(var + EPS) * w
        normed = _rmsnorm(x, norm_weight)
        logits = jnp.einsum('bsd,ed->bse', normed, router_weight)
        probs = jax.nn.softmax(logits, axis=-1)
        topk_w, topk_idx = jax.lax.top_k(probs, TOP_K)
        topk_w = topk_w / jnp.sum(topk_w, axis=-1, keepdims=True)
        combine = jnp.sum(jax.nn.one_hot(topk_idx, E, dtype=normed.dtype) * topk_w[..., None], axis=-2)
        moe_out = jnp.zeros_like(x)
        for e in range(E):
            gu = jnp.einsum('bsd,hd->bsh', normed, gate_up_weight[e])
            gate, up = (gu[..., :HID], gu[..., HID:])
            hidden = jax.nn.silu(gate) * up
            out_e = jnp.einsum('bsh,dh->bsd', hidden, down_weight[e])
            moe_out = moe_out + combine[..., e, None] * out_e
        alpha = jnp.clip(residual_alpha, -0.5, 2.0)
        return x + alpha * moe_out
    x = x + _L0_gnn_ref(_layernorm(x, axis=-1), src, dst, L0_gnn_W_self0, L0_gnn_W_neigh0, L0_gnn_b0, L0_gnn_W_self1, L0_gnn_W_neigh1, L0_gnn_b1)
    x = x + _L0_ffn_ref(_layernorm(x, axis=-1)[None], L0_ffn_G1_R, L0_ffn_G2_R, L0_ffn_G1_I, L0_ffn_G2_I, L0_ffn_bias_real, L0_ffn_bias_imag)[0]
    x = x + _L1_gnn_ref(_layernorm(x, axis=-1), L1_gnn_W, L1_gnn_a, src, dst)
    x = x + _L1_ffn_ref(_layernorm(x, axis=-1)[None], L1_ffn_norm_weight, L1_ffn_router_weight, L1_ffn_gate_up_weight, L1_ffn_down_weight, L1_ffn_residual_alpha)[0]
    return x

_drawn_inputs = setup_inputs


def setup_inputs(seed=0):
    import zlib

    import numpy as np

    out = dict(_drawn_inputs(seed))
    spreads = {'L0_gnn_b0': (0.0, 0.1),
     'L0_gnn_b1': (0.0, 0.1),
     'L0_ffn_bias_real': (0.0, 0.1),
     'L0_ffn_bias_imag': (0.0, 0.1),
     'L1_ffn_norm_weight': (1.0, 0.6)}
    factors = {'L1_gnn_a': 3.036,
     'L1_ffn_router_weight': 8.0,
     'L1_ffn_gate_up_weight': 8.0,
     'L1_ffn_down_weight': 8.0}
    for name, (base, spread) in spreads.items():
        noise = np.random.default_rng([zlib.crc32(name.encode()), seed]).standard_normal(out[name].shape)
        drawn = base * np.exp(spread * noise) if base else spread * noise
        out[name] = jnp.asarray(drawn.astype(out[name].dtype))
    for name, factor in factors.items():
        out[name] = (out[name] * factor).astype(out[name].dtype)
    return out
```

```python
import numpy as np
import concourse.bass as bass
from concourse import mybir
from contextlib import ExitStack

F32 = mybir.dt.float32
F32R = mybir.dt.float32r
ALU = mybir.AluOpType
ACT = mybir.ActivationFunctionType
AX = mybir.AxisListType
N, P, D = 1250, 125, 1024
T, K, H = N // P, D // 128, D // 2

BASE = 16512
W_BYTES = K * D * 4
G_BYTES = T * D * 4
RAW_AT = 0
WH_AT = RAW_AT + W_BYTES
WL_AT = WH_AT + W_BYTES
GH_AT = WL_AT + W_BYTES
GL_AT = GH_AT + G_BYTES
LOCAL_AT = GL_AT + G_BYTES


class Map:

    def __init__(self, nc, at, name):
        self.nc, self.at, self.name = nc, at, name

    def __call__(self, name, shape, dt=F32):
        words = 1
        for s in shape[1:]:
            words *= s
        t = self.nc.alloc_sbuf_tensor_at(f"{self.name}_{name}", shape, dt, offset=BASE + self.at)
        self.at += -(-words * 4 // 32) * 32
        return t


def node_rows(x, t):
    return x[bass.ds(t * P, P), :]


def project_phase(nc, name, rows, xt_out, raw, wh, wl, gh, gl, raw_loaded, loads, next_w,
                  normalize, relu, result, bias=None, out=None, score_w=None, scores=None):
    sem = lambda s: nc.alloc_semaphore(f"{name}_{s}")
    with ExitStack() as ctx:
        ps = lambda s, shape: ctx.enter_context(nc.psum_tensor(f"{name}_{s}", shape, F32))
        local = Map(nc, LOCAL_AT, name)
        xt = [local(f"xt{u}", [128, 2, K, P], F32R) for u in range(2)]
        if result == "residual":
            local = Map(nc, GH_AT, name)
            bias_row = local("bias_row", [P, D])
            biased = [local(f"biased{u}", [P, D]) for u in range(2)]
            xn = local("xn", [P, D])
            y = [local(f"y{u}", [P, D]) for u in range(2)]
        x = [local(f"x{u}", [P, D]) for u in range(2)]
        if result != "residual":
            xn = None
        ident = local("ident", [P, P])
        square = local("square", [P, P], mybir.dt.int32)
        power = local("power", [P, 1])
        eps = local("eps", [P, 1])
        waits = local("waits", [P, 1])
        stats = [local(f"stats{u}", [P, 12]) for u in range(2)]
        moments = [local(f"moments{u}", [P, 2]) for u in range(2)]
        rstd = [local(f"rstd{u}", [P, 1]) for u in range(2)]
        if result == "scores":
            score_parts = local("score_parts", [P, 2, 2, 2])
            scores_sb = local("scores_sb", [P, T, 2])
        acc = [[ps(f"acc{u}{j}", [128, 512]) for j in range(2)] for u in range(2)]
        turned = [ps(f"turned{r}", [128, 4, P]) for r in range(2)]

        x_loaded = [sem(f"x_loaded{u}") for u in range(2)]
        xt_high = sem("xt_high")
        xt_low = sem("xt_low")
        if xt_out is not None:
            xt_stored = [sem(f"xt_stored{u}") for u in range(2)]
        if normalize:
            stats_ready = sem("stats_ready")
            moments_ready = sem("moments_ready")
            rstd_ready = sem("rstd_ready")
            var_eps = sem("var_eps")
            xn_ready = sem("xn_ready")
        turned_ready = sem("turned_ready")
        acc_ready = sem("acc_ready")
        if result != "residual":
            acc_high = sem("acc_high")
            acc_free = sem("acc_free")
        w_high = sem("w_high")
        w_low = sem("w_low")
        made = sem("made")
        ident_ready = sem("ident_ready")
        if result != "split":
            extra = sem("extra")
        if result == "scores":
            scored = sem("scored")
            score_ready = sem("score_ready")
            finished = sem("finished")
        if result == "residual":
            biased_ready = sem("biased_ready")
            y_ready = sem("y_ready")
            y_stored = [sem(f"y_stored{u}") for u in range(2)]

        def xn_of(u):
            return x[u] if xn is None else xn

        block = ctx.enter_context(nc.Block())

        @block.sync
        def _(sp):
            if bias is not None:
                sp.dma_start(bias_row[:, :], bias.broadcast_to([P, D])).then_inc(extra, 16)

            def load(t, u, pair):
                if pair is not None:
                    sp.wait_ge(turned_ready, t - 1)
                    if result == "residual":
                        sp.wait_ge(biased_ready, t - 1)
                sp.dma_start(x[u][:, :], node_rows(rows, t)).then_inc(x_loaded[u], 16)

            def store(t, u):
                if xt_out is not None:
                    sp.wait_ge(xt_low, t + 1)
                    sp.dma_start(xt_out[bass.ds(t, 1), :, :, :, :].rearrange("o p a k n -> (o p) a k n"),
                                 xt[u][:, :, :, :].bitcast(F32)).then_inc(xt_stored[u], 16)
                if result == "residual":
                    sp.wait_ge(y_ready, 2 * t + 2)
                    sp.dma_start(node_rows(out, t), y[u][:, :]).then_inc(y_stored[u], 16)

            load(0, 0, None)
            load(1, 1, None)
            with sp.Fori(0, T // 2 - 1) as pair:
                for u in range(2):
                    load(pair * 2 + (u + 2), u, pair)
                    store(pair * 2 + u, u)
            for t in (T - 2, T - 1):
                store(t, t % 2)
            if xt_out is not None:
                for u in range(2):
                    sp.wait_ge(xt_stored[u], 16 * (T // 2))
            if result == "residual":
                for u in range(2):
                    sp.wait_ge(y_stored[u], 16 * (T // 2))
            if result == "scores":
                sp.wait_ge(score_ready, T)
                sp.dma_start(scores, scores_sb[:, :, :]).then_inc(finished, 16)
                sp.wait_ge(finished, 16)

        @block.gpsimd
        def _(pool):
            pool.iota(square[:, :], pattern=[[1, P]], base=0, channel_multiplier=-1).then_inc(made, 1)
            pool.memset(power[:, :], -0.5).then_inc(made, 1)
            pool.memset(eps[:, :], 1e-5).then_inc(made, 1)
            pool.wait_ge(made, 3)
            def tile(t, u, pair):
                if normalize:
                    pool.wait_ge(moments_ready, t + 1)
                    pool.tensor_tensor(rstd[u][:, :], moments[u][:, 1:2], eps[:, :], ALU.add).then_inc(var_eps, 1)
                    pool.wait_ge(var_eps, t + 1)
                    pool.tensor_tensor(rstd[u][:, :], rstd[u][:, :], power[:, :], ALU.pow).then_inc(rstd_ready, 1)
                if result == "residual":
                    pool.wait_ge(x_loaded[u], pair * 16 + 16)
                    if not (isinstance(pair, int) and pair == 0):
                        pool.wait_ge(y_ready, 2 * t - 2)
                    pool.tensor_tensor(biased[u][:, :], x[u][:, :], bias_row[:, :], ALU.add).then_inc(biased_ready, 1)

            if result == "residual":
                pool.wait_ge(extra, 16)
            if normalize or result == "residual":
                tile(0, 0, 0)
                tile(1, 1, 0)
                with pool.Fori(1, T // 2) as pair:
                    for u in range(2):
                        tile(pair * 2 + u, u, pair)

        @block.scalar
        def _(act):
            def turn(t, u, pair):
                act.wait_ge(turned_ready, t + 1)
                if not (isinstance(pair, int) and pair == 0):
                    act.wait_ge(acc_ready, 2 * t - 2)
                    if xt_out is not None:
                        act.wait_ge(xt_stored[u], 16 * pair)
                for r in range(2):
                    act.activation(xt[u][:, 0, 4 * r:4 * r + 4, :], turned[r][:, :, :],
                                         ACT.Relu if relu else ACT.Copy).then_inc(xt_high, 1)

            def result_of(t, u):
                for j in range(2):
                    if result == "residual":
                        continue
                    act.wait_ge(acc_ready, 2 * t + j + 1)
                    act.activation(gh[0:P, bass.ds(t, 1), j * H:(j + 1) * H].rearrange("p o n -> p (o n)"),
                                   acc[u][j][0:P, :], ACT.Copy).then_inc(acc_high, 1)

            turn(0, 0, 0)
            act.wait_ge(raw_loaded, 16 * loads)
            for k in range(K):
                act.activation(wh[:, k, :], raw[:, k, :], ACT.Copy).then_inc(w_high, 1)
            turn(1, 1, 0)
            if next_w is not None:
                act.wait_ge(w_low, K)
                act.dma_start(raw[:, :, :], next_w.rearrange("(k p) n -> p k n", p=128)).then_inc(raw_loaded, 16)
            if result == "scores":
                act.wait_ge(w_low, K)
                act.dma_start(raw[0:P, 0:2, :].rearrange("p c n -> p (c n)"), score_w.broadcast_to([P, 2 * D])).then_inc(extra, 16)
            result_of(0, 0)
            with act.Fori(0, T // 2 - 1) as pair:
                for u in range(2):
                    turn(pair * 2 + (u + 2), u, pair + 1)
                    result_of(pair * 2 + (u + 1), 1 - u)
            result_of(T - 1, 1)

        @block.vector
        def _(dve):
            dve.wait_ge(made, 3)
            dve.tensor_scalar(ident[:, :], square[:, :], 0.0, None, ALU.is_equal).then_inc(ident_ready, 1)

            def norm(t, u, pair):
                dve.wait_ge(x_loaded[u], 16 * (pair + 1))
                if not normalize:
                    return
                for j in range(2):
                    dve.bn_stats(stats[u][:, 6 * j:6 * j + 6], x[u][:, j * H:(j + 1) * H]).then_inc(stats_ready, 1)
                dve.wait_ge(stats_ready, 2 * t + 2)
                dve.memset(waits[:, :], 0.0)
                dve.bn_aggr(moments[u][:, :], stats[u][:, :]).then_inc(moments_ready, 1)
                dve.wait_ge(rstd_ready, t + 1)
                if xn is not None:
                    dve.wait_ge(turned_ready, t)
                dve.tensor_scalar(xn_of(u)[:, :], x[u][:, :], moments[u][:, 0:1], rstd[u][:, 0:1],
                                  ALU.subtract, ALU.mult).then_inc(xn_ready, 1)

            def turn(t, u):
                for r in range(2):
                    dve.wait_ge(xt_high, 2 * t + r + 1)
                    low, high = xt[u][:, 1, 4 * r:4 * r + 4, :], xt[u][:, 0, 4 * r:4 * r + 4, :].bitcast(F32)
                    if relu:
                        ins = dve.scalar_tensor_tensor(low, turned[r][:, :, :], 0.0, high, ALU.max, ALU.subtract)
                    else:
                        ins = dve.tensor_tensor(low, turned[r][:, :, :], high, ALU.subtract)
                ins.then_inc(xt_low, 1)

            def result_of(t, u, pair):
                for j in range(2):
                    cols = slice(j * H, (j + 1) * H)
                    if result == "residual":
                        dve.wait_ge(acc_ready, 2 * t + j + 1)
                        if j == 0:
                            dve.wait_ge(biased_ready, t + 1)
                            dve.wait_ge(y_stored[u], 16 * pair)
                        dve.tensor_tensor(y[u][:, cols], acc[u][j][0:P, :], biased[u][:, cols], ALU.add).then_inc(y_ready, 1)
                    else:
                        dve.wait_ge(acc_high, 2 * t + j + 1)
                        if result == "scores":
                            for c in range(2):
                                dve.wait_ge(scored, 4 * t)
                                dve.tensor_tensor_reduce(raw[0:P, 2 + 2 * j + c, 0:H], acc[u][j][0:P, :], raw[0:P, c, cols],
                                                         1.0, 0.0, ALU.mult, ALU.add,
                                                         score_parts[:, u, c, j:j + 1]).then_inc(scored, 1)
                        high = gh[0:P, bass.ds(t, 1), cols].rearrange("p o n -> p (o n)")
                        low = gl[0:P, bass.ds(t, 1), cols].rearrange("p o n -> p (o n)")
                        dve.tensor_tensor(low, acc[u][j][0:P, :], high.bitcast(F32), ALU.subtract).then_inc(acc_free, 1)
                if result == "scores":
                    dve.wait_ge(scored, 4 * t + 4)
                    dve.tensor_tensor(scores_sb[:, bass.ds(t, 1), :].rearrange("p o c -> p (o c)"), score_parts[:, u, :, 0],
                                      score_parts[:, u, :, 1], ALU.add).then_inc(score_ready, 1)

            norm(0, 0, 0)
            turn(0, 0)
            for k in range(K):
                dve.wait_ge(w_high, k + 1)
                dve.tensor_tensor(wl[:, k, :], raw[:, k, :], wh[:, k, :].bitcast(F32), ALU.subtract).then_inc(w_low, 1)
            norm(1, 1, 0)
            turn(1, 1)
            if result == "scores":
                dve.wait_ge(extra, 16)
            with dve.Fori(0, T // 2 - 1) as pair:
                for u in range(2):
                    norm(pair * 2 + (u + 2), u, pair + 1)
                    result_of(pair * 2 + u, u, pair)
                    turn(pair * 2 + (u + 2), u)
            for t in (T - 2, T - 1):
                result_of(t, t % 2, T // 2 - 1)

        @block.tensor
        def _(pe):
            pe.wait_ge(ident_ready, 1)

            def turn(t, u, pair):
                if normalize:
                    pe.wait_ge(xn_ready, t + 1)
                else:
                    pe.wait_ge(x_loaded[u], 16 * (pair + 1))
                pe.wait_ge(xt_low, t)
                for k in range(K):
                    ins = pe.transpose(turned[k // 4][:, k % 4, :], xn_of(u)[:, k * 128:(k + 1) * 128], ident[:, :])
                    if k == K - 1:
                        ins.then_inc(turned_ready, 1)

            def products(t, u, j, first):
                if not first:
                    pe.wait_ge(y_ready if result == "residual" else acc_free, 2 * t + j - 3)
                if j == 0:
                    pe.wait_ge(xt_low, t + 1)
                for k in range(K):
                    if isinstance(t, int) and t == 0 and j == 0:
                        pe.wait_ge(w_low, k + 1)
                    cols = slice(j * H, (j + 1) * H)
                    pe.matmul(acc[u][j][0:P, :], xt[u][:, 0, k, :], wh[:, k, cols], start=k == 0, stop=False)
                    pe.matmul(acc[u][j][0:P, :], xt[u][:, 0, k, :], wl[:, k, cols], start=False, stop=False)
                    ins = pe.matmul(acc[u][j][0:P, :], xt[u][:, 1, k, :], wh[:, k, cols], start=False, stop=k == K - 1)
                ins.then_inc(acc_ready, 1)

            turn(0, 0, 0)
            products(0, 0, 0, True)
            turn(1, 1, 0)
            products(0, 0, 1, True)
            products(1, 1, 0, True)
            turn(2, 0, 1)
            products(1, 1, 1, True)
            with pe.Fori(1, T // 2 - 1) as pair:
                for u in range(2):
                    t = pair * 2 + u
                    products(t, u, 0, False)
                    turn(t + 1, 1 - u, pair + u)
                    products(t, u, 1, False)
            products(T - 2, 0, 0, False)
            turn(T - 1, 1, T // 2 - 1)
            products(T - 2, 0, 1, False)
            products(T - 1, 1, 0, False)
            products(T - 1, 1, 1, False)


def aggregate_phase(nc, name, xt_in, counts_by_src, deg_inv, bias, residual, out, raw, wh, wl, gh, gl,
                    raw_loaded, loads, next_w):
    sem = lambda s: nc.alloc_semaphore(f"{name}_{s}")
    with ExitStack() as ctx:
        ps = lambda s, shape: ctx.enter_context(nc.psum_tensor(f"{name}_{s}", shape, F32))
        local = Map(nc, LOCAL_AT, name)
        xt = local("xt", [128, 2, K, P], F32R)
        counts = local("counts", [P, T, P], F32R)
        bias_row = local("bias_row", [P, D])
        x = local("x", [P, D]) if residual is not None else None
        mean = [local(f"mean{j}", [P, H]) for j in range(2)]
        y = local("y", [P, D])
        dinv = local("dinv", [P, T])
        own = [[ps(f"own{u}{j}", [128, 512]) for j in range(2)] for u in range(2)]
        agg = [[ps(f"agg{u}{j}", [128, 512]) for j in range(2)] for u in range(2)]
        once = sem("once")
        xt_loaded = sem("xt_loaded")
        counts_loaded = sem("counts_loaded")
        x_loaded = sem("x_loaded")
        own_ready = sem("own_ready")
        agg_ready = sem("agg_ready")
        mean_scaled = sem("mean_scaled")
        x_biased = sem("x_biased")
        mean_ready = sem("mean_ready")
        y_ready = sem("y_ready")
        y_stored = sem("y_stored")
        w_high = sem("w_high")
        w_low = sem("w_low")

        block = ctx.enter_context(nc.Block())

        @block.sync
        def _(sp):
            def loads_of(t, first):
                if not first:
                    sp.wait_ge(own_ready, 2 * t)
                sp.dma_start(xt[:, :, :, :].bitcast(F32),
                             xt_in[bass.ds(t, 1), :, :, :, :].rearrange("o p a k n -> (o p) a k n")).then_inc(xt_loaded, 16)
                if not first:
                    sp.wait_ge(agg_ready, 2 * t)
                sp.dma_start(counts[:, :, :].bitcast(F32),
                             counts_by_src[bass.ds(t, 1), :, :, :].rearrange("o s k d -> (o s) k d")).then_inc(counts_loaded, 16)
                if residual is not None:
                    if not first:
                        sp.wait_ge(mean_ready, 2 * t)
                    sp.dma_start(x[:, :], node_rows(residual, t)).then_inc(x_loaded, 16)

            def store(t):
                sp.wait_ge(y_ready, 2 * t + 2)
                sp.dma_start(node_rows(out, t), y[:, :]).then_inc(y_stored, 16)

            loads_of(0, True)
            with sp.Fori(1, T) as t:
                loads_of(t, False)
                store(t - 1)
            store(T - 1)
            sp.wait_ge(y_stored, 16 * T)

        @block.gpsimd
        def _(pool):
            pool.dma_start(bias_row[:, :], bias.broadcast_to([P, D])).then_inc(once, 16)
            pool.dma_start(dinv[:, :], deg_inv).then_inc(once, 16)
            pool.wait_ge(once, 32)
            with pool.Fori(0, T) as t:
                for j in range(2):
                    cols = slice(j * H, (j + 1) * H)
                    if residual is not None:
                        if j == 0:
                            pool.wait_ge(x_loaded, 16 * t + 16)
                            pool.tensor_tensor(x[:, :], x[:, :], bias_row[:, :], ALU.add).then_inc(x_biased, 1)
                            pool.wait_ge(x_biased, t + 1)
                        pool.wait_ge(mean_scaled, 2 * t + j + 1)
                        pool.tensor_tensor(mean[j][:, :], mean[j][:, :], x[:, cols], ALU.add).then_inc(mean_ready, 1)
                    else:
                        pool.wait_ge(mean_scaled, 2 * t + j + 1)
                        pool.tensor_tensor(mean[j][:, :], mean[j][:, :], bias_row[:, cols], ALU.add).then_inc(mean_ready, 1)

        @block.scalar
        def _(act):
            act.wait_ge(raw_loaded, 16 * loads)
            for k in range(K):
                act.activation(wh[:, k, :], raw[:, k, :], ACT.Copy).then_inc(w_high, 1)
            act.wait_ge(once, 32)
            if next_w is not None:
                act.wait_ge(w_low, K)
                act.dma_start(raw[:, :, :], next_w.rearrange("(k p) n -> p k n", p=128)).then_inc(raw_loaded, 16)
            with act.Fori(0, T // 2) as pair:
                for u in range(2):
                    t = pair * 2 + u
                    act.wait_ge(y_ready, 2 * t)
                    act.wait_ge(agg_ready, 2 * t + 2)
                    for j in range(2):
                        act.activation(mean[j][:, :], agg[u][j][0:P, :], ACT.Copy,
                                       scale=dinv[:, bass.ds(t, 1)]).then_inc(mean_scaled, 1)

        @block.vector
        def _(dve):
            for k in range(K):
                dve.wait_ge(w_high, k + 1)
                dve.tensor_tensor(wl[:, k, :], raw[:, k, :], wh[:, k, :].bitcast(F32), ALU.subtract).then_inc(w_low, 1)
            with dve.Fori(0, T // 2) as pair:
                for u in range(2):
                    t = pair * 2 + u
                    for j in range(2):
                        dve.wait_ge(mean_ready, 2 * t + j + 1)
                        if j == 0:
                            dve.wait_ge(own_ready, 2 * t + 2)
                            dve.wait_ge(y_stored, 16 * t)
                        dve.tensor_tensor(y[:, j * H:(j + 1) * H], own[u][j][0:P, :], mean[j][:, :], ALU.add).then_inc(y_ready, 1)

        @block.tensor
        def _(pe):
            def products(t, u, first, split):
                for j in range(2):
                    cols = slice(j * H, (j + 1) * H)
                    if not first:
                        pe.wait_ge(y_ready, 2 * t + j - 3)
                    if j == 0:
                        pe.wait_ge(xt_loaded, 16 * t + 16)
                    for k in range(K):
                        if split and j == 0:
                            pe.wait_ge(w_low, k + 1)
                        pe.matmul(own[u][j][0:P, :], xt[:, 0, k, :], wh[:, k, cols], start=k == 0, stop=False)
                        pe.matmul(own[u][j][0:P, :], xt[:, 0, k, :], wl[:, k, cols], start=False, stop=False)
                        ins = pe.matmul(own[u][j][0:P, :], xt[:, 1, k, :], wh[:, k, cols], start=False, stop=k == K - 1)
                    ins.then_inc(own_ready, 1)
                pe.wait_ge(counts_loaded, 16 * t + 16)
                for j in range(2):
                    cols = slice(j * H, (j + 1) * H)
                    for k in range(T):
                        pe.matmul(agg[u][j][0:P, :], counts[:, k, :], gh[0:P, k, cols], start=k == 0, stop=False)
                        ins = pe.matmul(agg[u][j][0:P, :], counts[:, k, :], gl[0:P, k, cols], start=False, stop=k == T - 1)
                    ins.then_inc(agg_ready, 1)

            products(0, 0, True, True)
            products(1, 1, True, False)
            with pe.Fori(1, T // 2) as pair:
                for u in range(2):
                    products(pair * 2 + u, u, False, False)


F16 = mybir.dt.float16
I32 = mybir.dt.int32
EDGE_TILE = 128
CHUNK = 2 * EDGE_TILE
CHUNKS = 84
NONE = 2047


def graph_phase(nc, name, edges_dst_chunks, edges_src_cols, edges_dst_cols, counts_by_src, counts_by_dst, deg_inv,
                raw=None, first_w=None, raw_loaded=None):
    sem = lambda s: nc.alloc_semaphore(f"{name}_{s}")
    with ExitStack() as ctx:
        sb = Map(nc, GH_AT, name)
        ps = lambda s, shape: ctx.enter_context(nc.psum_tensor(f"{name}_{s}", shape, F32))
        chunks_i = sb("chunks_i", [CHUNKS, CHUNK], I32)
        src_i = sb("src_i", [128, 2 * CHUNKS], I32)
        dst_i = sb("dst_i", [128, 2 * CHUNKS], I32)
        chunks_f = sb("chunks_f", [CHUNKS, CHUNK], F32)
        src_f = sb("src_f", [128, 2 * CHUNKS], F32)
        dst_f = sb("dst_f", [128, 2 * CHUNKS], F32)
        node_i = sb("node_i", [128, N], I32)
        node = sb("node", [128, N], F16)
        square = sb("square", [128, 128], I32)
        ident = sb("ident", [128, 128], F32)
        block_i = sb("block_i", [1, T, CHUNKS], I32)
        block_at = sb("block_at", [1, T, CHUNKS], F32)
        chunk_i = sb("chunk_i", [1, T, CHUNKS], I32)
        chunk_at = sb("chunk_at", [1, T, CHUNKS], F32)
        least = sb("least", [CHUNKS, 1], F32)
        most = sb("most", [CHUNKS, 1], F32)
        work = [sb(f"work{i}", [1, T, CHUNKS], F32) for i in range(4)]
        rows = sb("rows", [1, 2, CHUNKS], F32)
        bounds = sb("bounds", [1, 2, T], F32)
        bounds_i = sb("bounds_i", [1, 2, T], I32)
        zeros = sb("zeros", [128, 128], F16)
        hot_src = [sb(f"hot_src{i}", [128, N], F16) for i in range(2)]
        hot_dst = [sb(f"hot_dst{i}", [128, P], F16) for i in range(2)]
        by_dst = [sb(f"by_dst{i}", [P, N], F32) for i in range(2)]
        by_src = [sb(f"by_src{i}", [P, T, P], F32R) for i in range(2)]
        deg = sb("deg", [P, T], F32)
        counted = [ps(f"counted{i}", [128, 3, 512]) for i in range(2)]
        turned = [ps(f"turned{i}", [128, 512]) for i in range(2)]
        loaded = sem("loaded")
        made = sem("made")
        step = sem("step")
        rows_up = sem("rows_up")
        bounds_ready = sem("bounds_ready")
        hot_ready = sem("hot_ready")
        hot_free = sem("hot_free")
        counted_ready = sem("counted_ready")
        counted_free = sem("counted_free")
        by_dst_ready = sem("by_dst_ready")
        turned_ready = sem("turned_ready")
        turned_free = sem("turned_free")
        by_src_ready = sem("by_src_ready")
        dst_stored = [sem(f"dst_stored{i}") for i in range(2)]
        src_stored = [sem(f"src_stored{i}") for i in range(2)]
        deg_ready = sem("deg_ready")
        deg_stored = sem("deg_stored")
        BANKS = [(0, 418), (418, 416), (834, 416)]

        block = ctx.enter_context(nc.Block())

        @block.gpsimd
        def _(pool):
            pool.iota(square[:, :], pattern=[[1, 128]], base=0, channel_multiplier=-1).then_inc(made, 1)
            pool.iota(node_i[:, :], pattern=[[1, N]], base=0, channel_multiplier=0).then_inc(made, 1)
            pool.iota(block_i[:, :, :], pattern=[[P, T], [0, CHUNKS]], base=0, channel_multiplier=0).then_inc(made, 1)
            pool.iota(chunk_i[:, :, :], pattern=[[0, T], [1, CHUNKS]], base=0, channel_multiplier=0).then_inc(made, 1)

        @block.sync
        def _(sp):
            sp.dma_start(chunks_i[:, :], edges_dst_chunks).then_inc(loaded, 16)
            sp.dma_start(src_i[:, :], edges_src_cols).then_inc(loaded, 16)
            sp.dma_start(dst_i[:, :], edges_dst_cols).then_inc(loaded, 16)
            if raw is not None:
                sp.dma_start(raw[:, :, :], first_w.rearrange("(k p) n -> p k n", p=128)).then_inc(raw_loaded, 16)
            with sp.Fori(0, T // 2) as pair:
                for u in range(2):
                    b = pair * 2 + u
                    sp.wait_ge(by_dst_ready, b + 1)
                    sp.dma_start(counts_by_dst[:, :, bass.ds(b, 1), :].rearrange("t d o s -> d (t o) s"),
                                 by_dst[u][:, :].rearrange("d (t s) -> d t s", s=P)).then_inc(dst_stored[u], 16)
                    sp.wait_ge(by_src_ready, 3 * b + 3)
                    sp.dma_start(counts_by_src[bass.ds(b, 1), :, :, :].rearrange("o s k d -> (o s) k d"),
                                 by_src[u][:, :, :].bitcast(F32)).then_inc(src_stored[u], 16)
            sp.wait_ge(deg_ready, T + 1)
            sp.dma_start(deg_inv, deg[:, :]).then_inc(deg_stored, 16)
            for u in range(2):
                sp.wait_ge(dst_stored[u], 16 * (T // 2))
                sp.wait_ge(src_stored[u], 16 * (T // 2))
            sp.wait_ge(deg_stored, 16)

        @block.scalar
        def _(act):
            with act.Fori(0, T // 2) as pair:
                for u in range(2):
                    b = pair * 2 + u
                    act.wait_ge(counted_ready, b + 1)
                    act.wait_ge(dst_stored[u], pair * 16)
                    act.wait_ge(deg_ready, pair * 2)
                    for j, (at, n) in enumerate(BANKS):
                        ins = act.activation(by_dst[u][:, at:at + n], counted[u][0:P, j, 0:n], ACT.Copy)
                    ins.then_inc(by_dst_ready, 1)

        @block.vector
        def _(dve):
            dve.wait_ge(made, 4)
            dve.tensor_scalar(ident[:, :], square[:, :], 0.0, None, ALU.is_equal).then_inc(step, 1)
            dve.tensor_copy(node[:, :], node_i[:, :]).then_inc(step, 1)
            dve.tensor_copy(block_at[:, :, :], block_i[:, :, :]).then_inc(step, 1)
            dve.tensor_copy(chunk_at[:, :, :], chunk_i[:, :, :]).then_inc(step, 1)
            dve.memset(zeros[:, :], 0.0).then_inc(step, 1)
            dve.wait_ge(loaded, 48)
            dve.tensor_copy(chunks_f[:, :], chunks_i[:, :]).then_inc(step, 1)
            dve.tensor_copy(src_f[:, :], src_i[:, :]).then_inc(step, 1)
            dve.tensor_copy(dst_f[:, :], dst_i[:, :]).then_inc(step, 1)
            dve.wait_ge(step, 8)
            dve.tensor_reduce(least[:, :], chunks_f[:, :], AX.X, ALU.min).then_inc(step, 1)
            dve.tensor_reduce(most[:, :], chunks_f[:, :], AX.X, ALU.max).then_inc(step, 1)
            dve.wait_ge(rows_up, 1)
            dve.tensor_copy(rows[:, :, :], turned[0][0:1, 0:2 * CHUNKS].rearrange("p (a c) -> p a c", a=2)).then_inc(step, 1)
            dve.wait_ge(step, 11)
            low = rows[:, 0:1, :].broadcast_to([1, T, CHUNKS])
            high = rows[:, 1:2, :].broadcast_to([1, T, CHUNKS])
            dve.tensor_scalar(work[0][:, :, :], block_at[:, :, :], float(P), None, ALU.add).then_inc(step, 1)
            dve.wait_ge(step, 12)
            dve.tensor_tensor(work[1][:, :, :], low, work[0][:, :, :], ALU.is_lt).then_inc(step, 1)
            dve.tensor_tensor(work[2][:, :, :], high, block_at[:, :, :], ALU.is_ge).then_inc(step, 1)
            dve.wait_ge(step, 14)
            dve.tensor_tensor(work[3][:, :, :], work[1][:, :, :], work[2][:, :, :], ALU.mult).then_inc(step, 1)
            dve.wait_ge(step, 15)
            dve.tensor_scalar(work[0][:, :, :], chunk_at[:, :, :], float(CHUNKS - 1), None, ALU.subtract).then_inc(step, 1)
            dve.tensor_scalar(work[1][:, :, :], chunk_at[:, :, :], 1.0, None, ALU.add).then_inc(step, 1)
            dve.wait_ge(step, 17)
            dve.tensor_tensor(work[2][:, :, :], work[0][:, :, :], work[3][:, :, :], ALU.mult).then_inc(step, 1)
            dve.wait_ge(step, 18)
            dve.tensor_tensor(work[0][:, :, :], work[1][:, :, :], work[3][:, :, :], ALU.mult).then_inc(step, 1)
            dve.tensor_reduce(bounds[:, 0, :], work[2][:, :, :], AX.X, ALU.min).then_inc(step, 1)
            dve.wait_ge(step, 20)
            dve.tensor_reduce(bounds[:, 1, :], work[0][:, :, :], AX.X, ALU.max).then_inc(step, 1)
            dve.tensor_scalar(bounds[:, 0, :], bounds[:, 0, :], float(CHUNKS - 1), None, ALU.add).then_inc(step, 1)
            dve.wait_ge(step, 22)
            dve.tensor_scalar(work[0][:, 0, 0:T], bounds[:, 0, :], 1.0, None, ALU.add).then_inc(step, 1)
            dve.wait_ge(step, 23)
            dve.tensor_tensor(bounds[:, 1, :], bounds[:, 1, :], work[0][:, 0, 0:T], ALU.max).then_inc(step, 1)
            dve.wait_ge(step, 24)
            dve.tensor_copy(bounds_i[:, :, :], bounds[:, :, :]).then_inc(bounds_ready, 1)
            dve.wait_ge(bounds_ready, 1)

            done = dve.alloc_register("tiles_made")
            dve.reg_mov(done, 0)
            with dve.Fori(0, T // 2) as pair:
                for u in range(2):
                    b = pair * 2 + u
                    first = dve.value_load(bounds_i[0:1, 0, bass.ds(b, 1)], min_val=0, max_val=CHUNKS - 1)
                    last = dve.value_load(bounds_i[0:1, 1, bass.ds(b, 1)], min_val=1, max_val=CHUNKS)
                    with dve.Fori(first, last) as c:
                        for h in range(2):
                            dve.wait_ge(hot_free, dve.snap(done) + h)
                            dve.tensor_scalar(hot_dst[h][:, :], node[:, bass.ds(b * P, P)],
                                              dst_f[:, bass.ds(c * 2 + h, 1)], None, ALU.is_equal)
                            dve.tensor_scalar(hot_src[h][:, :], node[:, :],
                                              src_f[:, bass.ds(c * 2 + h, 1)], None, ALU.is_equal).then_inc(hot_ready, 1)
                        dve.reg_add(done, done, 2)
                    for r, (k0, kn) in enumerate([(0, 4), (4, 4), (8, 2)]):
                        dve.wait_ge(turned_ready, 3 * b + r + 1)
                        if r == 0:
                            dve.wait_ge(src_stored[u], pair * 16)
                        dve.tensor_copy(by_src[u][:, k0:k0 + kn, :],
                                        turned[r % 2][0:P, 0:kn * P].rearrange("s (k d) -> s k d", d=P)).then_inc(by_src_ready, 1)
                    dve.tensor_reduce(deg[:, bass.ds(b, 1)], by_dst[u][:, :], AX.X, ALU.add).then_inc(deg_ready, 1)
            dve.wait_ge(deg_ready, T)
            dve.tensor_scalar(deg[:, :], deg[:, :], 1.0, None, ALU.max).then_inc(step, 1)
            dve.wait_ge(step, 25)
            dve.reciprocal(deg[:, :], deg[:, :]).then_inc(deg_ready, 1)

        @block.tensor
        def _(pe):
            pe.wait_ge(step, 10)
            pe.matmul(turned[0][0:1, 0:CHUNKS], least[:, :], ident[0:CHUNKS, 0:CHUNKS], start=True, stop=True)
            pe.matmul(turned[0][0:1, CHUNKS:2 * CHUNKS], most[:, :], ident[0:CHUNKS, 0:CHUNKS],
                      start=True, stop=True).then_inc(rows_up, 1)
            pe.wait_ge(bounds_ready, 1)
            pe.sem_inc(hot_free, 1)
            done = pe.alloc_register("tiles_used")
            pe.reg_mov(done, 0)
            with pe.Fori(0, T // 2) as pair:
                for u in range(2):
                    b = pair * 2 + u
                    first = pe.value_load(bounds_i[0:1, 0, bass.ds(b, 1)], min_val=0, max_val=CHUNKS - 1)
                    last = pe.value_load(bounds_i[0:1, 1, bass.ds(b, 1)], min_val=1, max_val=CHUNKS)
                    for j, (at, n) in enumerate(BANKS):
                        pe.matmul(counted[u][:, j, 0:n], zeros[:, :], node[:, 0:n], start=True, stop=False)
                    with pe.Fori(first, last) as c:
                        for h in range(2):
                            pe.wait_ge(hot_ready, pe.snap(done) + (h + 1))
                            for j, (at, n) in enumerate(BANKS):
                                mm = pe.matmul(counted[u][0:P, j, 0:n], hot_dst[h][:, :], hot_src[h][:, at:at + n],
                                               start=False, stop=False)
                            mm.then_inc(hot_free, 1)
                        pe.reg_add(done, done, 2)
                    for j, (at, n) in enumerate(BANKS):
                        mm = pe.matmul(counted[u][:, j, 0:n], zeros[:, :], node[:, 0:n], start=False, stop=True)
                    mm.then_inc(counted_ready, 1)
                    pe.wait_ge(by_dst_ready, b + 1)
                    for r, (k0, kn) in enumerate([(0, 4), (4, 4), (8, 2)]):
                        pe.wait_ge(by_src_ready, 3 * b + (1 if r == 2 else 0))
                        for k in range(k0, k0 + kn):
                            mm = pe.transpose(turned[r % 2][0:P, (k - k0) * P:(k - k0 + 1) * P],
                                              by_dst[u][:, k * P:(k + 1) * P], ident[0:P, 0:P])
                        mm.then_inc(turned_ready, 1)


def unfold_phase(nc, name, g1, g2, w_full):
    sem = lambda s: nc.alloc_semaphore(f"{name}_{s}")
    C, B, E = 4, 32, 16
    KT = H // 128
    with ExitStack() as ctx:
        local = Map(nc, GH_AT, name)
        first = local("first", [128, 2, KT, C, B])
        second = local("second", [128, 2, C, E])
        terms = [local(f"terms{i}", [128, C, B, E]) for i in range(2)]
        w = local("w", [128, 2, KT, H])
        minus = local("minus", [128, KT, H])
        loaded = sem("loaded")
        terms_ready = sem("terms_ready")
        w_ready = sem("w_ready")
        minus_ready = sem("minus_ready")
        stored = sem("stored")
        block = ctx.enter_context(nc.Block())

        @block.sync
        def _(sp):
            for part in range(2):
                sp.dma_start(first[:, part, :, :, :].rearrange("p k c b -> p k (c b)"),
                             g1[part].rearrange("(k p) n -> p k n", p=128)).then_inc(loaded, 16)
                sp.dma_start(second[:, part, :, :].rearrange("p c e -> p (c e)"), g2[part]).then_inc(loaded, 16)
            quarter = lambda i, j: w_full[i * H:(i + 1) * H, j * H:(j + 1) * H].rearrange("(k p) n -> p k n", p=128)
            for part, places in enumerate([((0, 0), (1, 1)), ((0, 1),)]):
                sp.wait_ge(w_ready, KT * (part + 1))
                for i, j in places:
                    sp.dma_start(quarter(i, j), w[:, part, :, :]).then_inc(stored, 16)
            sp.wait_ge(minus_ready, 1)
            sp.dma_start(quarter(1, 0), minus[:, :, :]).then_inc(stored, 16)
            sp.wait_ge(stored, 64)

        @block.gpsimd
        def _(pool):
            pool.wait_ge(loaded, 64)
            for i in range(2 * KT):
                part, k = divmod(i, KT)
                if i >= 2:
                    pool.wait_ge(w_ready, i - 1)
                pool.tensor_tensor(terms[i % 2][:, :, :, :],
                                   first[:, part, k, :, :].unsqueeze(3).broadcast_to([128, C, B, E]),
                                   second[:, part, :, :].unsqueeze(2).broadcast_to([128, C, B, E]), ALU.mult).then_inc(terms_ready, 1)

        @block.vector
        def _(dve):
            for i in range(2 * KT):
                part, k = divmod(i, KT)
                dve.wait_ge(terms_ready, i + 1)
                dve.tensor_reduce(w[:, part, k, :], terms[i % 2][:, :, :, :].rearrange("p c b e -> p (b e) c"),
                                  AX.X, ALU.add).then_inc(w_ready, 1)

        @block.scalar
        def _(act):
            act.wait_ge(w_ready, 2 * KT)
            act.activation(minus[:, :, :], w[:, 1, :, :], ACT.Copy, scale=-1.0).then_inc(minus_ready, 1)


def attention_phase(nc, name, rows, counts_by_dst, scores, norm_w, router_t, gh, gl, base, tokens, logits):
    sem = lambda s: nc.alloc_semaphore(f"{name}_{s}")
    EXPERTS = 8
    with ExitStack() as ctx:
        ps = lambda s, shape: ctx.enter_context(nc.psum_tensor(f"{name}_{s}", shape, F32))
        local = Map(nc, RAW_AT, name)
        counts = [local(f"counts{u}", [P, T, P]) for u in range(2)]
        z = [local(f"z{u}", [P, T, P]) for u in range(2)]
        leaky = local("leaky", [P, T, P])
        e = local("e", [P, T, P])
        weight = [local(f"weight{u}", [P, T, P]) for u in range(2)]
        ph = [local(f"ph{u}", [P, T, P], F32R) for u in range(2)]
        pl = [local(f"pl{u}", [P, T, P], F32R) for u in range(2)]
        al_row = local("al_row", [P, T, P])
        x = [local(f"x{u}", [P, D]) for u in range(2)]
        low = local("low", [P, D])
        high = local("high", [P, D])
        nw_row = local("nw_row", [P, D])
        assert local.at <= GH_AT, local.at
        local = Map(nc, LOCAL_AT, name)
        h = [local(f"h{u}", [P, D]) for u in range(2)]
        y = local("y", [P, D])
        token = [local(f"token{u}", [P, D]) for u in range(2)]
        token_t = local("token_t", [128, K, P])
        ident = local("ident", [P, P])
        square = local("square", [P, P], mybir.dt.int32)
        router = local("router", [128, K, EXPERTS])
        sc = local("sc", [P, T, 2])
        ones = local("ones", [P, 2], F32R)
        ones_f = local("ones_f", [P, 2])
        small = lambda s: [local(f"{s}{u}", [P, 1]) for u in range(2)]
        total, rtotal, rstd, rrms, sumsq = small("total"), small("rtotal"), small("rstd"), small("rrms"), small("sumsq")
        stats = [local(f"stats{u}", [P, 12]) for u in range(2)]
        moments = [local(f"moments{u}", [P, 2]) for u in range(2)]
        power, eps, eps_rms, waits, inv_d, pool_waits = (
            local(s, [P, 1]) for s in ("power", "eps", "eps_rms", "waits", "inv_d", "pool_waits"))
        logit_rows = local("logit_rows", [P, T, EXPERTS])
        assert BASE + local.at <= 229344, local.at
        acc = [[ps(f"acc{u}{j}", [128, 512]) for j in range(2)] for u in range(2)]
        turned = [ps(f"turned{r}", [128, 4, P]) for r in range(2)]
        sums = ps("sums", [128, 2])
        logit_ps = ps("logit_ps", [128, EXPERTS])

        once = sem("once")
        made = sem("made")
        consts = sem("consts")
        row_ready = sem("row_ready")
        al_ready = sem("al_ready")
        counts_loaded = [sem(f"counts_loaded{u}") for u in range(2)]
        x_loaded = [sem(f"x_loaded{u}") for u in range(2)]
        z_added = sem("z_added")
        z_ready = sem("z_ready")
        leaky_ready = sem("leaky_ready")
        e_ready = sem("e_ready")
        weight_ready = sem("weight_ready")
        ph_ready = sem("ph_ready")
        pl_ready = sem("pl_ready")
        acc_ready = sem("acc_ready")
        sums_ready = sem("sums_ready")
        total_ready = sem("total_ready")
        rtotal_ready = sem("rtotal_ready")
        h_ready = sem("h_ready")
        low_ready = sem("low_ready")
        exp_ready = sem("exp_ready")
        elu_ready = sem("elu_ready")
        x3_ready = sem("x3_ready")
        stats_ready = sem("stats_ready")
        moments_ready = sem("moments_ready")
        pool_step = sem("pool_step")
        rstd_ready = sem("rstd_ready")
        y_ready = sem("y_ready")
        sumsq_ready = sem("sumsq_ready")
        rrms_ready = sem("rrms_ready")
        token_ready = sem("token_ready")
        base_ready = sem("base_ready")
        turned_ready = sem("turned_ready")
        token_t_ready = sem("token_t_ready")
        logit_ready = sem("logit_ready")
        logit_read = sem("logit_read")
        base_stored = [sem(f"base_stored{u}") for u in range(2)]
        token_stored = [sem(f"token_stored{u}") for u in range(2)]

        block = ctx.enter_context(nc.Block())

        @block.sync
        def _(sp):
            sp.dma_start(sc[:, :, :], scores).then_inc(once, 16)
            sp.dma_start(nw_row[:, :], norm_w.broadcast_to([P, D])).then_inc(once, 16)
            sp.dma_start(router[:, :, :], router_t.rearrange("p (k e) -> p k e", e=EXPERTS)).then_inc(once, 16)

            def load(t, u, pair):
                if pair is not None:
                    sp.wait_ge(weight_ready, t - 1)
                sp.dma_start(counts[u][:, :, :], counts_by_dst[bass.ds(t, 1), :, :, :].rearrange("o d k s -> (o d) k s")).then_inc(counts_loaded[u], 16)

            def load_x(t, u, pair):
                if pair is not None:
                    sp.wait_ge(base_stored[u], 16 * pair)
                sp.dma_start(x[u][:, :], node_rows(rows, t)).then_inc(x_loaded[u], 16)

            def store(t, u):
                sp.wait_ge(token_ready, t + 1)
                sp.dma_start(node_rows(tokens, t), token[u][:, :]).then_inc(token_stored[u], 16)
                sp.wait_ge(base_ready, t + 1)
                sp.dma_start(node_rows(base, t), x[u][:, :]).then_inc(base_stored[u], 16)

            for t in range(2):
                load(t, t, None)
                load_x(t, t, None)
            with sp.Fori(0, T // 2 - 1) as pair:
                for u in range(2):
                    load(pair * 2 + (u + 2), u, pair)
                    store(pair * 2 + u, u)
                    load_x(pair * 2 + (u + 2), u, pair + 1)
            for u in range(2):
                store(T - 2 + u, u)
            for u in range(2):
                sp.wait_ge(token_stored[u], 16 * (T // 2))
                sp.wait_ge(base_stored[u], 16 * (T // 2))
            sp.wait_ge(logit_read, T)
            sp.dma_start(logits, logit_rows[:, :, :]).then_inc(once, 16)
            sp.wait_ge(once, 64)

        @block.gpsimd
        def _(pool):
            pool.iota(square[:, :], pattern=[[1, P]], base=0, channel_multiplier=-1).then_inc(made, 1)
            pool.memset(power[:, :], -0.5).then_inc(made, 1)
            pool.memset(eps[:, :], 1e-5).then_inc(made, 1)
            pool.memset(eps_rms[:, :], 1e-6).then_inc(made, 1)
            pool.memset(inv_d[:, :], 1.0 / D).then_inc(made, 1)
            pool.memset(ones_f[:, :], 1.0).then_inc(made, 1)
            pool.wait_ge(made, 6)
            pool.wait_ge(al_ready, 3)

            def edges(t, u, pair):
                if pair is not None:
                    pool.wait_ge(leaky_ready, t - 1)
                pool.tensor_tensor(z[u][:, :, :], al_row[:, bass.ds(t, 1), :].broadcast_to([P, T, P]),
                                   sc[:, :, 1:2].broadcast_to([P, T, P]), ALU.add).then_inc(z_added, 1)
                pool.wait_ge(z_added, t + 1)
                pool.tensor_tensor(pool_waits[:, :], eps[:, :], eps[:, :], ALU.add)
                pool.tensor_scalar(z[u][:, :, :], z[u][:, :, :], -880.0, None, ALU.max).then_inc(z_ready, 1)

            def row(t, u):
                pool.wait_ge(moments_ready, t + 1)
                pool.tensor_tensor(rstd[u][:, :], moments[u][:, 1:2], eps[:, :], ALU.add).then_inc(pool_step, 1)
                pool.wait_ge(pool_step, 3 * t + 1)
                pool.tensor_tensor(rstd[u][:, :], rstd[u][:, :], power[:, :], ALU.pow).then_inc(rstd_ready, 1)
                pool.wait_ge(sumsq_ready, t + 1)
                pool.tensor_tensor(rrms[u][:, :], sumsq[u][:, :], inv_d[:, :], ALU.mult).then_inc(pool_step, 1)
                pool.wait_ge(pool_step, 3 * t + 2)
                pool.tensor_tensor(rrms[u][:, :], rrms[u][:, :], eps_rms[:, :], ALU.add).then_inc(pool_step, 1)
                pool.wait_ge(pool_step, 3 * t + 3)
                pool.tensor_tensor(rrms[u][:, :], rrms[u][:, :], power[:, :], ALU.pow).then_inc(rrms_ready, 1)
                pool.tensor_tensor(x[u][:, :], x[u][:, :], y[:, :], ALU.add).then_inc(base_ready, 1)

            edges(0, 0, None)
            edges(1, 1, None)
            with pool.Fori(0, T // 2 - 1) as pair:
                for u in range(2):
                    edges(pair * 2 + (u + 2), u, pair)
                    row(pair * 2 + u, u)
            for u in range(2):
                row(T - 2 + u, u)

        @block.scalar
        def _(act):
            act.wait_ge(row_ready, 1)
            for r, (k0, kn) in enumerate([(0, 4), (4, 4), (8, 2)]):
                act.activation(al_row[:, k0:k0 + kn, :],
                               acc[r // 2][r % 2][0:P, 0:kn * P].rearrange("p (k n) -> p k n", n=P), ACT.Copy).then_inc(al_ready, 1)

            def edges(t, u, late=True):
                act.wait_ge(leaky_ready, t + 1)
                act.wait_ge(weight_ready, t)
                act.activation(e[:, :, :], leaky[:, :, :], ACT.Exp, scale=-1.0).then_inc(e_ready, 1)
                act.wait_ge(weight_ready, t + 1)
                if late:
                    act.wait_ge(sums_ready, t - 1)
                act.activation(ph[u][:, :, :], weight[u][:, :, :], ACT.Copy).then_inc(ph_ready, 1)

            def row(t, u, pair):
                act.wait_ge(acc_ready, 2 * t + 2)
                act.wait_ge(rtotal_ready, t + 1)
                for j in range(2):
                    act.activation(h[u][:, j * H:(j + 1) * H], acc[u][j][0:P, :], ACT.Copy, scale=rtotal[u][:, 0:1]).then_inc(h_ready, 1)
                act.wait_ge(low_ready, t + 1)
                act.activation(low[:, :], low[:, :], ACT.Exp).then_inc(exp_ready, 1)
                act.wait_ge(y_ready, t + 1)
                act.activation(high[:, :], y[:, :], ACT.Square, accum_out=sumsq[u][:, 0:1]).then_inc(sumsq_ready, 1)

            def turn(t):
                act.wait_ge(turned_ready, t + 1)
                act.wait_ge(logit_ready, t)
                for r in range(2):
                    ins = act.activation(token_t[:, 4 * r:4 * r + 4, :], turned[r][:, :, :], ACT.Copy)
                ins.then_inc(token_t_ready, 1)
                act.wait_ge(logit_ready, t + 1)
                act.activation(logit_rows[:, bass.ds(t, 1), :].rearrange("p o n -> p (o n)"),
                               logit_ps[0:P, :], ACT.Copy).then_inc(logit_read, 1)

            edges(0, 0, False)
            edges(1, 1, False)
            edges(2, 0)
            row(0, 0, 0)
            edges(3, 1)
            row(1, 1, 0)
            with act.Fori(0, T // 2 - 2) as back:
                pair = back + 1
                for u in range(2):
                    turn(back * 2 + u)
                    edges(pair * 2 + (u + 2), u)
                    row(pair * 2 + u, u, pair)
            for u in range(2):
                turn(T - 4 + u)
                row(T - 2 + u, u, T // 2 - 1)
            turn(T - 2)
            turn(T - 1)

        @block.vector
        def _(dve):
            dve.wait_ge(made, 6)
            dve.tensor_scalar(ident[:, :], square[:, :], 0.0, None, ALU.is_equal).then_inc(consts, 1)
            dve.tensor_copy(ones[:, :], ones_f[:, :]).then_inc(consts, 1)

            def edges(t, u, pair):
                dve.wait_ge(z_ready, t + 1)
                dve.wait_ge(e_ready, t)
                dve.scalar_tensor_tensor(leaky[:, :, :], z[u][:, :, :], 0.1, z[u][:, :, :], ALU.mult, ALU.max).then_inc(leaky_ready, 1)
                dve.wait_ge(e_ready, t + 1)
                dve.wait_ge(counts_loaded[u], 16 * pair + 16)
                dve.tensor_tensor(weight[u][:, :, :], e[:, :, :], counts[u][:, :, :], ALU.mult).then_inc(weight_ready, 1)
                dve.wait_ge(ph_ready, t + 1)
                dve.tensor_tensor(pl[u][:, :, :], weight[u][:, :, :], ph[u][:, :, :].bitcast(F32), ALU.subtract).then_inc(pl_ready, 1)

            def row(t, u, pair):
                dve.wait_ge(sums_ready, t + 1)
                dve.tensor_scalar(total[u][:, :], sums[0:P, 0:1], 1e-5, None, ALU.add).then_inc(total_ready, 1)
                dve.wait_ge(total_ready, t + 1)
                dve.reciprocal(rtotal[u][:, :], total[u][:, :]).then_inc(rtotal_ready, 1)
                dve.wait_ge(h_ready, 2 * t + 2)
                dve.tensor_scalar(low[:, :], h[u][:, :], 0.0, None, ALU.min).then_inc(low_ready, 1)
                dve.wait_ge(exp_ready, t + 1)
                dve.scalar_tensor_tensor(high[:, :], h[u][:, :], 0.0, low[:, :], ALU.max, ALU.add).then_inc(elu_ready, 1)
                dve.wait_ge(elu_ready, t + 1)
                dve.wait_ge(x_loaded[u], 16 * pair + 16)
                dve.scalar_tensor_tensor(x[u][:, :], high[:, :], -1.0, x[u][:, :], ALU.add, ALU.add).then_inc(x3_ready, 1)
                dve.wait_ge(x3_ready, t + 1)
                for j in range(2):
                    dve.bn_stats(stats[u][:, 6 * j:6 * j + 6], x[u][:, j * H:(j + 1) * H]).then_inc(stats_ready, 1)
                dve.wait_ge(stats_ready, 2 * t + 2)
                dve.memset(waits[:, :], 0.0)
                dve.bn_aggr(moments[u][:, :], stats[u][:, :]).then_inc(moments_ready, 1)
                dve.wait_ge(rstd_ready, t + 1)
                dve.wait_ge(base_ready, t)
                dve.tensor_scalar(y[:, :], x[u][:, :], moments[u][:, 0:1], rstd[u][:, 0:1], ALU.subtract, ALU.mult).then_inc(y_ready, 1)
                dve.wait_ge(rrms_ready, t + 1)
                dve.wait_ge(token_stored[u], 16 * pair)
                if t_is_late(pair):
                    dve.wait_ge(turned_ready, t - 1)
                dve.scalar_tensor_tensor(token[u][:, :], y[:, :], rrms[u][:, 0:1], nw_row[:, :], ALU.mult, ALU.mult).then_inc(token_ready, 1)

            def t_is_late(pair):
                return not (isinstance(pair, int) and pair == 0)

            edges(0, 0, 0)
            edges(1, 1, 0)
            edges(2, 0, 1)
            dve.wait_ge(once, 48)
            row(0, 0, 0)
            edges(3, 1, 1)
            row(1, 1, 0)
            with dve.Fori(1, T // 2 - 1) as pair:
                for u in range(2):
                    edges(pair * 2 + (u + 2), u, pair + 1)
                    row(pair * 2 + u, u, pair)
            for u in range(2):
                row(T - 2 + u, u, T // 2 - 1)

        @block.tensor
        def _(pe):
            pe.wait_ge(consts, 2)
            pe.wait_ge(once, 48)
            for t in range(T):
                r = t // 4
                ins = pe.matmul(acc[r // 2][r % 2][0:P, (t % 4) * P:(t % 4 + 1) * P],
                                sc[:, t, 0:1].broadcast_to([P, P]), ident[:, :], start=True, stop=True)
            ins.then_inc(row_ready, 1)
            pe.wait_ge(al_ready, 3)

            def half(t, u, j, first):
                if j == 0:
                    pe.wait_ge(pl_ready, t + 1)
                if not first:
                    pe.wait_ge(h_ready, 2 * t + j - 3)
                cols = slice(j * H, (j + 1) * H)
                for k in range(T):
                    pe.matmul(acc[u][j][0:P, :], ph[u][:, k, :], gh[0:P, k, cols], start=k == 0, stop=False)
                    pe.matmul(acc[u][j][0:P, :], ph[u][:, k, :], gl[0:P, k, cols], start=False, stop=False)
                    ins = pe.matmul(acc[u][j][0:P, :], pl[u][:, k, :], gh[0:P, k, cols], start=False, stop=k == T - 1)
                ins.then_inc(acc_ready, 1)

            def sum_of(t, u):
                pe.wait_ge(total_ready, t)
                for k in range(T):
                    pe.matmul(sums[0:P, :], ph[u][:, k, :], ones[:, :], start=k == 0, stop=False)
                    ins = pe.matmul(sums[0:P, :], pl[u][:, k, :], ones[:, :], start=False, stop=k == T - 1)
                ins.then_inc(sums_ready, 1)

            def turn(t, u):
                pe.wait_ge(token_ready, t + 1)
                pe.wait_ge(token_t_ready, t)
                for k in range(K):
                    ins = pe.transpose(turned[k // 4][:, k % 4, :], token[u][:, k * 128:(k + 1) * 128], ident[:, :])
                ins.then_inc(turned_ready, 1)

            def route(t):
                pe.wait_ge(token_t_ready, t + 1)
                pe.wait_ge(logit_read, t)
                for k in range(K):
                    ins = pe.matmul(logit_ps[0:P, :], token_t[:, k, :], router[:, k, :], start=k == 0, stop=k == K - 1)
                ins.then_inc(logit_ready, 1)

            for t in range(2):
                half(t, t, 0, True)
                half(t, t, 1, True)
                sum_of(t, t)
            with pe.Fori(1, T // 2) as pair:
                for u in range(2):
                    t = pair * 2 + u
                    half(t, u, 0, False)
                    turn(t - 2, u)
                    half(t, u, 1, False)
                    route(t - 2)
                    sum_of(t, u)
            for t in (T - 2, T - 1):
                turn(t, t % 2)
                route(t)


U32 = mybir.dt.uint32
EXPERTS, TOP, HID = 8, 2, 352
BLOCK = 128
BLOCKS = (TOP * N + EXPERTS * (BLOCK - 1) + EXPERTS) // BLOCK
SLOT_BLOCKS = BLOCKS + 1
HK = 3
HROWS = [128, 128, HID - 256]


def route_phase(nc, name, logits, table, slots_out, weights_out, plan_out):
    sem = lambda s: nc.alloc_semaphore(f"{name}_{s}")
    E = EXPERTS
    with ExitStack() as ctx:
        ps = lambda s, shape: ctx.enter_context(nc.psum_tensor(f"{name}_{s}", shape, F32))
        local = Map(nc, 0, name)
        lg = local("lg", [P, T, E])
        top = local("top", [P, T, E])
        top_at = local("top_at", [P, T, E], U32)
        peak = local("peak", [P, T, 1])
        total = local("total", [P, T, 1])
        pick = local("pick", [P, T, TOP])
        wsum = local("wsum", [P, T, 1])
        weight = local("weight", [P, T, TOP])
        expert_i = local("expert_i", [P, T, E], I32)
        expert = local("expert", [P, T, E])
        hot = [local(f"hot{j}", [P, T, E]) for j in range(TOP)]
        both = local("both", [P, T, E])
        node_i = local("node_i", [P, T], I32)
        square = local("square", [P, P], I32)
        before = local("before", [P, P])
        ones = local("ones", [P, P])
        place = local("place", [P, T, E])
        count = local("count", [P, T, E])
        start = local("start", [P, T + 1, E])
        steps_i = local("steps_i", [P, E, T - 1], I32)
        steps = local("steps", [P, E, T - 1])
        over = local("over", [P, E, T - 1])
        blocks = local("blocks", [P, E])
        first = local("first", [P, E + 1])
        offset = local("offset", [P, E])
        at = [local(f"at{j}", [P, T, E]) for j in range(TOP)]
        slot = local("slot", [P, T, TOP])
        slot_i = local("slot_i", [P, T, TOP], I32)
        block_i = local("block_i", [1, BLOCKS, E], I32)
        block_f = local("block_f", [1, BLOCKS, E])
        begun = local("begun", [1, BLOCKS, E])
        sign_i = local("sign_i", [1, E // 2, 2], I32)
        sign = local("sign", [1, E])
        signed = local("signed", [1, BLOCKS, E])
        plan = local("plan", [1, PLAN])
        plan_i = local("plan_i", [1, PLAN], I32)
        zeros = local("zeros", [128, SLOT_BLOCKS], I32)
        place_ps = ps("place_ps", [128, T * E])
        count_ps = ps("count_ps", [128, T * E])

        loaded = sem("loaded")
        made = sem("made")
        step = sem("step")
        expd = sem("expd")
        peak_ready = sem("peak_ready")
        both_ready = sem("both_ready")
        placed = sem("placed")
        slots_ready = sem("slots_ready")
        plan_ready = sem("plan_ready")
        zeroed = sem("zeroed")
        scattered = sem("scattered")
        stored = sem("stored")

        block = ctx.enter_context(nc.Block())

        @block.sync
        def _(sp):
            sp.dma_start(lg[:, :, :], logits).then_inc(loaded, 16)
            sp.wait_ge(made, 1)
            sp.dma_start(table.rearrange("(p b) o -> p (b o)", p=128), zeros[:, :]).then_inc(zeroed, 16)
            sp.wait_ge(slots_ready, 1)
            sp.dma_start(slots_out, slot_i[:, :, :]).then_inc(stored, 16)
            sp.dma_start(weights_out, weight[:, :, :]).then_inc(stored, 16)
            sp.wait_ge(plan_ready, 1)
            sp.dma_start(plan_out, plan_i[:, :]).then_inc(stored, 16)
            sp.wait_ge(stored, 48)

        @block.gpsimd
        def _(pool):
            pool.memset(zeros[:, :], 0).then_inc(made, 1)
            pool.iota(expert_i[:, :, :], pattern=[[0, T], [1, E]], base=0, channel_multiplier=0).then_inc(made, 1)
            pool.iota(node_i[:, :], pattern=[[P, T]], base=0, channel_multiplier=1).then_inc(made, 1)
            pool.iota(square[:, :], pattern=[[1, P]], base=0, channel_multiplier=-1).then_inc(made, 1)
            pool.iota(steps_i[:, :, :], pattern=[[0, E], [BLOCK, T - 1]], base=BLOCK, channel_multiplier=0).then_inc(made, 1)
            pool.iota(block_i[:, :, :], pattern=[[1, BLOCKS], [0, E]], base=0, channel_multiplier=0).then_inc(made, 1)
            pool.iota(sign_i[:, :, :], pattern=[[0, E // 2], [2, 2]], base=-1, channel_multiplier=0).then_inc(made, 1)
            pool.memset(ones[:, :], 1.0).then_inc(made, 1)
            pool.wait_ge(zeroed, 16)
            pool.wait_ge(slots_ready, 1)
            pool.wait_ge(made, 8)
            for t in range(T):
                for j in range(TOP):
                    pool.indirect_dma_start(table, bass.IndirectOffsetOnAxis(slot_i[:, t, j:j + 1], 0),
                                            node_i[:, t:t + 1], None).then_inc(scattered, 16)
            pool.wait_ge(scattered, 16 * T * TOP)

        @block.scalar
        def _(act):
            act.wait_ge(peak_ready, 1)
            act.activation(lg[:, :, :], lg[:, :, :], ACT.Exp).then_inc(expd, 1)

        @block.tensor
        def _(pe):
            pe.wait_ge(both_ready, 1)
            rhs = both[:, :, :].rearrange("p t e -> p (t e)")
            pe.matmul(place_ps[0:P, :], before[:, :], rhs, start=True, stop=True).then_inc(placed, 1)
            pe.matmul(count_ps[0:P, :], ones[:, :], rhs, start=True, stop=True).then_inc(placed, 1)

        @block.vector
        def _(dve):
            n = [0]

            def then(ins):
                n[0] += 1
                ins.then_inc(step, 1)
                dve.wait_ge(step, n[0])

            dve.wait_ge(made, 8)
            dve.wait_ge(loaded, 16)
            tte = lambda ap: ap.broadcast_to([P, T, E])
            then(dve.tensor_reduce(peak[:, :, 0], lg[:, :, :], AX.X, ALU.max))
            dve.tensor_tensor(lg[:, :, :], lg[:, :, :], tte(peak[:, :, :]), ALU.subtract).then_inc(peak_ready, 1)
            dve.wait_ge(expd, 1)
            then(dve.tensor_reduce(total[:, :, 0], lg[:, :, :], AX.X, ALU.add))
            then(dve.reciprocal(total[:, :, :], total[:, :, :]))
            then(dve.tensor_tensor(lg[:, :, :], lg[:, :, :], tte(total[:, :, :]), ALU.mult))
            for t in range(T):
                then(dve.max(top[:, t, :], lg[:, t, :]))
                then(dve.max_index(top_at[:, t, :], top[:, t, :], lg[:, t, :]))
            then(dve.tensor_tensor(wsum[:, :, :], top[:, :, 0:1], top[:, :, 1:2], ALU.add))
            then(dve.reciprocal(wsum[:, :, :], wsum[:, :, :]))
            then(dve.tensor_tensor(weight[:, :, :], top[:, :, 0:TOP], wsum[:, :, :].broadcast_to([P, T, TOP]), ALU.mult))
            then(dve.tensor_copy(pick[:, :, :], top_at[:, :, 0:TOP]))
            then(dve.tensor_copy(expert[:, :, :], expert_i[:, :, :]))
            for j in range(TOP):
                then(dve.tensor_tensor(hot[j][:, :, :], expert[:, :, :], tte(pick[:, :, j:j + 1]), ALU.is_equal))
            then(dve.tensor_scalar(before[:, :], square[:, :], 0.0, None, ALU.is_gt))
            dve.tensor_tensor(both[:, :, :], hot[0][:, :, :], hot[1][:, :, :], ALU.add).then_inc(both_ready, 1)
            dve.wait_ge(placed, 2)
            then(dve.tensor_copy(place[:, :, :], place_ps[0:P, :].rearrange("p (t e) -> p t e", e=E)))
            then(dve.tensor_copy(count[:, :, :], count_ps[0:P, :].rearrange("p (t e) -> p t e", e=E)))
            then(dve.memset(start[:, 0, :], 0.0))
            for t in range(T):
                then(dve.tensor_tensor(start[:, t + 1, :], start[:, t, :], count[:, t, :], ALU.add))
            then(dve.tensor_copy(steps[:, :, :], steps_i[:, :, :]))
            then(dve.tensor_tensor(over[:, :, :], start[:, T, :].unsqueeze(2).broadcast_to([P, E, T - 1]), steps[:, :, :], ALU.is_gt))
            then(dve.tensor_reduce(blocks[:, :], over[:, :, :], AX.X, ALU.add))
            then(dve.tensor_scalar(blocks[:, :], blocks[:, :], 1.0, None, ALU.add))
            then(dve.memset(first[:, 0:1], 0.0))
            for e in range(E):
                then(dve.tensor_tensor(first[:, e + 1:e + 2], first[:, e:e + 1], blocks[:, e:e + 1], ALU.add))
            then(dve.tensor_scalar(offset[:, :], first[:, 0:E], float(BLOCK), None, ALU.mult))
            then(dve.tensor_tensor(place[:, :, :], place[:, :, :], start[:, 0:T, :], ALU.add))
            then(dve.tensor_tensor(place[:, :, :], place[:, :, :], offset[:, :].unsqueeze(1).broadcast_to([P, T, E]), ALU.add))
            for j in range(TOP):
                then(dve.tensor_tensor(at[j][:, :, :], place[:, :, :], hot[j][:, :, :], ALU.mult))
                then(dve.tensor_reduce(slot[:, :, j], at[j][:, :, :], AX.X, ALU.add))
            dve.tensor_copy(slot_i[:, :, :], slot[:, :, :]).then_inc(slots_ready, 1)
            then(dve.tensor_copy(block_f[:, :, :], block_i[:, :, :]))
            then(dve.tensor_tensor(begun[:, :, :], block_f[:, :, :], first[0:1, 0:E].unsqueeze(1).broadcast_to([1, BLOCKS, E]), ALU.is_ge))
            then(dve.memset(plan[:, :], 0.0))
            then(dve.tensor_reduce(plan[:, AT_EXPERT:AT_EXPERT + BLOCKS], begun[:, :, :], AX.X, ALU.add))
            then(dve.tensor_copy(sign[:, :], sign_i[:, :, :].rearrange("p a b -> p (a b)")))
            then(dve.memset(sign[:, 0:1], 0.0))
            then(dve.tensor_tensor(signed[:, :, :], begun[:, :, :], sign[:, :].unsqueeze(1).broadcast_to([1, BLOCKS, E]), ALU.mult))
            then(dve.tensor_reduce(plan[:, AT_SIDE + 1:AT_SIDE + 1 + BLOCKS], signed[:, :, :], AX.X, ALU.add))
            then(dve.tensor_copy(plan[:, AT_COUNT:AT_COUNT + E], blocks[0:1, :]))
            then(dve.tensor_copy(plan[:, AT_TOTAL:AT_TOTAL + 1], first[0:1, E:E + 1]))
            then(dve.tensor_scalar(plan[:, AT_REST:AT_REST + 1], first[0:1, E:E + 1], -1.0, float(SLOT_BLOCKS), ALU.mult, ALU.add))
            dve.tensor_copy(plan_i[:, :], plan[:, :]).then_inc(plan_ready, 1)


AT_EXPERT = 0
AT_SIDE = AT_EXPERT + BLOCKS
AT_COUNT = AT_SIDE + BLOCKS + 1
AT_TOTAL = AT_COUNT + EXPERTS
AT_REST = AT_TOTAL + 1
PLAN = AT_REST + 1


def expert_phase(nc, name, tokens, table, plan_in, gate_up_t, down_t, results):
    sem = lambda s: nc.alloc_semaphore(f"{name}_{s}")
    E, KU, W2 = EXPERTS, K, 2 * HID
    with ExitStack() as ctx:
        ps = lambda s, shape: ctx.enter_context(nc.psum_tensor(f"{name}_{s}", shape, F32))
        local = Map(nc, 0, name)
        up_w = local("up_w", [128, 2, 2, K, W2], F32R)
        down_w = local("down_w", [128, 2, 2, HK, D], F32R)
        up_raw = local("up_raw", [128, K, W2])
        down_raw = local("down_raw", [128, HK, D])
        x = local("x", [BLOCK, D])
        xt = local("xt", [128, 2, K, BLOCK], F32R)
        gate = local("gate", [BLOCK, HID])
        hidden = local("hidden", [BLOCK, HK * 128])
        ht = local("ht", [128, 2, HK, BLOCK], F32R)
        y = local("y", [BLOCK, D])
        index = local("index", [128, SLOT_BLOCKS], I32)
        index_now = local("index_now", [128, 1], I32)
        waits = local("waits", [128, 2])
        zeros = local("zeros", [128, 256])
        plan = local("plan", [1, PLAN], I32)
        ident = local("ident", [128, 128])
        square = local("square", [128, 128], I32)
        assert BASE + local.at <= 229344, local.at
        gate_ps = ps("gate_ps", [128, HID])
        up_ps = ps("up_ps", [128, HID])
        y_ps = [ps(f"y_ps{j}", [128, H]) for j in range(2)]
        turned = [ps(f"turned{r}", [128, 4, BLOCK]) for r in range(2)]
        ht_ps = ps("ht_ps", [128, HK, BLOCK])

        once = sem("once")
        made = sem("made")
        ident_ready = sem("ident_ready")
        ht_cleared = sem("ht_cleared")
        raw_loaded = sem("raw_loaded")
        w_high = sem("w_high")
        w_ready = sem("w_ready")
        index_ready = sem("index_ready")
        gathered = sem("gathered")
        x_turned = sem("x_turned")
        xt_high = sem("xt_high")
        xt_ready = sem("xt_ready")
        gate_done = sem("gate_done")
        up_done = sem("up_done")
        down_cleared = sem("down_cleared")
        once_dve = sem("once_dve")
        gate_ready = sem("gate_ready")
        hidden_ready = sem("hidden_ready")
        h_turned = sem("h_turned")
        ht_high = sem("ht_high")
        ht_ready = sem("ht_ready")
        down_ready = sem("down_ready")
        y_ready = sem("y_ready")
        y_stored = sem("y_stored")
        cleared = sem("cleared")
        GROUPS = [((0, 3), 0), ((3, 6), 1), ((6, 8), 2)]

        block = ctx.enter_context(nc.Block())

        @block.sync
        def _(sp):
            sp.dma_start(plan[:, :], plan_in).then_inc(once, 16)
            with nc.allow_non_contiguous_dma(reason="slots of a block over the partitions; a small table"):
                sp.dma_start(index[:, :], table.rearrange("(b p) o -> p (b o)", p=128)).then_inc(once, 16)
            sp.wait_ge(once, 32)
            with sp.Fori(0, E) as e:
                sp.wait_ge(w_ready, 3 * e)
                sp.dma_start(up_raw[:, :, :], gate_up_t[bass.ds(e, 1), :, :].rearrange("o p (k n) -> (o p) k n", n=W2)).then_inc(raw_loaded, 16)
                sp.dma_start(down_raw[:, 0:2, :], down_t[bass.ds(e, 1), 0:256, :].rearrange("o (k p) n -> (o p) k n", p=128)).then_inc(raw_loaded, 16)
                sp.dma_start(down_raw[0:HROWS[2], 2, :], down_t[bass.ds(e, 1), 256:HID, :].rearrange("o p n -> (o p) n")).then_inc(raw_loaded, 16)
            sp.wait_ge(once_dve, 2)
            total = sp.value_load(plan[0:1, AT_TOTAL:AT_TOTAL + 1], min_val=E, max_val=BLOCKS)
            with sp.Fori(total + 1, SLOT_BLOCKS + 1) as i:
                sp.dma_start(results[bass.ds(i * BLOCK, BLOCK), :].rearrange("p (r n) -> p r n", n=256),
                             zeros[:, :].unsqueeze(1).broadcast_to([128, D // 256, 256])).then_inc(cleared, 16)
            sp.wait_ge(raw_loaded, 48 * E)

        @block.gpsimd
        def _(pool):
            pool.iota(square[:, :], pattern=[[1, 128]], base=0, channel_multiplier=-1).then_inc(made, 1)
            pool.memset(waits[:, 1:2], 0.0).then_inc(made, 1)
            pool.wait_ge(made, 2)
            pool.wait_ge(once, 32)
            total = pool.value_load(plan[0:1, AT_TOTAL:AT_TOTAL + 1], min_val=E, max_val=BLOCKS)
            with pool.Fori(0, total + 1) as i:
                pool.wait_ge(x_turned, i)
                pool.tensor_copy(index_now[:, :], index[:, bass.ds(i, 1)]).then_inc(index_ready, 1)
                pool.wait_ge(index_ready, i + 1)
                pool.tensor_tensor(waits[:, 0:1], waits[:, 1:2], waits[:, 1:2], ALU.add)
                pool.indirect_dma_start(x[:, :], None, tokens, bass.IndirectOffsetOnAxis(index_now[:, :], 0)).then_inc(gathered, 16)
                pool.wait_ge(gathered, 16 * i + 16)
            rest = pool.value_load(plan[0:1, AT_REST:AT_REST + 1], min_val=1, max_val=SLOT_BLOCKS)
            pool.wait_ge(cleared, rest * 16)
            pool.wait_ge(y_stored, 16 * total + 16)

        @block.scalar
        def _(act):
            def split(e, side, g):
                (k0, k1), d = GROUPS[g]
                act.wait_ge(raw_loaded, 48 * e + 48)
                act.activation(up_w[:, side, 0, k0:k1, :], up_raw[:, k0:k1, :], ACT.Copy)
                act.activation(down_w[:, side, 0, d, :], down_raw[:, d, :], ACT.Copy).then_inc(w_high, 1)

            def xt_part(i):
                act.wait_ge(x_turned, i + 1)
                for r in range(2):
                    ins = act.activation(xt[:, 0, 4 * r:4 * r + 4, :], turned[r][:, :, :], ACT.Copy)
                ins.then_inc(xt_high, 1)

            def result(i):
                act.wait_ge(down_ready, i + 1)
                act.wait_ge(y_stored, 16 * i)
                for j in range(2):
                    ins = act.activation(y[:, j * H:(j + 1) * H], y_ps[j][:, :], ACT.Copy)
                ins.then_inc(y_ready, 1)
                act.wait_ge(y_ready, i + 1)
                act.dma_start(results[bass.ds(i * BLOCK, BLOCK), :], y[:, :]).then_inc(y_stored, 16)

            def one_block(i):
                act.wait_ge(gate_done, i + 1)
                act.wait_ge(hidden_ready, i)
                act.activation(gate[:, :], gate_ps[:, :], ACT.Silu).then_inc(gate_ready, 1)
                act.wait_ge(up_done, i + 1)
                xt_part(i + 1)
                result(i)
                act.wait_ge(h_turned, i + 1)
                act.activation(ht[:, 0, :, :], ht_ps[:, :, :], ACT.Copy).then_inc(ht_high, 1)

            def expert(e, side, last):
                mine = act.value_load(plan[0:1, bass.ds(AT_COUNT + e, 1)], min_val=1, max_val=T)
                with act.Fori(0, mine) as b:
                    one_block(act.snap(count))
                    act.reg_add(count, count, 1)
                    if not last:
                        for g in range(3):
                            with act.If(b == g):
                                split(e + 1, 1 - side, g)
                if not last:
                    for g in range(1, 3):
                        with act.If(mine <= g):
                            split(e + 1, 1 - side, g)

            act.wait_ge(down_cleared, 1)
            for g in range(3):
                split(0, 0, g)
            xt_part(0)
            act.wait_ge(once, 32)
            count = act.alloc_register(f"{name}_act_blocks")
            act.reg_mov(count, 0)
            with act.Fori(0, E // 2 - 1) as pair:
                for side in range(2):
                    expert(pair * 2 + side, side, False)
            expert(E - 2, 0, False)
            expert(E - 1, 1, True)
            total = act.snap(count)
            result(total)

        @block.vector
        def _(dve):
            def split(e, side, g):
                (k0, k1), d = GROUPS[g]
                dve.wait_ge(w_high, 3 * e + (g + 1))
                dve.tensor_tensor(up_w[:, side, 1, k0:k1, :], up_raw[:, k0:k1, :], up_w[:, side, 0, k0:k1, :].bitcast(F32), ALU.subtract)
                dve.tensor_tensor(down_w[:, side, 1, d, :], down_raw[:, d, :], down_w[:, side, 0, d, :].bitcast(F32), ALU.subtract).then_inc(w_ready, 1)

            def xt_part(i):
                dve.wait_ge(xt_high, i + 1)
                for r in range(2):
                    ins = dve.tensor_tensor(xt[:, 1, 4 * r:4 * r + 4, :], turned[r][:, :, :],
                                            xt[:, 0, 4 * r:4 * r + 4, :].bitcast(F32), ALU.subtract)
                ins.then_inc(xt_ready, 1)

            def one_block(i):
                dve.wait_ge(gate_ready, i + 1)
                dve.wait_ge(up_done, i + 1)
                dve.wait_ge(h_turned, i)
                dve.tensor_tensor(hidden[:, 0:HID], up_ps[:, :], gate[:, :], ALU.mult).then_inc(hidden_ready, 1)
                xt_part(i + 1)
                dve.wait_ge(ht_high, i + 1)
                dve.tensor_tensor(ht[:, 1, :, :], ht_ps[:, :, :], ht[:, 0, :, :].bitcast(F32), ALU.subtract).then_inc(ht_ready, 1)

            def expert(e, side, last):
                mine = dve.value_load(plan[0:1, bass.ds(AT_COUNT + e, 1)], min_val=1, max_val=T)
                with dve.Fori(0, mine) as b:
                    one_block(dve.snap(count))
                    dve.reg_add(count, count, 1)
                    if not last:
                        for g in range(3):
                            with dve.If(b == g):
                                split(e + 1, 1 - side, g)
                if not last:
                    for g in range(1, 3):
                        with dve.If(mine <= g):
                            split(e + 1, 1 - side, g)

            dve.memset(down_raw[96:128, 2, :], 0.0).then_inc(down_cleared, 1)
            dve.memset(hidden[:, HID:HK * 128], 0.0).then_inc(once_dve, 1)
            dve.memset(zeros[:, :], 0.0).then_inc(once_dve, 1)
            dve.memset(ht[:, :, :, :].bitcast(F32), 0.0).then_inc(ht_ready, 1)
            dve.wait_ge(made, 1)
            dve.tensor_scalar(ident[:, :], square[:, :], 0.0, None, ALU.is_equal).then_inc(ident_ready, 1)
            for g in range(3):
                split(0, 0, g)
            xt_part(0)
            dve.wait_ge(once, 32)
            count = dve.alloc_register(f"{name}_dve_blocks")
            dve.reg_mov(count, 0)
            with dve.Fori(0, E // 2 - 1) as pair:
                for side in range(2):
                    expert(pair * 2 + side, side, False)
            expert(E - 2, 0, False)
            expert(E - 1, 1, True)

        @block.tensor
        def _(pe):
            def turn_x(i):
                pe.wait_ge(gathered, 16 * i + 16)
                for k in range(K):
                    ins = pe.transpose(turned[k // 4][:, k % 4, :], x[:, k * 128:(k + 1) * 128], ident[:, :])
                ins.then_inc(x_turned, 1)

            def up(i):
                begun = pe.value_load(plan[0:1, bass.ds(AT_EXPERT + i, 1)], min_val=1, max_val=E)
                side = pe.value_load(plan[0:1, bass.ds(AT_SIDE + 1 + i, 1)], min_val=0, max_val=1)
                pe.wait_ge(w_ready, begun * 3)
                pe.wait_ge(xt_ready, i + 1)
                pe.wait_ge(hidden_ready, i)
                for out, c0, done in ((gate_ps, 0, gate_done), (up_ps, HID, up_done)):
                    for k in range(K):
                        high, low = (up_w[:, bass.ds(side, 1), part, k, c0:c0 + HID].rearrange("p o n -> p (o n)") for part in range(2))
                        pe.matmul(out[:, :], xt[:, 0, k, :], high, start=k == 0, stop=False)
                        pe.matmul(out[:, :], xt[:, 0, k, :], low, start=False, stop=False)
                        ins = pe.matmul(out[:, :], xt[:, 1, k, :], high, start=False, stop=k == K - 1)
                    ins.then_inc(done, 1)

            def down(i):
                side = pe.value_load(plan[0:1, bass.ds(AT_SIDE + i, 1)], min_val=0, max_val=1)
                pe.wait_ge(ht_ready, i + 1)
                pe.wait_ge(y_ready, i)
                for j in range(2):
                    for k in range(HK):
                        high, low = (down_w[:, bass.ds(side, 1), part, k, j * H:(j + 1) * H].rearrange("p o n -> p (o n)") for part in range(2))
                        pe.matmul(y_ps[j][:, :], ht[:, 0, k, :], high, start=k == 0, stop=False)
                        pe.matmul(y_ps[j][:, :], ht[:, 0, k, :], low, start=False, stop=False)
                        ins = pe.matmul(y_ps[j][:, :], ht[:, 1, k, :], high, start=False, stop=k == HK - 1)
                ins.then_inc(down_ready, 1)

            def turn_h(i):
                pe.wait_ge(hidden_ready, i + 1)
                for k in range(HK):
                    ins = pe.transpose(ht_ps[:, k, :], hidden[:, k * 128:(k + 1) * 128], ident[:, :])
                ins.then_inc(h_turned, 1)

            pe.wait_ge(once, 32)
            pe.wait_ge(once_dve, 1)
            pe.wait_ge(ident_ready, 1)
            turn_x(0)
            total = pe.value_load(plan[0:1, AT_TOTAL:AT_TOTAL + 1], min_val=E, max_val=BLOCKS)
            with pe.Fori(0, total) as i:
                up(i)
                turn_x(i + 1)
                down(i)
                turn_h(i)
            down(total)


def combine_phase(nc, name, base, results, slots, weights, alpha, out):
    sem = lambda s: nc.alloc_semaphore(f"{name}_{s}")
    DEPTH = 5
    with ExitStack() as ctx:
        local = Map(nc, 0, name)
        row = [[local(f"row{d}{j}", [P, D]) for j in range(TOP)] for d in range(DEPTH)]
        x = [local(f"x{d}", [P, D]) for d in range(DEPTH)]
        slot = local("slot", [P, T, TOP], I32)
        weight = local("weight", [P, T, TOP])
        scale = local("scale", [P, 1])
        scaled = local("scaled", [P, T, TOP])
        once = sem("once")
        scaled_ready = sem("scaled_ready")
        x_loaded = [sem(f"x_loaded{d}") for d in range(DEPTH)]
        gathered = [[sem(f"gathered{d}{j}") for j in range(TOP)] for d in range(DEPTH)]
        added = sem("added")
        stored = [sem(f"stored{d}") for d in range(DEPTH)]
        block = ctx.enter_context(nc.Block())

        @block.sync
        def _(sp):
            sp.dma_start(slot[:, :, :], slots).then_inc(once, 16)
            sp.dma_start(weight[:, :, :], weights).then_inc(once, 16)
            sp.dma_start(scale[:, :], alpha.broadcast_to([P, 1])).then_inc(once, 16)
            for t in range(T):
                d = t % DEPTH
                if t >= DEPTH:
                    sp.wait_ge(stored[d], 16 * (t // DEPTH))
                sp.dma_start(x[d][:, :], base[t * P:(t + 1) * P, :]).then_inc(x_loaded[d], 16)

        @block.scalar
        def _(act):
            for t in range(T):
                act.wait_ge(added, TOP * (t + 1))
                act.dma_start(out[t * P:(t + 1) * P, :], x[t % DEPTH][:, :]).then_inc(stored[t % DEPTH], 16)
            for d in range(DEPTH):
                act.wait_ge(stored[d], 16 * (T // DEPTH))

        @block.gpsimd
        def _(pool):
            pool.wait_ge(once, 48)
            for t in range(T):
                d = t % DEPTH
                if t >= DEPTH:
                    pool.wait_ge(added, TOP * (t - DEPTH + 1))
                for j in range(TOP):
                    pool.indirect_dma_start(row[d][j][:, :], None, results,
                                            bass.IndirectOffsetOnAxis(slot[:, t, j:j + 1], 0),
                                            element_offset=BLOCK * D).then_inc(gathered[d][j], 16)

        @block.vector
        def _(dve):
            dve.wait_ge(once, 48)
            dve.tensor_scalar(scale[:, :], scale[:, :], -0.5, 2.0, ALU.max, ALU.min).then_inc(scaled_ready, 1)
            dve.wait_ge(scaled_ready, 1)
            dve.tensor_scalar(scaled[:, :, :], weight[:, :, :], scale[:, 0:1], None, ALU.mult).then_inc(scaled_ready, 1)
            dve.wait_ge(scaled_ready, 2)
            for t in range(T):
                d = t % DEPTH
                dve.wait_ge(x_loaded[d], 16 * (t // DEPTH + 1))
                for j in range(TOP):
                    dve.wait_ge(gathered[d][j], 16 * (t // DEPTH + 1))
                    if j:
                        dve.wait_ge(added, TOP * t + j)
                    dve.scalar_tensor_tensor(x[d][:, :], row[d][j][:, :], scaled[:, t, j:j + 1], x[d][:, :],
                                             ALU.mult, ALU.add).then_inc(added, 1)


def gnn_ffn_gnn_moe_kernel(nc, x, edges_src_cols, edges_dst_cols, edges_dst_chunks, w_self0, w_neigh0, bias0,
                           w_self1, w_neigh1, bias1, train1, train2, ffn_bias, att_w, att_a, norm_w, router_t,
                           gate_up_t, down_t, alpha, out):
    dram = lambda name, shape, dt=F32: nc.dram_tensor(name, shape, dt, kind="Internal").ap()
    counts_by_src = dram("counts_by_src", [T, P, T, P])
    counts_by_dst = dram("counts_by_dst", [T, P, T, P])
    deg_inv = dram("deg_inv", [P, T])
    w_ffn = dram("w_ffn", [D, D])
    xt0 = dram("xt0", [T, 128, 2, K, P])
    xt1 = dram("xt1", [T, 128, 2, K, P])
    h0 = dram("h0", [N, D])
    x1 = dram("x1", [N, D])
    x2 = dram("x2", [N, D])
    base = dram("base", [N, D])
    tokens = dram("tokens", [N, D])
    scores = dram("scores", [P, T, 2])
    logits = dram("logits", [P, T, EXPERTS])
    table = dram("table", [SLOT_BLOCKS * BLOCK, 1], I32)
    slots = dram("slots", [P, T, TOP], I32)
    weights = dram("weights", [P, T, TOP])
    plan = dram("plan", [1, PLAN], I32)
    results = dram("results", [(SLOT_BLOCKS + 1) * BLOCK, D])

    place = lambda name, shape, dt, at: nc.alloc_sbuf_tensor_at(name, shape, dt, offset=BASE + at)
    raw = place("raw", [128, K, D], F32, RAW_AT)
    wh = place("wh", [128, K, D], F32R, WH_AT)
    wl = place("wl", [128, K, D], F32R, WL_AT)
    gh = place("gh", [128, T, D], F32R, GH_AT)
    gl = place("gl", [128, T, D], F32R, GL_AT)

    raw_loaded = nc.alloc_semaphore("raw_loaded")

    def clear_semaphores(before):
        nc.clear_and_free_semaphores(nc.allocated_since(before))
        nc.all_engine_barrier()

    before = nc.snapshot_sems()
    graph_phase(nc, "graph", edges_dst_chunks, edges_src_cols, edges_dst_cols,
                counts_by_src, counts_by_dst, deg_inv, raw, w_neigh0, raw_loaded)
    unfold_phase(nc, "unfold", train1, train2, w_ffn)
    project_phase(nc, "neigh0", x, xt0, raw, wh, wl, gh, gl, raw_loaded, 1, w_self0,
                  normalize=True, relu=False, result="split")
    aggregate_phase(nc, "self0", xt0, counts_by_src, deg_inv, bias0, None, h0,
                    raw, wh, wl, gh, gl, raw_loaded, 2, w_neigh1)
    project_phase(nc, "neigh1", h0, xt1, raw, wh, wl, gh, gl, raw_loaded, 3, w_self1,
                  normalize=False, relu=True, result="split")
    aggregate_phase(nc, "self1", xt1, counts_by_src, deg_inv, bias1, x, x1,
                    raw, wh, wl, gh, gl, raw_loaded, 4, w_ffn)
    clear_semaphores(before)
    before = nc.snapshot_sems()
    project_phase(nc, "ffn", x1, None, raw, wh, wl, None, None, raw_loaded, 5, att_w,
                  normalize=True, relu=False, result="residual", bias=ffn_bias, out=x2)
    project_phase(nc, "att_h", x2, None, raw, wh, wl, gh, gl, raw_loaded, 6, None,
                  normalize=True, relu=False, result="scores", score_w=att_a, scores=scores)
    attention_phase(nc, "att", x2, counts_by_dst, scores, norm_w, router_t, gh, gl, base, tokens, logits)
    route_phase(nc, "route", logits, table, slots, weights, plan)
    clear_semaphores(before)
    expert_phase(nc, "experts", tokens, table, plan, gate_up_t, down_t, results)
    combine_phase(nc, "combine", base, results, slots, weights, alpha, out)


_NAMES = ["x", "edges_src_cols", "edges_dst_cols", "edges_dst_chunks", "w_self0", "w_neigh0", "bias0",
          "w_self1", "w_neigh1", "bias1", "train1", "train2", "ffn_bias", "att_w", "att_a", "norm_w", "router_t",
          "gate_up_t", "down_t", "alpha"]


def _layout(inputs):
    a = {k: np.asarray(v) for k, v in inputs.items()}
    pad = np.full(CHUNKS * CHUNK - a["src"].shape[0], NONE, a["src"].dtype)
    src = np.concatenate([a["src"], pad])
    dst = np.concatenate([a["dst"], pad])
    cols = lambda e: e.reshape(2 * CHUNKS, EDGE_TILE).T
    train1 = lambda g: np.repeat(g[0].transpose(2, 1, 0).reshape(32, 128), 16, axis=0)
    train2 = lambda g: np.tile(g[:, :, 0, :].transpose(2, 0, 1).reshape(16, 64), (8, 1))
    row = lambda v: v.reshape(1, -1)
    return dict(
        x=a["x"], edges_src_cols=cols(src), edges_dst_cols=cols(dst), edges_dst_chunks=dst.reshape(CHUNKS, CHUNK),
        w_self0=a["L0_gnn_W_self0"], w_neigh0=a["L0_gnn_W_neigh0"], bias0=row(a["L0_gnn_b0"]),
        w_self1=a["L0_gnn_W_self1"], w_neigh1=a["L0_gnn_W_neigh1"], bias1=row(a["L0_gnn_b1"]),
        train1=np.stack([train1(a["L0_ffn_G1_R"]), train1(a["L0_ffn_G1_I"])]),
        train2=np.stack([train2(a["L0_ffn_G2_R"]), train2(a["L0_ffn_G2_I"])]),
        ffn_bias=row(np.concatenate([a["L0_ffn_bias_real"], a["L0_ffn_bias_imag"]])),
        att_w=a["L1_gnn_W"], att_a=row(a["L1_gnn_a"]), norm_w=row(a["L1_ffn_norm_weight"]),
        router_t=a["L1_ffn_router_weight"].reshape(EXPERTS, K, 128).transpose(2, 1, 0).reshape(128, K * EXPERTS),
        gate_up_t=a["L1_ffn_gate_up_weight"].reshape(EXPERTS, 2 * HID, K, 128).transpose(0, 3, 2, 1).reshape(EXPERTS, 128, K * 2 * HID),
        down_t=a["L1_ffn_down_weight"].transpose(0, 2, 1),
        alpha=a["L1_ffn_residual_alpha"].reshape(1, 1))


def kernel(**inputs):
    import concourse.bacc as _bacc
    from concourse import mybir as _mybir
    from concourse.bass_utils import run_bass_kernel_spmd as _run

    nc = _bacc.Bacc("TRN2", target_bir_lowering=False, num_devices=1)
    data = _layout(inputs)
    arrays, args = {}, []
    for name in _NAMES:
        a = np.ascontiguousarray(data[name])
        arrays[f"in_{name}"] = a
        args.append(nc.dram_tensor(f"in_{name}", a.shape, _mybir.dt.from_np(a.dtype), kind="ExternalInput").ap())
    args.append(nc.dram_tensor("out_rows", (N, D), _mybir.dt.float32, kind="ExternalOutput").ap())
    gnn_ffn_gnn_moe_kernel(nc, *args)
    r = _run(nc, [arrays], core_ids=[0])
    return r.results[0]["out_rows"]
```

```python
import numpy as np
import concourse.bass as bass
from concourse import mybir
from contextlib import ExitStack

F32 = mybir.dt.float32
F32R = mybir.dt.float32r
ALU = mybir.AluOpType
ACT = mybir.ActivationFunctionType
AX = mybir.AxisListType
N, P, D = 1250, 125, 1024
T, K, H = N // P, D // 128, D // 2

BASE = 16512
W_BYTES = K * D * 4
G_BYTES = T * D * 4
RAW_AT = 0
WH_AT = RAW_AT + W_BYTES
WL_AT = WH_AT + W_BYTES
GH_AT = WL_AT + W_BYTES
GL_AT = GH_AT + G_BYTES
LOCAL_AT = GL_AT + G_BYTES


class Map:

    def __init__(self, nc, at, name):
        self.nc, self.at, self.name = nc, at, name

    def __call__(self, name, shape, dt=F32):
        size = 2 if dt == mybir.dt.float16 else 4
        for s in shape[1:]:
            size *= s
        t = self.nc.alloc_sbuf_tensor_at(f"{self.name}_{name}", shape, dt, offset=BASE + self.at)
        self.at += -(-size // 32) * 32
        return t


def node_rows(x, t):
    return x[bass.ds(t * P, P), :]


def project_phase(nc, name, rows, xt_out, raw, wh, wl, gh, gl, raw_loaded, loads, next_w,
                  normalize, relu, result, bias=None, out=None, score_w=None, scores=None):
    sem = lambda s: nc.alloc_semaphore(f"{name}_{s}")
    with ExitStack() as ctx:
        ps = lambda s, shape: ctx.enter_context(nc.psum_tensor(f"{name}_{s}", shape, F32))
        local = Map(nc, LOCAL_AT, name)
        xt = [local(f"xt{u}", [128, 2, K, P], F32R) for u in range(2)]
        if result == "residual":
            local = Map(nc, GH_AT, name)
            bias_row = local("bias_row", [P, D])
            biased = [local(f"biased{u}", [P, D]) for u in range(2)]
            xn = local("xn", [P, D])
            y = [local(f"y{u}", [P, D]) for u in range(2)]
        x = [local(f"x{u}", [P, D]) for u in range(2)]
        if result != "residual":
            xn = None
        ident = local("ident", [P, P])
        square = local("square", [P, P], mybir.dt.int32)
        power = local("power", [P, 1])
        eps = local("eps", [P, 1])
        waits = local("waits", [P, 1])
        stats = [local(f"stats{u}", [P, 12]) for u in range(2)]
        moments = [local(f"moments{u}", [P, 2]) for u in range(2)]
        rstd = [local(f"rstd{u}", [P, 1]) for u in range(2)]
        if result == "scores":
            score_parts = local("score_parts", [P, 2, 2, 2])
            scores_sb = local("scores_sb", [P, T, 2])
        acc = [[ps(f"acc{u}{j}", [128, 512]) for j in range(2)] for u in range(2)]
        turned = [ps(f"turned{r}", [128, 4, P]) for r in range(2)]

        x_loaded = [sem(f"x_loaded{u}") for u in range(2)]
        xt_high = sem("xt_high")
        xt_low = sem("xt_low")
        if xt_out is not None:
            xt_stored = [sem(f"xt_stored{u}") for u in range(2)]
        if normalize:
            stats_ready = sem("stats_ready")
            moments_ready = sem("moments_ready")
            rstd_ready = sem("rstd_ready")
            var_eps = sem("var_eps")
            xn_ready = sem("xn_ready")
        turned_ready = sem("turned_ready")
        acc_ready = sem("acc_ready")
        if result != "residual":
            acc_high = sem("acc_high")
            acc_free = sem("acc_free")
        w_high = sem("w_high")
        w_low = sem("w_low")
        made = sem("made")
        ident_ready = sem("ident_ready")
        if result != "split":
            extra = sem("extra")
        if result == "scores":
            scored = sem("scored")
            score_ready = sem("score_ready")
            finished = sem("finished")
        if result == "residual":
            biased_ready = sem("biased_ready")
            y_ready = sem("y_ready")
            y_stored = [sem(f"y_stored{u}") for u in range(2)]

        def xn_of(u):
            return x[u] if xn is None else xn

        block = ctx.enter_context(nc.Block())

        @block.sync
        def _(sp):
            if bias is not None:
                sp.dma_start(bias_row[:, :], bias.broadcast_to([P, D])).then_inc(extra, 16)

            def load(t, u, pair):
                if pair is not None:
                    sp.wait_ge(turned_ready, t - 1)
                    if result == "residual":
                        sp.wait_ge(biased_ready, t - 1)
                sp.dma_start(x[u][:, :], node_rows(rows, t)).then_inc(x_loaded[u], 16)

            def store(t, u):
                if xt_out is not None:
                    sp.wait_ge(xt_low, t + 1)
                    sp.dma_start(xt_out[bass.ds(t, 1), :, :, :, :].rearrange("o p a k n -> (o p) a k n"),
                                 xt[u][:, :, :, :].bitcast(F32)).then_inc(xt_stored[u], 16)
                if result == "residual":
                    sp.wait_ge(y_ready, 2 * t + 2)
                    sp.dma_start(node_rows(out, t), y[u][:, :]).then_inc(y_stored[u], 16)

            load(0, 0, None)
            load(1, 1, None)
            with sp.Fori(0, T // 2 - 1) as pair:
                for u in range(2):
                    load(pair * 2 + (u + 2), u, pair)
                    store(pair * 2 + u, u)
            for t in (T - 2, T - 1):
                store(t, t % 2)
            if xt_out is not None:
                for u in range(2):
                    sp.wait_ge(xt_stored[u], 16 * (T // 2))
            if result == "residual":
                for u in range(2):
                    sp.wait_ge(y_stored[u], 16 * (T // 2))
            if result == "scores":
                sp.wait_ge(score_ready, T)
                sp.dma_start(scores, scores_sb[:, :, :]).then_inc(finished, 16)
                sp.wait_ge(finished, 16)

        @block.gpsimd
        def _(pool):
            pool.iota(square[:, :], pattern=[[1, P]], base=0, channel_multiplier=-1).then_inc(made, 1)
            pool.memset(power[:, :], -0.5).then_inc(made, 1)
            pool.memset(eps[:, :], 1e-5).then_inc(made, 1)
            pool.wait_ge(made, 3)
            def tile(t, u, pair):
                if normalize:
                    pool.wait_ge(moments_ready, t + 1)
                    pool.tensor_tensor(rstd[u][:, :], moments[u][:, 1:2], eps[:, :], ALU.add).then_inc(var_eps, 1)
                    pool.wait_ge(var_eps, t + 1)
                    pool.tensor_tensor(rstd[u][:, :], rstd[u][:, :], power[:, :], ALU.pow).then_inc(rstd_ready, 1)
                if result == "residual":
                    pool.wait_ge(x_loaded[u], pair * 16 + 16)
                    if not (isinstance(pair, int) and pair == 0):
                        pool.wait_ge(y_ready, 2 * t - 2)
                    pool.tensor_tensor(biased[u][:, :], x[u][:, :], bias_row[:, :], ALU.add).then_inc(biased_ready, 1)

            if result == "residual":
                pool.wait_ge(extra, 16)
            if normalize or result == "residual":
                tile(0, 0, 0)
                tile(1, 1, 0)
                with pool.Fori(1, T // 2) as pair:
                    for u in range(2):
                        tile(pair * 2 + u, u, pair)

        @block.scalar
        def _(act):
            def turn(t, u, pair):
                act.wait_ge(turned_ready, t + 1)
                if not (isinstance(pair, int) and pair == 0):
                    act.wait_ge(acc_ready, 2 * t - 2)
                    if xt_out is not None:
                        act.wait_ge(xt_stored[u], 16 * pair)
                for r in range(2):
                    act.activation(xt[u][:, 0, 4 * r:4 * r + 4, :], turned[r][:, :, :],
                                         ACT.Relu if relu else ACT.Copy).then_inc(xt_high, 1)

            def result_of(t, u):
                for j in range(2):
                    if result == "residual":
                        continue
                    act.wait_ge(acc_ready, 2 * t + j + 1)
                    act.activation(gh[0:P, bass.ds(t, 1), j * H:(j + 1) * H].rearrange("p o n -> p (o n)"),
                                   acc[u][j][0:P, :], ACT.Copy).then_inc(acc_high, 1)

            turn(0, 0, 0)
            act.wait_ge(raw_loaded, 16 * loads)
            for k in range(K):
                act.activation(wh[:, k, :], raw[:, k, :], ACT.Copy).then_inc(w_high, 1)
            turn(1, 1, 0)
            if next_w is not None:
                act.wait_ge(w_low, K)
                act.dma_start(raw[:, :, :], next_w.rearrange("(k p) n -> p k n", p=128)).then_inc(raw_loaded, 16)
            if result == "scores":
                act.wait_ge(w_low, K)
                act.dma_start(raw[0:P, 0:2, :].rearrange("p c n -> p (c n)"), score_w.broadcast_to([P, 2 * D])).then_inc(extra, 16)
            result_of(0, 0)
            with act.Fori(0, T // 2 - 1) as pair:
                for u in range(2):
                    turn(pair * 2 + (u + 2), u, pair + 1)
                    result_of(pair * 2 + (u + 1), 1 - u)
            result_of(T - 1, 1)

        @block.vector
        def _(dve):
            dve.wait_ge(made, 3)
            dve.tensor_scalar(ident[:, :], square[:, :], 0.0, None, ALU.is_equal).then_inc(ident_ready, 1)

            def norm(t, u, pair):
                dve.wait_ge(x_loaded[u], 16 * (pair + 1))
                if not normalize:
                    return
                for j in range(2):
                    dve.bn_stats(stats[u][:, 6 * j:6 * j + 6], x[u][:, j * H:(j + 1) * H]).then_inc(stats_ready, 1)
                dve.wait_ge(stats_ready, 2 * t + 2)
                dve.memset(waits[:, :], 0.0)
                dve.bn_aggr(moments[u][:, :], stats[u][:, :]).then_inc(moments_ready, 1)
                dve.wait_ge(rstd_ready, t + 1)
                if xn is not None:
                    dve.wait_ge(turned_ready, t)
                dve.tensor_scalar(xn_of(u)[:, :], x[u][:, :], moments[u][:, 0:1], rstd[u][:, 0:1],
                                  ALU.subtract, ALU.mult).then_inc(xn_ready, 1)

            def turn(t, u):
                for r in range(2):
                    dve.wait_ge(xt_high, 2 * t + r + 1)
                    low, high = xt[u][:, 1, 4 * r:4 * r + 4, :], xt[u][:, 0, 4 * r:4 * r + 4, :].bitcast(F32)
                    if relu:
                        ins = dve.scalar_tensor_tensor(low, turned[r][:, :, :], 0.0, high, ALU.max, ALU.subtract)
                    else:
                        ins = dve.tensor_tensor(low, turned[r][:, :, :], high, ALU.subtract)
                ins.then_inc(xt_low, 1)

            def result_of(t, u, pair):
                for j in range(2):
                    cols = slice(j * H, (j + 1) * H)
                    if result == "residual":
                        dve.wait_ge(acc_ready, 2 * t + j + 1)
                        if j == 0:
                            dve.wait_ge(biased_ready, t + 1)
                            dve.wait_ge(y_stored[u], 16 * pair)
                        dve.tensor_tensor(y[u][:, cols], acc[u][j][0:P, :], biased[u][:, cols], ALU.add).then_inc(y_ready, 1)
                    else:
                        dve.wait_ge(acc_high, 2 * t + j + 1)
                        if result == "scores":
                            for c in range(2):
                                dve.wait_ge(scored, 4 * t)
                                dve.tensor_tensor_reduce(raw[0:P, 2 + 2 * j + c, 0:H], acc[u][j][0:P, :], raw[0:P, c, cols],
                                                         1.0, 0.0, ALU.mult, ALU.add,
                                                         score_parts[:, u, c, j:j + 1]).then_inc(scored, 1)
                        high = gh[0:P, bass.ds(t, 1), cols].rearrange("p o n -> p (o n)")
                        low = gl[0:P, bass.ds(t, 1), cols].rearrange("p o n -> p (o n)")
                        dve.tensor_tensor(low, acc[u][j][0:P, :], high.bitcast(F32), ALU.subtract).then_inc(acc_free, 1)
                if result == "scores":
                    dve.wait_ge(scored, 4 * t + 4)
                    dve.tensor_tensor(scores_sb[:, bass.ds(t, 1), :].rearrange("p o c -> p (o c)"), score_parts[:, u, :, 0],
                                      score_parts[:, u, :, 1], ALU.add).then_inc(score_ready, 1)

            norm(0, 0, 0)
            turn(0, 0)
            for k in range(K):
                dve.wait_ge(w_high, k + 1)
                dve.tensor_tensor(wl[:, k, :], raw[:, k, :], wh[:, k, :].bitcast(F32), ALU.subtract).then_inc(w_low, 1)
            norm(1, 1, 0)
            turn(1, 1)
            if result == "scores":
                dve.wait_ge(extra, 16)
            with dve.Fori(0, T // 2 - 1) as pair:
                for u in range(2):
                    norm(pair * 2 + (u + 2), u, pair + 1)
                    result_of(pair * 2 + u, u, pair)
                    turn(pair * 2 + (u + 2), u)
            for t in (T - 2, T - 1):
                result_of(t, t % 2, T // 2 - 1)

        @block.tensor
        def _(pe):
            pe.wait_ge(ident_ready, 1)

            def turn(t, u, pair):
                if normalize:
                    pe.wait_ge(xn_ready, t + 1)
                else:
                    pe.wait_ge(x_loaded[u], 16 * (pair + 1))
                pe.wait_ge(xt_low, t)
                for k in range(K):
                    ins = pe.transpose(turned[k // 4][:, k % 4, :], xn_of(u)[:, k * 128:(k + 1) * 128], ident[:, :])
                    if k == K - 1:
                        ins.then_inc(turned_ready, 1)

            def products(t, u, j, first):
                if not first:
                    pe.wait_ge(y_ready if result == "residual" else acc_free, 2 * t + j - 3)
                if j == 0:
                    pe.wait_ge(xt_low, t + 1)
                for k in range(K):
                    if isinstance(t, int) and t == 0 and j == 0:
                        pe.wait_ge(w_low, k + 1)
                    cols = slice(j * H, (j + 1) * H)
                    pe.matmul(acc[u][j][0:P, :], xt[u][:, 0, k, :], wh[:, k, cols], start=k == 0, stop=False)
                    pe.matmul(acc[u][j][0:P, :], xt[u][:, 0, k, :], wl[:, k, cols], start=False, stop=False)
                    ins = pe.matmul(acc[u][j][0:P, :], xt[u][:, 1, k, :], wh[:, k, cols], start=False, stop=k == K - 1)
                ins.then_inc(acc_ready, 1)

            turn(0, 0, 0)
            products(0, 0, 0, True)
            turn(1, 1, 0)
            products(0, 0, 1, True)
            products(1, 1, 0, True)
            turn(2, 0, 1)
            products(1, 1, 1, True)
            with pe.Fori(1, T // 2 - 1) as pair:
                for u in range(2):
                    t = pair * 2 + u
                    products(t, u, 0, False)
                    turn(t + 1, 1 - u, pair + u)
                    products(t, u, 1, False)
            products(T - 2, 0, 0, False)
            turn(T - 1, 1, T // 2 - 1)
            products(T - 2, 0, 1, False)
            products(T - 1, 1, 0, False)
            products(T - 1, 1, 1, False)


def aggregate_phase(nc, name, xt_in, counts_by_src, deg_inv, bias, residual, out, raw, wh, wl, gh, gl,
                    raw_loaded, loads, next_w, own_w=None, unfold=None):
    sem = lambda s: nc.alloc_semaphore(f"{name}_{s}")
    with ExitStack() as ctx:
        ps = lambda s, shape: ctx.enter_context(nc.psum_tensor(f"{name}_{s}", shape, F32))
        local = Map(nc, LOCAL_AT, name)
        xt = local("xt", [128, 2, K, P], F32R)
        counts = local("counts", [P, T, P], F32R)
        bias_row = local("bias_row", [P, D])
        x = local("x", [P, D]) if residual is not None else None
        mean = [local(f"mean{j}", [P, H]) for j in range(2)]
        y = local("y", [P, D])
        dinv = local("dinv", [P, T])
        if unfold is not None:
            C, B, E = 4, 32, 16
            KT = H // 128
            zero, taken = local("zero", [128, 1]), local("taken", [128, 1])
            local = Map(nc, RAW_AT, f"{name}_unfold")
            first = local("first", [128, 2, KT, C, B])
            second = local("second", [128, 2, C, E])
            terms = local("terms", [128, C, B, E])
            w_part = [local(f"w{i}", [128, H]) for i in range(2)]
            minus = local("minus", [128, H])
            assert local.at <= WH_AT
            zeroed = sem("zeroed")
            trains_loaded = sem("trains_loaded")
            unfold_step = sem("unfold_step")
            w_stored = sem("w_stored")
        own = [[ps(f"own{u}{j}", [128, 512]) for j in range(2)] for u in range(2)]
        agg = [[ps(f"agg{u}{j}", [128, 512]) for j in range(2)] for u in range(2)]
        once = sem("once")
        xt_loaded = sem("xt_loaded")
        counts_loaded = sem("counts_loaded")
        x_loaded = sem("x_loaded")
        own_ready = sem("own_ready")
        agg_ready = sem("agg_ready")
        mean_scaled = sem("mean_scaled")
        x_biased = sem("x_biased")
        mean_ready = sem("mean_ready")
        y_ready = sem("y_ready")
        y_stored = sem("y_stored")
        w_high = sem("w_high")
        w_low = sem("w_low")

        block = ctx.enter_context(nc.Block())

        @block.sync
        def _(sp):
            def loads_of(t, first):
                if not first:
                    sp.wait_ge(agg_ready, 2 * t)
                sp.dma_start(counts[:, :, :].bitcast(F32),
                             counts_by_src[bass.ds(t, 1), :, :, :].rearrange("o s k d -> (o s) k d")).then_inc(counts_loaded, 16)
                if not first:
                    sp.wait_ge(own_ready, 2 * t)
                sp.dma_start(xt[:, :, :, :].bitcast(F32),
                             xt_in[bass.ds(t, 1), :, :, :, :].rearrange("o p a k n -> (o p) a k n")).then_inc(xt_loaded, 16)
                if residual is not None:
                    if not first:
                        sp.wait_ge(mean_ready, 2 * t)
                    sp.dma_start(x[:, :], node_rows(residual, t)).then_inc(x_loaded, 16)

            def store(t):
                sp.wait_ge(y_ready, 2 * t + 2)
                sp.dma_start(node_rows(out, t), y[:, :]).then_inc(y_stored, 16)

            loads_of(0, True)
            with sp.Fori(1, T - 1) as t:
                loads_of(t, False)
                store(t - 1)
            loads_of(T - 1, False)
            if unfold is not None:
                sp.wait_ge(w_stored, 64 * KT)
                if next_w is not None:
                    sp.dma_start(raw[:, :, :], next_w.rearrange("(k p) n -> p k n", p=128)).then_inc(raw_loaded, 16)
            store(T - 2)
            store(T - 1)
            sp.wait_ge(y_stored, 16 * T)

        @block.gpsimd
        def _(pool):
            pool.dma_start(bias_row[:, :], bias.broadcast_to([P, D])).then_inc(once, 16)
            pool.dma_start(dinv[:, :], deg_inv).then_inc(once, 16)
            pool.wait_ge(once, 32)

            def tile(t):
                for j in range(2):
                    cols = slice(j * H, (j + 1) * H)
                    if residual is not None:
                        if j == 0:
                            pool.wait_ge(x_loaded, 16 * t + 16)
                            pool.tensor_tensor(x[:, :], x[:, :], bias_row[:, :], ALU.add).then_inc(x_biased, 1)
                            pool.wait_ge(x_biased, t + 1)
                        pool.wait_ge(mean_scaled, 2 * t + j + 1)
                        pool.tensor_tensor(mean[j][:, :], mean[j][:, :], x[:, cols], ALU.add).then_inc(mean_ready, 1)
                    else:
                        pool.wait_ge(mean_scaled, 2 * t + j + 1)
                        pool.tensor_tensor(mean[j][:, :], mean[j][:, :], bias_row[:, cols], ALU.add).then_inc(mean_ready, 1)

            def unfold_tile(k):
                n = [0]

                def then(ins):
                    n[0] += 1
                    ins.then_inc(unfold_step, 1)
                    pool.wait_ge(unfold_step, 7 * k + n[0])

                pool.wait_ge(w_stored, 64 * k)
                for part in range(2):
                    if part:
                        pool.wait_ge(unfold_step, 7 * k + 3)
                    then(pool.tensor_tensor(terms[:, :, :, :],
                                            first[:, part, bass.ds(k, 1), :, :].rearrange("p o c b -> p (o c) b").unsqueeze(3).broadcast_to([128, C, B, E]),
                                            second[:, part, :, :].unsqueeze(2).broadcast_to([128, C, B, E]), ALU.mult))
                    then(pool.tensor_tensor(terms[:, 0:2, :, :], terms[:, 0:2, :, :], terms[:, 2:4, :, :], ALU.add))
                    then(pool.tensor_tensor(w_part[part][:, :], terms[:, 0, :, :].rearrange("p b e -> p (b e)"),
                                            terms[:, 1, :, :].rearrange("p b e -> p (b e)"), ALU.add))
                then(pool.tensor_tensor(minus[:, :], zero[:, :].broadcast_to([128, H]), w_part[1][:, :], ALU.subtract))
                pool.tensor_tensor(taken[:, :], zero[:, :], zero[:, :], ALU.add)
                for src, i, j in ((w_part[0], 0, 0), (w_part[0], 1, 1), (w_part[1], 0, 1), (minus, 1, 0)):
                    pool.dma_start(unfold[2][bass.ds(k * 128 + i * H, 128), j * H:(j + 1) * H], src[:, :]).then_inc(w_stored, 16)

            if unfold is None:
                with pool.Fori(0, T) as t:
                    tile(t)
            else:
                pool.wait_ge(w_low, K)
                for part in range(2):
                    pool.dma_start(first[:, part, :, :, :].rearrange("p k c b -> p k (c b)"),
                                   unfold[0][part].rearrange("(k p) n -> p k n", p=128)).then_inc(trains_loaded, 16)
                    pool.dma_start(second[:, part, :, :].rearrange("p c e -> p (c e)"), unfold[1][part]).then_inc(trains_loaded, 16)
                pool.memset(zero[:, :], 0.0).then_inc(zeroed, 1)
                pool.wait_ge(zeroed, 1)
                pool.wait_ge(trains_loaded, 64)
                with pool.Fori(0, KT) as pair:
                    tile(pair * 2)
                    tile(pair * 2 + 1)
                    unfold_tile(pair)
                for t in range(2 * KT, T):
                    tile(t)

        @block.scalar
        def _(act):
            if own_w is not None:
                act.dma_start(raw[:, :, :], own_w.rearrange("(k p) n -> p k n", p=128)).then_inc(raw_loaded, 16)
            act.wait_ge(raw_loaded, 16 * loads)
            for k in range(K):
                act.activation(wh[:, k, :], raw[:, k, :], ACT.Copy).then_inc(w_high, 1)
            act.wait_ge(once, 32)
            if next_w is not None and unfold is None:
                act.wait_ge(w_low, K)
                act.dma_start(raw[:, :, :], next_w.rearrange("(k p) n -> p k n", p=128)).then_inc(raw_loaded, 16)
            with act.Fori(0, T // 2) as pair:
                for u in range(2):
                    t = pair * 2 + u
                    act.wait_ge(y_ready, 2 * t)
                    act.wait_ge(agg_ready, 2 * t + 2)
                    for j in range(2):
                        act.activation(mean[j][:, :], agg[u][j][0:P, :], ACT.Copy,
                                       scale=dinv[:, bass.ds(t, 1)]).then_inc(mean_scaled, 1)

        @block.vector
        def _(dve):
            for k in range(K):
                dve.wait_ge(w_high, k + 1)
                dve.tensor_tensor(wl[:, k, :], raw[:, k, :], wh[:, k, :].bitcast(F32), ALU.subtract).then_inc(w_low, 1)
            with dve.Fori(0, T // 2) as pair:
                for u in range(2):
                    t = pair * 2 + u
                    for j in range(2):
                        dve.wait_ge(mean_ready, 2 * t + j + 1)
                        if j == 0:
                            dve.wait_ge(own_ready, 2 * t + 2)
                            dve.wait_ge(y_stored, 16 * t)
                        dve.tensor_tensor(y[:, j * H:(j + 1) * H], own[u][j][0:P, :], mean[j][:, :], ALU.add).then_inc(y_ready, 1)

        @block.tensor
        def _(pe):
            def products(t, u, first, split):
                pe.wait_ge(counts_loaded, 16 * t + 16)
                for j in range(2):
                    cols = slice(j * H, (j + 1) * H)
                    if not first:
                        pe.wait_ge(y_ready, 2 * t + j - 3)
                    for k in range(T):
                        pe.matmul(agg[u][j][0:P, :], counts[:, k, :], gh[0:P, k, cols], start=k == 0, stop=False)
                        ins = pe.matmul(agg[u][j][0:P, :], counts[:, k, :], gl[0:P, k, cols], start=False, stop=k == T - 1)
                    ins.then_inc(agg_ready, 1)
                pe.wait_ge(xt_loaded, 16 * t + 16)
                for j in range(2):
                    cols = slice(j * H, (j + 1) * H)
                    for k in range(K):
                        if split and j == 0:
                            pe.wait_ge(w_low, k + 1)
                        pe.matmul(own[u][j][0:P, :], xt[:, 0, k, :], wh[:, k, cols], start=k == 0, stop=False)
                        pe.matmul(own[u][j][0:P, :], xt[:, 0, k, :], wl[:, k, cols], start=False, stop=False)
                        ins = pe.matmul(own[u][j][0:P, :], xt[:, 1, k, :], wh[:, k, cols], start=False, stop=k == K - 1)
                    ins.then_inc(own_ready, 1)

            products(0, 0, True, True)
            products(1, 1, True, False)
            with pe.Fori(1, T // 2) as pair:
                for u in range(2):
                    products(pair * 2 + u, u, False, False)


F16 = mybir.dt.float16
I32 = mybir.dt.int32
EDGE_TILE = 128
TILES = 4
CHUNK = TILES * EDGE_TILE
EDGES = 21250
CHUNKS = -(-EDGES // CHUNK)
NONE = 2047


class GraphBuffers:

    def __init__(self, nc):
        place = Map(nc, RAW_AT, "graph")
        self.place = place
        self.node = place("node", [128, N], F16)
        self.src = place("src", [128, TILES * CHUNKS])
        self.dst = place("dst", [128, TILES * CHUNKS])
        self.bounds = place("bounds", [1, 2, T], I32)


def prepare_phase(nc, name, graph, edges_dst_chunks, edges_src_cols, edges_dst_cols, first_w, raw, wh, wl):
    sem = lambda s: nc.alloc_semaphore(f"{name}_{s}")
    with ExitStack() as ctx:
        local = Map(nc, GH_AT, name)
        chunks_i = local("chunks_i", [CHUNKS, CHUNK], I32)
        src_i = local("src_i", [128, TILES * CHUNKS], I32)
        dst_i = local("dst_i", [128, TILES * CHUNKS], I32)
        chunks_f = local("chunks_f", [CHUNKS, CHUNK])
        src_f = local("src_f", [128, TILES * CHUNKS])
        dst_f = local("dst_f", [128, TILES * CHUNKS])
        node_i = local("node_i", [128, N], I32)
        square = local("square", [128, 128], I32)
        ident = local("ident", [128, 128])
        block_i = local("block_i", [1, T, CHUNKS], I32)
        block_at = local("block_at", [1, T, CHUNKS])
        chunk_i = local("chunk_i", [1, T, CHUNKS], I32)
        chunk_at = local("chunk_at", [1, T, CHUNKS])
        least = local("least", [CHUNKS, 1])
        most = local("most", [CHUNKS, 1])
        rows = local("rows", [1, 2, CHUNKS])
        local = Map(nc, LOCAL_AT, name)
        work = [local(f"work{i}", [1, T, CHUNKS]) for i in range(4)]
        bounds = local("bounds", [1, 2, T])
        rows_ps = ctx.enter_context(nc.psum_tensor(f"{name}_rows_ps", [128, 512], F32))

        raw_in = sem("raw_in")
        chunks_loaded = sem("chunks_loaded")
        cols_loaded = sem("cols_loaded")
        made = sem("made")
        step = sem("step")
        rows_up = sem("rows_up")
        bounds_made = sem("bounds_made")
        w_high = sem("w_high")
        w_low = sem("w_low")

        block = ctx.enter_context(nc.Block())

        @block.sync
        def _(sp):
            sp.dma_start(chunks_i[:, :], edges_dst_chunks).then_inc(chunks_loaded, 16)
            sp.dma_start(src_i[:, :], edges_src_cols).then_inc(cols_loaded, 16)
            sp.dma_start(dst_i[:, :], edges_dst_cols).then_inc(cols_loaded, 16)

        @block.gpsimd
        def _(pool):
            pool.iota(block_i[:, :, :], pattern=[[P, T], [0, CHUNKS]], base=0, channel_multiplier=0).then_inc(made, 1)
            pool.iota(chunk_i[:, :, :], pattern=[[0, T], [1, CHUNKS]], base=0, channel_multiplier=0).then_inc(made, 1)
            pool.iota(square[:, :], pattern=[[1, 128]], base=0, channel_multiplier=-1).then_inc(made, 1)
            pool.iota(node_i[:, :], pattern=[[1, N]], base=0, channel_multiplier=0).then_inc(made, 1)

        @block.scalar
        def _(act):
            act.dma_start(raw[:, :, :], first_w.rearrange("(k p) n -> p k n", p=128)).then_inc(raw_in, 16)
            act.wait_ge(raw_in, 16)
            for k in range(K):
                act.activation(wh[:, k, :], raw[:, k, :], ACT.Copy).then_inc(w_high, 1)

        @block.tensor
        def _(pe):
            pe.wait_ge(step, 6)
            pe.matmul(rows_ps[0:1, 0:CHUNKS], least[:, :], ident[0:CHUNKS, 0:CHUNKS], start=True, stop=True)
            pe.matmul(rows_ps[0:1, CHUNKS:2 * CHUNKS], most[:, :], ident[0:CHUNKS, 0:CHUNKS],
                      start=True, stop=True).then_inc(rows_up, 1)

        @block.vector
        def _(dve):
            n = [0]

            def then(ins, wait=True):
                n[0] += 1
                ins.then_inc(step, 1)
                if wait:
                    dve.wait_ge(step, n[0])

            dve.wait_ge(made, 3)
            then(dve.tensor_scalar(ident[:, :], square[:, :], 0.0, None, ALU.is_equal), False)
            then(dve.tensor_copy(block_at[:, :, :], block_i[:, :, :]), False)
            then(dve.tensor_copy(chunk_at[:, :, :], chunk_i[:, :, :]), False)
            dve.wait_ge(chunks_loaded, 16)
            then(dve.tensor_copy(chunks_f[:, :], chunks_i[:, :]))
            then(dve.tensor_reduce(least[:, :], chunks_f[:, :], AX.X, ALU.min), False)
            then(dve.tensor_reduce(most[:, :], chunks_f[:, :], AX.X, ALU.max), False)
            dve.wait_ge(rows_up, 1)
            then(dve.tensor_copy(rows[:, :, :], rows_ps[0:1, 0:2 * CHUNKS].rearrange("p (a c) -> p a c", a=2)), False)
            low = rows[:, 0:1, :].broadcast_to([1, T, CHUNKS])
            high = rows[:, 1:2, :].broadcast_to([1, T, CHUNKS])
            then(dve.tensor_scalar(work[0][:, :, :], block_at[:, :, :], float(P), None, ALU.add))
            then(dve.tensor_tensor(work[1][:, :, :], low, work[0][:, :, :], ALU.is_lt), False)
            then(dve.tensor_tensor(work[2][:, :, :], high, block_at[:, :, :], ALU.is_ge))
            then(dve.tensor_tensor(work[3][:, :, :], work[1][:, :, :], work[2][:, :, :], ALU.mult))
            then(dve.tensor_scalar(work[0][:, :, :], chunk_at[:, :, :], float(CHUNKS - 1), None, ALU.subtract), False)
            then(dve.tensor_scalar(work[1][:, :, :], chunk_at[:, :, :], 1.0, None, ALU.add))
            then(dve.tensor_tensor(work[2][:, :, :], work[0][:, :, :], work[3][:, :, :], ALU.mult))
            then(dve.tensor_tensor(work[0][:, :, :], work[1][:, :, :], work[3][:, :, :], ALU.mult), False)
            then(dve.tensor_reduce(bounds[:, 0, :], work[2][:, :, :], AX.X, ALU.min))
            then(dve.tensor_reduce(bounds[:, 1, :], work[0][:, :, :], AX.X, ALU.max), False)
            then(dve.tensor_scalar(bounds[:, 0, :], bounds[:, 0, :], float(CHUNKS - 1), None, ALU.add))
            then(dve.tensor_scalar(work[0][:, 0, 0:T], bounds[:, 0, :], 1.0, None, ALU.add))
            then(dve.tensor_tensor(bounds[:, 1, :], bounds[:, 1, :], work[0][:, 0, 0:T], ALU.max))
            dve.wait_ge(cols_loaded, 32)
            then(dve.tensor_copy(src_f[:, :], src_i[:, :]), False)
            then(dve.tensor_copy(dst_f[:, :], dst_i[:, :]))
            for k in range(K):
                dve.wait_ge(w_high, k + 1)
                dve.tensor_tensor(wl[:, k, :], raw[:, k, :], wh[:, k, :].bitcast(F32), ALU.subtract).then_inc(w_low, 1)
            dve.wait_ge(w_low, K)
            dve.wait_ge(made, 4)
            dve.tensor_copy(graph.bounds[:, :, :], bounds[:, :, :])
            dve.tensor_copy(graph.src[:, :], src_f[:, :])
            dve.tensor_copy(graph.dst[:, :], dst_f[:, :])
            dve.tensor_copy(graph.node[:, :], node_i[:, :])


def count_project_phase(nc, name, graph, rows, xt_out, wh, wl, gh, gl, counts_by_src, counts_by_dst, deg_inv):
    sem = lambda s: nc.alloc_semaphore(f"{name}_{s}")
    BANKS = [(0, 418), (418, 416), (834, 416)]
    ROUNDS = [(0, 4), (4, 4), (8, 2)]
    with ExitStack() as ctx:
        ps = lambda s, shape: ctx.enter_context(nc.psum_tensor(f"{name}_{s}", shape, F32))
        local = graph.place
        zeros = local("zeros", [128, 128], F16)
        hot_src = [local(f"hot_src{i}", [128, N], F16) for i in range(TILES)]
        hot_dst = [local(f"hot_dst{i}", [128, P], F16) for i in range(TILES)]
        by_dst = [local(f"by_dst{i}", [P, N]) for i in range(2)]
        by_src = local("by_src", [P, T, P], F32R)
        deg = local("deg", [P, T])
        assert local.at <= WH_AT
        local = Map(nc, LOCAL_AT, name)
        xt = [local(f"xt{u}", [128, 2, K, P], F32R) for u in range(2)]
        x = [local(f"x{u}", [P, D]) for u in range(2)]
        ident = local("ident", [P, P])
        square = local("square", [P, P], I32)
        power, eps, waits = (local(s, [P, 1]) for s in ("power", "eps", "waits"))
        stats = [local(f"stats{u}", [P, 12]) for u in range(2)]
        moments = [local(f"moments{u}", [P, 2]) for u in range(2)]
        rstd = [local(f"rstd{u}", [P, 1]) for u in range(2)]
        assert BASE + local.at <= 229344, local.at
        counted = ps("counted", [128, 3, 512])
        acc = [ps(f"acc{j}", [128, 512]) for j in range(2)]
        turned = [ps(f"turned{r}", [128, 4, P]) for r in range(2)]
        count_turned = ps("count_turned", [128, 512])

        made = sem("made")
        consts = sem("consts")
        x_loaded = [sem(f"x_loaded{u}") for u in range(2)]
        stats_ready = sem("stats_ready")
        moments_ready = sem("moments_ready")
        var_eps = sem("var_eps")
        rstd_ready = sem("rstd_ready")
        xn_ready = sem("xn_ready")
        turned_ready = sem("turned_ready")
        xt_high = sem("xt_high")
        xt_low = sem("xt_low")
        xt_stored = [sem(f"xt_stored{u}") for u in range(2)]
        acc_ready = sem("acc_ready")
        acc_high = sem("acc_high")
        acc_free = sem("acc_free")
        hot_ready = sem("hot_ready")
        hot_free = sem("hot_free")
        counted_ready = sem("counted_ready")
        by_dst_ready = sem("by_dst_ready")
        round_ready = sem("round_ready")
        by_src_ready = sem("by_src_ready")
        dst_stored = [sem(f"dst_stored{i}") for i in range(2)]
        src_stored = sem("src_stored")
        deg_ready = sem("deg_ready")
        deg_stored = sem("deg_stored")

        fixed = lambda t: isinstance(t, int)

        def tiles(eng, step):
            for t in range(2):
                step(t, t % 2, t // 2)
            with eng.Fori(0, (T - 4) // 2) as i:
                step(i * 2 + 2, 0, i + 1)
                step(i * 2 + 3, 1, i + 1)
            for t in range(T - 2, T):
                step(t, t % 2, t // 2)

        block = ctx.enter_context(nc.Block())

        @block.sync
        def _(sp):
            def load_x(t, u):
                sp.dma_start(x[u][:, :], node_rows(rows, t)).then_inc(x_loaded[u], 16)

            def store_by_src(t):
                sp.wait_ge(by_src_ready, 3 * t + 3)
                sp.dma_start(counts_by_src[bass.ds(t, 1), :, :, :].rearrange("o s k d -> (o s) k d"),
                             by_src[:, :, :].bitcast(F32)).then_inc(src_stored, 16)

            def step(t, u, q):
                if not (fixed(t) and t == 0):
                    store_by_src(t - 1)
                sp.wait_ge(xt_low, t + 1)
                sp.dma_start(xt_out[bass.ds(t, 1), :, :, :, :].rearrange("o p a k n -> (o p) a k n"),
                             xt[u][:, :, :, :].bitcast(F32)).then_inc(xt_stored[u], 16)
                if not fixed(t) or t + 2 < T:
                    sp.wait_ge(turned_ready, t + 1)
                    load_x(t + 2, u)
                sp.wait_ge(by_dst_ready, t + 1)
                sp.dma_start(counts_by_dst[:, :, bass.ds(t, 1), :].rearrange("t d o s -> d (t o) s"),
                             by_dst[u][:, :].rearrange("d (t s) -> d t s", s=P)).then_inc(dst_stored[u], 16)

            load_x(0, 0)
            load_x(1, 1)
            tiles(sp, step)
            store_by_src(T - 1)
            sp.wait_ge(deg_ready, T + 1)
            sp.dma_start(deg_inv, deg[:, :]).then_inc(deg_stored, 16)
            for u in range(2):
                sp.wait_ge(dst_stored[u], 16 * (T // 2))
                sp.wait_ge(xt_stored[u], 16 * (T // 2))
            sp.wait_ge(src_stored, 16 * T)
            sp.wait_ge(deg_stored, 16)

        @block.gpsimd
        def _(pool):
            pool.iota(square[:, :], pattern=[[1, P]], base=0, channel_multiplier=-1).then_inc(made, 1)
            pool.memset(power[:, :], -0.5).then_inc(made, 1)
            pool.memset(eps[:, :], 1e-5).then_inc(made, 1)
            pool.wait_ge(made, 3)

            def step(t, u, q):
                pool.wait_ge(moments_ready, t + 1)
                pool.tensor_tensor(rstd[u][:, :], moments[u][:, 1:2], eps[:, :], ALU.add).then_inc(var_eps, 1)
                pool.wait_ge(var_eps, t + 1)
                pool.tensor_tensor(rstd[u][:, :], rstd[u][:, :], power[:, :], ALU.pow).then_inc(rstd_ready, 1)

            tiles(pool, step)

        @block.scalar
        def _(act):
            def turn(t, u, q):
                act.wait_ge(turned_ready, t + 1)
                if not (fixed(t) and t < 2):
                    act.wait_ge(acc_ready, 2 * t - 2)
                    act.wait_ge(xt_stored[u], 16 * q)
                for r in range(2):
                    act.activation(xt[u][:, 0, 4 * r:4 * r + 4, :], turned[r][:, :, :], ACT.Copy).then_inc(xt_high, 1)

            def round_of(t, r):
                k0, kn = ROUNDS[r]
                act.wait_ge(round_ready, 3 * t + r + 1)
                if r == 0 and not (fixed(t) and t == 0):
                    act.wait_ge(src_stored, 16 * t)
                act.activation(by_src[:, k0:k0 + kn, :], count_turned[0:P, 0:kn * P].rearrange("s (k d) -> s k d", d=P),
                               ACT.Copy).then_inc(by_src_ready, 1)

            def high(t, j):
                act.wait_ge(acc_ready, 2 * t + j + 1)
                act.activation(gh[0:P, bass.ds(t, 1), j * H:(j + 1) * H].rearrange("p o n -> p (o n)"),
                               acc[j][0:P, :], ACT.Copy).then_inc(acc_high, 1)

            def step(t, u, q):
                act.wait_ge(counted_ready, t + 1)
                if not (fixed(t) and t < 2):
                    act.wait_ge(dst_stored[u], 16 * q)
                    act.wait_ge(deg_ready, t - 1)
                for j, (at, n) in enumerate(BANKS):
                    ins = act.activation(by_dst[u][:, at:at + n], counted[0:P, j, 0:n], ACT.Copy)
                ins.then_inc(by_dst_ready, 1)
                if not fixed(t) or t + 1 < T:
                    turn(t + 1, 1 - u, q + u)
                round_of(t, 0)
                high(t, 0)
                round_of(t, 1)
                high(t, 1)
                round_of(t, 2)

            turn(0, 0, 0)
            tiles(act, step)

        @block.vector
        def _(dve):
            dve.wait_ge(made, 3)
            dve.tensor_scalar(ident[:, :], square[:, :], 0.0, None, ALU.is_equal).then_inc(consts, 1)
            dve.memset(zeros[:, :], 0.0).then_inc(consts, 1)
            done = dve.alloc_register(f"{name}_hot_made")
            dve.reg_mov(done, 0)

            def norm(t, u, q):
                dve.wait_ge(x_loaded[u], 16 * (q + 1))
                for j in range(2):
                    dve.bn_stats(stats[u][:, 6 * j:6 * j + 6], x[u][:, j * H:(j + 1) * H]).then_inc(stats_ready, 1)
                dve.wait_ge(stats_ready, 2 * t + 2)
                dve.memset(waits[:, :], 0.0)
                dve.bn_aggr(moments[u][:, :], stats[u][:, :]).then_inc(moments_ready, 1)
                dve.wait_ge(rstd_ready, t + 1)
                dve.tensor_scalar(x[u][:, :], x[u][:, :], moments[u][:, 0:1], rstd[u][:, 0:1],
                                  ALU.subtract, ALU.mult).then_inc(xn_ready, 1)

            def turn(t, u):
                for r in range(2):
                    dve.wait_ge(xt_high, 2 * t + r + 1)
                    ins = dve.tensor_tensor(xt[u][:, 1, 4 * r:4 * r + 4, :], turned[r][:, :, :],
                                            xt[u][:, 0, 4 * r:4 * r + 4, :].bitcast(F32), ALU.subtract)
                ins.then_inc(xt_low, 1)

            def low(t, j):
                dve.wait_ge(acc_high, 2 * t + j + 1)
                part = lambda g: g[0:P, bass.ds(t, 1), j * H:(j + 1) * H].rearrange("p o n -> p (o n)")
                dve.tensor_tensor(part(gl), acc[j][0:P, :], part(gh).bitcast(F32), ALU.subtract).then_inc(acc_free, 1)

            def hots(t):
                first = dve.value_load(graph.bounds[0:1, 0, bass.ds(t, 1)], min_val=0, max_val=CHUNKS - 1)
                last = dve.value_load(graph.bounds[0:1, 1, bass.ds(t, 1)], min_val=1, max_val=CHUNKS)
                with dve.Fori(first, last) as c:
                    for h in range(TILES):
                        dve.wait_ge(hot_free, dve.snap(done) + h)
                        dve.tensor_scalar(hot_dst[h][:, :], graph.node[:, bass.ds(t * P, P)],
                                          graph.dst[:, bass.ds(c * TILES + h, 1)], None, ALU.is_equal)
                        dve.tensor_scalar(hot_src[h][:, :], graph.node[:, :],
                                          graph.src[:, bass.ds(c * TILES + h, 1)], None, ALU.is_equal).then_inc(hot_ready, 1)
                    dve.reg_add(done, done, TILES)

            def rest(t, u):
                low(t, 0)
                low(t, 1)
                dve.wait_ge(by_dst_ready, t + 1)
                dve.tensor_reduce(deg[:, bass.ds(t, 1)], by_dst[u][:, :], AX.X, ALU.add).then_inc(deg_ready, 1)

            def step(t, u, q):
                hots(t)
                if not (fixed(t) and t == 0):
                    rest(t - 1, 1 - u)
                if not fixed(t) or t + 1 < T:
                    turn(t + 1, 1 - u)
                if not fixed(t) or t + 2 < T:
                    norm(t + 2, u, q + 1)

            norm(0, 0, 0)
            turn(0, 0)
            norm(1, 1, 0)
            tiles(dve, step)
            rest(T - 1, 1)
            dve.wait_ge(deg_ready, T)
            dve.tensor_scalar(deg[:, :], deg[:, :], 1.0, None, ALU.max).then_inc(consts, 1)
            dve.wait_ge(consts, 3)
            dve.reciprocal(deg[:, :], deg[:, :]).then_inc(deg_ready, 1)

        @block.tensor
        def _(pe):
            pe.wait_ge(consts, 2)
            pe.sem_inc(hot_free, TILES - 1)
            done = pe.alloc_register(f"{name}_hot_used")
            pe.reg_mov(done, 0)

            def turn(t, u):
                pe.wait_ge(xn_ready, t + 1)
                pe.wait_ge(xt_low, t)
                for k in range(K):
                    ins = pe.transpose(turned[k // 4][:, k % 4, :], x[u][:, k * 128:(k + 1) * 128], ident[:, :])
                ins.then_inc(turned_ready, 1)

            def count(t):
                first = pe.value_load(graph.bounds[0:1, 0, bass.ds(t, 1)], min_val=0, max_val=CHUNKS - 1)
                last = pe.value_load(graph.bounds[0:1, 1, bass.ds(t, 1)], min_val=1, max_val=CHUNKS)
                if not (fixed(t) and t == 0):
                    pe.wait_ge(by_dst_ready, t)
                for j, (at, n) in enumerate(BANKS):
                    pe.matmul(counted[:, j, 0:n], zeros[:, :], graph.node[:, 0:n], start=True, stop=False)
                with pe.Fori(first, last) as c:
                    for h in range(TILES):
                        pe.wait_ge(hot_ready, pe.snap(done) + (h + 1))
                        for j, (at, n) in enumerate(BANKS):
                            mm = pe.matmul(counted[0:P, j, 0:n], hot_dst[h][:, :], hot_src[h][:, at:at + n],
                                           start=False, stop=False)
                        mm.then_inc(hot_free, 1)
                    pe.reg_add(done, done, TILES)
                for j, (at, n) in enumerate(BANKS):
                    mm = pe.matmul(counted[:, j, 0:n], zeros[:, :], graph.node[:, 0:n], start=False, stop=True)
                mm.then_inc(counted_ready, 1)

            def round_of(t, u, r):
                if r == 0:
                    pe.wait_ge(by_dst_ready, t + 1)
                if not (fixed(t) and t == 0 and r == 0):
                    pe.wait_ge(by_src_ready, 3 * t + r)
                k0, kn = ROUNDS[r]
                for k in range(k0, k0 + kn):
                    mm = pe.transpose(count_turned[0:P, (k - k0) * P:(k - k0 + 1) * P],
                                      by_dst[u][:, k * P:(k + 1) * P], ident[:, :])
                mm.then_inc(round_ready, 1)

            def products(t, u, j):
                if not (fixed(t) and t == 0):
                    pe.wait_ge(acc_free, 2 * t + j - 1)
                pe.wait_ge(xt_low, t + 1)
                cols = slice(j * H, (j + 1) * H)
                for k in range(K):
                    pe.matmul(acc[j][0:P, :], xt[u][:, 0, k, :], wh[:, k, cols], start=k == 0, stop=False)
                    pe.matmul(acc[j][0:P, :], xt[u][:, 0, k, :], wl[:, k, cols], start=False, stop=False)
                    ins = pe.matmul(acc[j][0:P, :], xt[u][:, 1, k, :], wh[:, k, cols], start=False, stop=k == K - 1)
                ins.then_inc(acc_ready, 1)

            def step(t, u, q):
                count(t)
                if not fixed(t) or t + 1 < T:
                    turn(t + 1, 1 - u)
                round_of(t, u, 0)
                products(t, u, 0)
                round_of(t, u, 1)
                products(t, u, 1)
                round_of(t, u, 2)

            turn(0, 0)
            tiles(pe, step)


def attention_phase(nc, name, rows, counts_by_dst, scores, norm_w, router_t, gh, gl, base, tokens, logits):
    sem = lambda s: nc.alloc_semaphore(f"{name}_{s}")
    EXPERTS = 8
    LARGEST = 3.4028234e38
    with ExitStack() as ctx:
        ps = lambda s, shape: ctx.enter_context(nc.psum_tensor(f"{name}_{s}", shape, F32))
        local = Map(nc, RAW_AT, name)
        counts = [local(f"counts{u}", [P, T, P]) for u in range(2)]
        z = [local(f"z{u}", [P, T, P]) for u in range(2)]
        e = local("e", [P, T, P])
        weight = local("weight", [P, T, P])
        ph = [local(f"ph{u}", [P, T, P], F32R) for u in range(2)]
        pl = [local(f"pl{u}", [P, T, P], F32R) for u in range(2)]
        al_row = local("al_row", [P, T, P])
        x = [local(f"x{u}", [P, D]) for u in range(2)]
        low = local("low", [P, D])
        nw_row = local("nw_row", [P, D])
        h = [local(f"h{u}", [P, D]) for u in range(2)]
        assert local.at <= GH_AT, local.at
        local = Map(nc, LOCAL_AT, name)
        y = [local(f"y{u}", [P, D]) for u in range(2)]
        token = [local(f"token{u}", [P, D]) for u in range(2)]
        token_t = local("token_t", [128, K, P])
        ident = local("ident", [P, P])
        square = local("square", [P, P], mybir.dt.int32)
        router = local("router", [128, K, EXPERTS])
        sc = local("sc", [P, T, 2])
        ones = local("ones", [P, 2], F32R)
        ones_f = local("ones_f", [P, 2])
        small = lambda s: [local(f"{s}{u}", [P, 1]) for u in range(2)]
        total, rtotal, rstd, rrms, meansq = small("total"), small("rtotal"), small("rstd"), small("rrms"), small("meansq")
        stats = [local(f"stats{u}", [P, 12]) for u in range(2)]
        moments = [local(f"moments{u}", [P, 2]) for u in range(2)]
        power, eps, eps_rms, waits = (local(s, [P, 1]) for s in ("power", "eps", "eps_rms", "waits"))
        logit_rows = local("logit_rows", [P, T, EXPERTS])
        assert BASE + local.at <= 229344, local.at
        acc = [[ps(f"acc{u}{j}", [128, 512]) for j in range(2)] for u in range(2)]
        turned = [ps(f"turned{r}", [128, 4, P]) for r in range(2)]
        sums = ps("sums", [128, 2])
        logit_ps = ps("logit_ps", [128, EXPERTS])

        once = sem("once")
        made = sem("made")
        consts = sem("consts")
        row_ready = sem("row_ready")
        al_ready = sem("al_ready")
        counts_loaded = [sem(f"counts_loaded{u}") for u in range(2)]
        x_loaded = [sem(f"x_loaded{u}") for u in range(2)]
        z_ready = sem("z_ready")
        leaky_ready = sem("leaky_ready")
        e_ready = sem("e_ready")
        weight_ready = sem("weight_ready")
        ph_ready = sem("ph_ready")
        pl_ready = sem("pl_ready")
        acc_ready = sem("acc_ready")
        sums_ready = sem("sums_ready")
        total_ready = sem("total_ready")
        rtotal_ready = sem("rtotal_ready")
        h_ready = sem("h_ready")
        low_ready = sem("low_ready")
        exp_ready = sem("exp_ready")
        elu_ready = sem("elu_ready")
        x3_ready = sem("x3_ready")
        stats_ready = sem("stats_ready")
        moments_ready = sem("moments_ready")
        pool_step = sem("pool_step")
        rstd_ready = sem("rstd_ready")
        y_ready = sem("y_ready")
        meansq_ready = sem("meansq_ready")
        rrms_ready = sem("rrms_ready")
        token_ready = sem("token_ready")
        base_ready = sem("base_ready")
        turned_ready = sem("turned_ready")
        token_t_ready = sem("token_t_ready")
        logit_ready = sem("logit_ready")
        logit_read = sem("logit_read")
        base_stored = [sem(f"base_stored{u}") for u in range(2)]
        token_stored = [sem(f"token_stored{u}") for u in range(2)]

        def tiles(eng, step):
            for t in range(3):
                step(t, t % 2, t // 2)
            with eng.Fori(0, (T - 6) // 2) as i:
                step(i * 2 + 3, 1, i + 1)
                step(i * 2 + 4, 0, i + 2)
            for t in range(T - 3, T):
                step(t, t % 2, t // 2)

        fixed = lambda t: isinstance(t, int)
        block = ctx.enter_context(nc.Block())

        @block.sync
        def _(sp):
            sp.dma_start(sc[:, :, :], scores).then_inc(once, 16)
            sp.dma_start(nw_row[:, :], norm_w.broadcast_to([P, D])).then_inc(once, 16)
            sp.dma_start(router[:, :, :], router_t.rearrange("p (k e) -> p k e", e=EXPERTS)).then_inc(once, 16)

            def load_counts(t, u):
                sp.dma_start(counts[u][:, :, :], counts_by_dst[bass.ds(t, 1), :, :, :].rearrange("o d k s -> (o d) k s")).then_inc(counts_loaded[u], 16)

            def load_x(t, u):
                sp.dma_start(x[u][:, :], node_rows(rows, t)).then_inc(x_loaded[u], 16)

            def store_token(t, u):
                sp.wait_ge(token_ready, t + 1)
                sp.dma_start(node_rows(tokens, t), token[u][:, :]).then_inc(token_stored[u], 16)

            def step(t, u, q):
                more = not fixed(t) or t + 2 < T
                if not fixed(t) or t + 3 < T:
                    sp.wait_ge(weight_ready, t + 2)
                    load_counts(t + 3, 1 - u)
                if not (fixed(t) and t == 0):
                    store_token(t - 1, 1 - u)
                sp.wait_ge(base_ready, t + 1)
                sp.dma_start(node_rows(base, t), x[u][:, :]).then_inc(base_stored[u], 16)
                if more:
                    sp.wait_ge(base_stored[u], 16 * q + 16)
                    load_x(t + 2, u)

            for t in range(2):
                load_counts(t, t)
                load_x(t, t)
            sp.wait_ge(weight_ready, 1)
            load_counts(2, 0)
            tiles(sp, step)
            store_token(T - 1, (T - 1) % 2)
            for u in range(2):
                sp.wait_ge(token_stored[u], 16 * (T // 2))
                sp.wait_ge(base_stored[u], 16 * (T // 2))
            sp.wait_ge(logit_read, T)
            sp.dma_start(logits, logit_rows[:, :, :]).then_inc(once, 16)
            sp.wait_ge(once, 64)

        @block.gpsimd
        def _(pool):
            pool.iota(square[:, :], pattern=[[1, P]], base=0, channel_multiplier=-1).then_inc(made, 1)
            pool.memset(power[:, :], -0.5).then_inc(made, 1)
            pool.memset(eps[:, :], 1e-5).then_inc(made, 1)
            pool.memset(eps_rms[:, :], 1e-6).then_inc(made, 1)
            pool.memset(ones_f[:, :], 1.0).then_inc(made, 1)
            pool.wait_ge(made, 5)
            pool.wait_ge(al_ready, 3)

            def edge_z(t, u):
                if not (fixed(t) and t < 2):
                    pool.wait_ge(leaky_ready, t - 1)
                pool.tensor_tensor(z[u][:, :, :], al_row[:, bass.ds(t, 1), :].broadcast_to([P, T, P]),
                                   sc[:, :, 1:2].broadcast_to([P, T, P]), ALU.add).then_inc(z_ready, 1)

            def step(t, u, q):
                pool.wait_ge(moments_ready, t + 1)
                pool.tensor_tensor(rstd[u][:, :], moments[u][:, 1:2], eps[:, :], ALU.add).then_inc(pool_step, 1)
                pool.wait_ge(pool_step, 2 * t + 1)
                pool.tensor_tensor(rstd[u][:, :], rstd[u][:, :], power[:, :], ALU.pow).then_inc(rstd_ready, 1)
                if not fixed(t) or t + 3 < T:
                    edge_z(t + 3, 1 - u)
                pool.wait_ge(meansq_ready, t + 1)
                pool.tensor_tensor(rrms[u][:, :], meansq[u][:, :], eps_rms[:, :], ALU.add).then_inc(pool_step, 1)
                pool.wait_ge(pool_step, 2 * t + 2)
                pool.tensor_tensor(rrms[u][:, :], rrms[u][:, :], power[:, :], ALU.pow).then_inc(rrms_ready, 1)
                pool.tensor_tensor(x[u][:, :], x[u][:, :], y[u][:, :], ALU.add).then_inc(base_ready, 1)

            for t in range(3):
                edge_z(t, t % 2)
            tiles(pool, step)

        @block.scalar
        def _(act):
            act.wait_ge(row_ready, 1)
            for r, (k0, kn) in enumerate([(0, 4), (4, 4), (8, 2)]):
                act.activation(al_row[:, k0:k0 + kn, :],
                               acc[r // 2][r % 2][0:P, 0:kn * P].rearrange("p (k n) -> p k n", n=P), ACT.Copy).then_inc(al_ready, 1)

            def edge_exp(t):
                act.wait_ge(leaky_ready, t + 1)
                act.activation(e[:, :, :], e[:, :, :], ACT.Exp, scale=-1.0).then_inc(e_ready, 1)

            def edge_high(t, u):
                act.wait_ge(weight_ready, t + 1)
                act.activation(ph[u][:, :, :], weight[:, :, :], ACT.Copy).then_inc(ph_ready, 1)

            def turn(t):
                act.wait_ge(turned_ready, t + 1)
                act.wait_ge(logit_ready, t)
                for r in range(2):
                    ins = act.activation(token_t[:, 4 * r:4 * r + 4, :], turned[r][:, :, :], ACT.Copy)
                ins.then_inc(token_t_ready, 1)

            def logit(t):
                act.wait_ge(logit_ready, t + 1)
                act.activation(logit_rows[:, bass.ds(t, 1), :].rearrange("p o n -> p (o n)"),
                               logit_ps[0:P, :], ACT.Copy).then_inc(logit_read, 1)

            def step(t, u, q):
                ahead = not fixed(t) or t + 2 < T
                if ahead:
                    edge_exp(t + 2)
                act.wait_ge(acc_ready, 2 * t + 2)
                act.wait_ge(rtotal_ready, t + 1)
                for j in range(2):
                    act.activation(h[u][:, j * H:(j + 1) * H], acc[u][j][0:P, :], ACT.Copy, scale=rtotal[u][:, 0:1]).then_inc(h_ready, 1)
                if ahead:
                    edge_high(t + 2, u)
                act.wait_ge(low_ready, t + 1)
                act.activation(low[:, :], low[:, :], ACT.Exp).then_inc(exp_ready, 1)
                if not (fixed(t) and t < 3):
                    logit(t - 3)
                if not (fixed(t) and t < 2):
                    turn(t - 2)
                act.wait_ge(y_ready, t + 1)
                act.activation(low[:, :], y[u][:, :], ACT.Square, scale=D ** -0.5, accum_out=meansq[u][:, 0:1]).then_inc(meansq_ready, 1)

            for t in range(2):
                edge_exp(t)
                edge_high(t, t)
            tiles(act, step)
            logit(T - 3)
            for t in (T - 2, T - 1):
                turn(t)
                logit(t)

        @block.vector
        def _(dve):
            dve.wait_ge(made, 5)
            dve.tensor_scalar(ident[:, :], square[:, :], 0.0, None, ALU.is_equal).then_inc(consts, 1)
            dve.tensor_copy(ones[:, :], ones_f[:, :]).then_inc(consts, 1)

            def edge_leaky(t, u):
                dve.wait_ge(z_ready, t + 1)
                dve.wait_ge(weight_ready, t)
                dve.scalar_tensor_tensor(e[:, :, :], z[u][:, :, :], 0.1, z[u][:, :, :], ALU.mult, ALU.max).then_inc(leaky_ready, 1)

            def edge_weight(t, u, q):
                dve.wait_ge(e_ready, t + 1)
                dve.wait_ge(counts_loaded[u], 16 * q + 16)
                dve.wait_ge(pl_ready, t)
                dve.scalar_tensor_tensor(weight[:, :, :], e[:, :, :], LARGEST, counts[u][:, :, :], ALU.min, ALU.mult).then_inc(weight_ready, 1)

            def edge_low(t, u):
                dve.wait_ge(ph_ready, t + 1)
                dve.tensor_tensor(pl[u][:, :, :], weight[:, :, :], ph[u][:, :, :].bitcast(F32), ALU.subtract).then_inc(pl_ready, 1)

            def make_token(t, u, q):
                dve.wait_ge(rrms_ready, t + 1)
                if not (fixed(t) and t < 2):
                    dve.wait_ge(token_stored[u], 16 * q)
                    dve.wait_ge(turned_ready, t - 1)
                dve.scalar_tensor_tensor(token[u][:, :], y[u][:, :], rrms[u][:, 0:1], nw_row[:, :], ALU.mult, ALU.mult).then_inc(token_ready, 1)

            def step(t, u, q):
                ahead = not fixed(t) or t + 2 < T
                if ahead:
                    edge_leaky(t + 2, u)
                dve.wait_ge(sums_ready, t + 1)
                dve.tensor_scalar(total[u][:, :], sums[0:P, 0:1], 1e-5, None, ALU.add).then_inc(total_ready, 1)
                dve.wait_ge(total_ready, t + 1)
                dve.reciprocal(rtotal[u][:, :], total[u][:, :]).then_inc(rtotal_ready, 1)
                if ahead:
                    edge_weight(t + 2, u, q + 1)
                dve.wait_ge(h_ready, 2 * t + 2)
                dve.wait_ge(meansq_ready, t)
                dve.tensor_scalar(low[:, :], h[u][:, :], 0.0, None, ALU.min).then_inc(low_ready, 1)
                if ahead:
                    edge_low(t + 2, u)
                dve.wait_ge(exp_ready, t + 1)
                dve.scalar_tensor_tensor(h[u][:, :], h[u][:, :], 0.0, low[:, :], ALU.max, ALU.add).then_inc(elu_ready, 1)
                dve.wait_ge(elu_ready, t + 1)
                dve.wait_ge(x_loaded[u], 16 * q + 16)
                dve.scalar_tensor_tensor(x[u][:, :], h[u][:, :], -1.0, x[u][:, :], ALU.add, ALU.add).then_inc(x3_ready, 1)
                dve.wait_ge(x3_ready, t + 1)
                for j in range(2):
                    dve.bn_stats(stats[u][:, 6 * j:6 * j + 6], x[u][:, j * H:(j + 1) * H]).then_inc(stats_ready, 1)
                dve.wait_ge(stats_ready, 2 * t + 2)
                dve.memset(waits[:, :], 0.0)
                dve.bn_aggr(moments[u][:, :], stats[u][:, :]).then_inc(moments_ready, 1)
                if not (fixed(t) and t == 0):
                    make_token(t - 1, 1 - u, q - 1 + u)
                dve.wait_ge(rstd_ready, t + 1)
                if not (fixed(t) and t < 2):
                    dve.wait_ge(base_ready, t - 1)
                dve.tensor_scalar(y[u][:, :], x[u][:, :], moments[u][:, 0:1], rstd[u][:, 0:1], ALU.subtract, ALU.mult).then_inc(y_ready, 1)

            for t in range(2):
                edge_leaky(t, t)
                edge_weight(t, t, 0)
                edge_low(t, t)
            dve.wait_ge(once, 48)
            tiles(dve, step)
            make_token(T - 1, (T - 1) % 2, (T - 1) // 2)

        @block.tensor
        def _(pe):
            pe.wait_ge(consts, 2)
            pe.wait_ge(once, 48)
            for t in range(T):
                r = t // 4
                ins = pe.matmul(acc[r // 2][r % 2][0:P, (t % 4) * P:(t % 4 + 1) * P],
                                sc[:, t, 0:1].broadcast_to([P, P]), ident[:, :], start=True, stop=True)
            ins.then_inc(row_ready, 1)
            pe.wait_ge(al_ready, 3)

            def half(t, u, j):
                if not (fixed(t) and t < 2):
                    pe.wait_ge(h_ready, 2 * t + j - 3)
                cols = slice(j * H, (j + 1) * H)
                for k in range(T):
                    pe.matmul(acc[u][j][0:P, :], ph[u][:, k, :], gh[0:P, k, cols], start=k == 0, stop=False)
                    pe.matmul(acc[u][j][0:P, :], ph[u][:, k, :], gl[0:P, k, cols], start=False, stop=False)
                    ins = pe.matmul(acc[u][j][0:P, :], pl[u][:, k, :], gh[0:P, k, cols], start=False, stop=k == T - 1)
                ins.then_inc(acc_ready, 1)

            def sum_of(t, u):
                pe.wait_ge(pl_ready, t + 1)
                pe.wait_ge(total_ready, t)
                for k in range(T):
                    pe.matmul(sums[0:P, :], ph[u][:, k, :], ones[:, :], start=k == 0, stop=False)
                    ins = pe.matmul(sums[0:P, :], pl[u][:, k, :], ones[:, :], start=False, stop=k == T - 1)
                ins.then_inc(sums_ready, 1)

            def turn(t, u):
                pe.wait_ge(token_ready, t + 1)
                pe.wait_ge(token_t_ready, t)
                for k in range(K):
                    ins = pe.transpose(turned[k // 4][:, k % 4, :], token[u][:, k * 128:(k + 1) * 128], ident[:, :])
                ins.then_inc(turned_ready, 1)

            def route(t):
                pe.wait_ge(token_t_ready, t + 1)
                pe.wait_ge(logit_read, t)
                for k in range(K):
                    ins = pe.matmul(logit_ps[0:P, :], token_t[:, k, :], router[:, k, :], start=k == 0, stop=k == K - 1)
                ins.then_inc(logit_ready, 1)

            def step(t, u, q):
                sum_of(t, u)
                half(t, u, 0)
                if not (fixed(t) and t < 3):
                    turn(t - 3, 1 - u)
                half(t, u, 1)
                if not (fixed(t) and t < 3):
                    route(t - 3)

            tiles(pe, step)
            for t in range(T - 3, T):
                turn(t, t % 2)
                route(t)


U32 = mybir.dt.uint32
EXPERTS, TOP, HID = 8, 2, 352
BLOCK = 128
BLOCKS = (TOP * N + EXPERTS * (BLOCK - 1) + EXPERTS) // BLOCK
SLOT_BLOCKS = BLOCKS + 2
HK = 3
HROWS = [128, 128, HID - 256]


AT_EXPERT = 0
AT_SIDE = AT_EXPERT + BLOCKS
AT_COUNT = AT_SIDE + BLOCKS + 1
AT_TOTAL = AT_COUNT + EXPERTS
AT_REST = AT_TOTAL + 1
PLAN = AT_REST + 1


class ExpertBuffers:

    def __init__(self, nc):
        place = Map(nc, 0, "expert")
        self.up_w = place("up_w", [128, 2, 2, K, 2 * HID], F32R)
        self.down_w = place("down_w", [128, 2, 2, HK, D], F32R)
        raw_at = place.at
        self.up_raw = place("up_raw", [128, K, 2 * HID])
        self.down_raw = place("down_raw", [128, HK, D])
        self.early = (place.at - raw_at) // (4 * D)
        self.base_rows = Map(nc, raw_at, "expert")("base_rows", [P, T, D])
        self.place = place
        place = Map(nc, 199040, "expert")
        self.slot = place("slot", [P, T, TOP], I32)
        self.weight = place("weight", [P, T, TOP])
        self.plan = place("plan", [1, PLAN], I32)
        self.late_at, self.late = place.at, place

    def load_raw(self, eng, gate_up_t, down_t, e, done):
        eng.dma_start(self.up_raw[:, :, :], gate_up_t[bass.ds(e, 1), :, :].rearrange("o p (k n) -> (o p) k n", n=2 * HID)).then_inc(done, 16)
        eng.dma_start(self.down_raw[:, 0:2, :], down_t[bass.ds(e, 1), 0:256, :].rearrange("o (k p) n -> (o p) k n", p=128)).then_inc(done, 16)
        eng.dma_start(self.down_raw[0:HROWS[2], 2, :], down_t[bass.ds(e, 1), 256:HID, :].rearrange("o p n -> (o p) n")).then_inc(done, 16)


GROUPS = [((0, 3), 0), ((3, 6), 1), ((6, 8), 2)]


def route_phase(nc, name, buffers, logits, table, gate_up_t, down_t):
    sem = lambda s: nc.alloc_semaphore(f"{name}_{s}")
    E = EXPERTS
    with ExitStack() as ctx:
        ps = lambda s, shape: ctx.enter_context(nc.psum_tensor(f"{name}_{s}", shape, F32))
        local = buffers.late
        weight, slot_i, plan_i = buffers.weight, buffers.slot, buffers.plan
        lg = local("lg", [P, T, E])
        top = local("top", [P, T, E])
        top_at = local("top_at", [P, T, E], U32)
        peak = local("peak", [P, T, 1])
        total = local("total", [P, T, 1])
        pick = local("pick", [P, T, TOP])
        wsum = local("wsum", [P, T, 1])
        expert_i = local("expert_i", [P, T, E], I32)
        expert = local("expert", [P, T, E])
        hot = [local(f"hot{j}", [P, T, E]) for j in range(TOP)]
        both = local("both", [P, T, E])
        node_i = local("node_i", [P, T], I32)
        square = local("square", [P, P], I32)
        below = local("below", [P, P])
        ones = local("ones", [P, P])
        place = local("place", [P, T, E])
        count = local("count", [P, T, E])
        start = local("start", [P, T + 1, E])
        steps_i = local("steps_i", [P, E, T - 1], I32)
        steps = local("steps", [P, E, T - 1])
        over = local("over", [P, E, T - 1])
        blocks = local("blocks", [P, E])
        first = local("first", [P, E + 1])
        offset = local("offset", [P, E])
        at = [local(f"at{j}", [P, T, E]) for j in range(TOP)]
        slot = local("slot", [P, T, TOP])
        block_i = local("block_i", [1, BLOCKS, E], I32)
        block_f = local("block_f", [1, BLOCKS, E])
        begun = local("begun", [1, BLOCKS, E])
        sign_i = local("sign_i", [1, E // 2, 2], I32)
        sign = local("sign", [1, E])
        signed = local("signed", [1, BLOCKS, E])
        plan = local("plan", [1, PLAN])
        zeros = local("zeros", [128, SLOT_BLOCKS], I32)
        assert BASE + local.at <= 229344, local.at
        place_ps = ps("place_ps", [128, T * E])
        count_ps = ps("count_ps", [128, T * E])

        loaded = sem("loaded")
        made = sem("made")
        step = sem("step")
        expd = sem("expd")
        peak_ready = sem("peak_ready")
        both_ready = sem("both_ready")
        placed = sem("placed")
        slots_ready = sem("slots_ready")
        plan_ready = sem("plan_ready")
        zeroed = sem("zeroed")
        scattered = sem("scattered")
        raw_loaded = sem("raw_loaded")
        down_cleared = sem("down_cleared")
        w_high = sem("w_high")

        block = ctx.enter_context(nc.Block())

        @block.sync
        def _(sp):
            sp.dma_start(lg[:, :, :], logits).then_inc(loaded, 16)
            sp.wait_ge(made, 1)
            sp.dma_start(table.rearrange("(p b) o -> p (b o)", p=128), zeros[:, :]).then_inc(zeroed, 16)
            buffers.load_raw(sp, gate_up_t, down_t, 0, raw_loaded)

        @block.gpsimd
        def _(pool):
            pool.memset(zeros[:, :], 0).then_inc(made, 1)
            pool.iota(expert_i[:, :, :], pattern=[[0, T], [1, E]], base=0, channel_multiplier=0).then_inc(made, 1)
            pool.iota(node_i[:, :], pattern=[[P, T]], base=0, channel_multiplier=1).then_inc(made, 1)
            pool.iota(square[:, :], pattern=[[1, P]], base=0, channel_multiplier=-1).then_inc(made, 1)
            pool.iota(steps_i[:, :, :], pattern=[[0, E], [BLOCK, T - 1]], base=BLOCK, channel_multiplier=0).then_inc(made, 1)
            pool.iota(block_i[:, :, :], pattern=[[1, BLOCKS], [0, E]], base=0, channel_multiplier=0).then_inc(made, 1)
            pool.iota(sign_i[:, :, :], pattern=[[0, E // 2], [2, 2]], base=-1, channel_multiplier=0).then_inc(made, 1)
            pool.memset(ones[:, :], 1.0).then_inc(made, 1)
            pool.wait_ge(zeroed, 16)
            pool.wait_ge(slots_ready, 1)
            pool.wait_ge(made, 8)
            for t in range(T):
                for j in range(TOP):
                    pool.indirect_dma_start(table, bass.IndirectOffsetOnAxis(slot_i[:, t, j:j + 1], 0),
                                            node_i[:, t:t + 1], None).then_inc(scattered, 16)
            pool.wait_ge(scattered, 16 * T * TOP)

        @block.scalar
        def _(act):
            act.wait_ge(peak_ready, 1)
            act.activation(lg[:, :, :], lg[:, :, :], ACT.Exp).then_inc(expd, 1)
            act.wait_ge(raw_loaded, 48)
            act.wait_ge(down_cleared, 1)
            for (k0, k1), d in GROUPS:
                act.activation(buffers.up_w[:, 0, 0, k0:k1, :], buffers.up_raw[:, k0:k1, :], ACT.Copy)
                act.activation(buffers.down_w[:, 0, 0, d, :], buffers.down_raw[:, d, :], ACT.Copy).then_inc(w_high, 1)

        @block.tensor
        def _(pe):
            pe.wait_ge(both_ready, 1)
            rhs = both[:, :, :].rearrange("p t e -> p (t e)")
            pe.matmul(place_ps[0:P, :], below[:, :], rhs, start=True, stop=True).then_inc(placed, 1)
            pe.matmul(count_ps[0:P, :], ones[:, :], rhs, start=True, stop=True).then_inc(placed, 1)

        @block.vector
        def _(dve):
            n = [0]

            def then(ins, wait=True):
                n[0] += 1
                ins.then_inc(step, 1)
                if wait:
                    dve.wait_ge(step, n[0])

            dve.memset(buffers.down_raw[96:128, 2, :], 0.0).then_inc(down_cleared, 1)
            dve.wait_ge(made, 8)
            dve.wait_ge(loaded, 16)
            tte = lambda ap: ap.broadcast_to([P, T, E])
            then(dve.tensor_reduce(peak[:, :, 0], lg[:, :, :], AX.X, ALU.max))
            dve.tensor_tensor(lg[:, :, :], lg[:, :, :], tte(peak[:, :, :]), ALU.subtract).then_inc(peak_ready, 1)
            dve.wait_ge(expd, 1)
            then(dve.tensor_reduce(total[:, :, 0], lg[:, :, :], AX.X, ALU.add))
            then(dve.reciprocal(total[:, :, :], total[:, :, :]))
            then(dve.tensor_tensor(lg[:, :, :], lg[:, :, :], tte(total[:, :, :]), ALU.mult))
            for t in range(T):
                then(dve.max(top[:, t, :], lg[:, t, :]), t == T - 1)
            for t in range(T):
                then(dve.max_index(top_at[:, t, :], top[:, t, :], lg[:, t, :]), t == T - 1)
            then(dve.tensor_tensor(wsum[:, :, :], top[:, :, 0:1], top[:, :, 1:2], ALU.add))
            then(dve.reciprocal(wsum[:, :, :], wsum[:, :, :]))
            then(dve.tensor_tensor(weight[:, :, :], top[:, :, 0:TOP], wsum[:, :, :].broadcast_to([P, T, TOP]), ALU.mult))
            then(dve.tensor_copy(pick[:, :, :], top_at[:, :, 0:TOP]))
            then(dve.tensor_copy(expert[:, :, :], expert_i[:, :, :]))
            for j in range(TOP):
                then(dve.tensor_tensor(hot[j][:, :, :], expert[:, :, :], tte(pick[:, :, j:j + 1]), ALU.is_equal))
            then(dve.tensor_scalar(below[:, :], square[:, :], 0.0, None, ALU.is_gt))
            dve.tensor_tensor(both[:, :, :], hot[0][:, :, :], hot[1][:, :, :], ALU.add).then_inc(both_ready, 1)
            then(dve.tensor_copy(steps[:, :, :], steps_i[:, :, :]), False)
            then(dve.memset(start[:, 0, :], 0.0))
            dve.wait_ge(placed, 2)
            then(dve.tensor_copy(place[:, :, :], place_ps[0:P, :].rearrange("p (t e) -> p t e", e=E)), False)
            then(dve.tensor_copy(count[:, :, :], count_ps[0:P, :].rearrange("p (t e) -> p t e", e=E)))
            for t in range(T):
                then(dve.tensor_tensor(start[:, t + 1, :], start[:, t, :], count[:, t, :], ALU.add))
            then(dve.tensor_tensor(place[:, :, :], place[:, :, :], start[:, 0:T, :], ALU.add), False)
            then(dve.tensor_tensor(over[:, :, :], start[:, T, :].unsqueeze(2).broadcast_to([P, E, T - 1]), steps[:, :, :], ALU.is_gt))
            then(dve.tensor_reduce(blocks[:, :], over[:, :, :], AX.X, ALU.add))
            then(dve.tensor_scalar(blocks[:, :], blocks[:, :], 1.0, None, ALU.add))
            then(dve.memset(first[:, 0:1], 0.0))
            for e in range(E):
                then(dve.tensor_tensor(first[:, e + 1:e + 2], first[:, e:e + 1], blocks[:, e:e + 1], ALU.add))
            then(dve.tensor_scalar(offset[:, :], first[:, 0:E], float(BLOCK), None, ALU.mult))
            then(dve.tensor_tensor(place[:, :, :], place[:, :, :], offset[:, :].unsqueeze(1).broadcast_to([P, T, E]), ALU.add))
            for j in range(TOP):
                then(dve.tensor_tensor(at[j][:, :, :], place[:, :, :], hot[j][:, :, :], ALU.mult), j == TOP - 1)
            for j in range(TOP):
                then(dve.tensor_reduce(slot[:, :, j], at[j][:, :, :], AX.X, ALU.add), j == TOP - 1)
            dve.tensor_copy(slot_i[:, :, :], slot[:, :, :]).then_inc(slots_ready, 1)
            then(dve.tensor_copy(block_f[:, :, :], block_i[:, :, :]))
            then(dve.tensor_tensor(begun[:, :, :], block_f[:, :, :], first[0:1, 0:E].unsqueeze(1).broadcast_to([1, BLOCKS, E]), ALU.is_ge))
            then(dve.memset(plan[:, :], 0.0))
            then(dve.tensor_reduce(plan[:, AT_EXPERT:AT_EXPERT + BLOCKS], begun[:, :, :], AX.X, ALU.add))
            then(dve.tensor_copy(sign[:, :], sign_i[:, :, :].rearrange("p a b -> p (a b)")))
            then(dve.memset(sign[:, 0:1], 0.0))
            then(dve.tensor_tensor(signed[:, :, :], begun[:, :, :], sign[:, :].unsqueeze(1).broadcast_to([1, BLOCKS, E]), ALU.mult))
            then(dve.tensor_reduce(plan[:, AT_SIDE + 1:AT_SIDE + 1 + BLOCKS], signed[:, :, :], AX.X, ALU.add))
            then(dve.tensor_copy(plan[:, AT_COUNT:AT_COUNT + E], blocks[0:1, :]))
            then(dve.tensor_copy(plan[:, AT_TOTAL:AT_TOTAL + 1], first[0:1, E:E + 1]))
            then(dve.tensor_scalar(plan[:, AT_REST:AT_REST + 1], first[0:1, E:E + 1], -1.0, float(SLOT_BLOCKS - 1), ALU.mult, ALU.add))
            dve.tensor_copy(plan_i[:, :], plan[:, :]).then_inc(plan_ready, 1)
            for g, ((k0, k1), d) in enumerate(GROUPS):
                dve.wait_ge(w_high, g + 1)
                dve.tensor_tensor(buffers.up_w[:, 0, 1, k0:k1, :], buffers.up_raw[:, k0:k1, :],
                                  buffers.up_w[:, 0, 0, k0:k1, :].bitcast(F32), ALU.subtract)
                dve.tensor_tensor(buffers.down_w[:, 0, 1, d, :], buffers.down_raw[:, d, :],
                                  buffers.down_w[:, 0, 0, d, :].bitcast(F32), ALU.subtract)


def expert_phase(nc, name, buffers, tokens, table, gate_up_t, down_t, base, results, base_loaded):
    sem = lambda s: nc.alloc_semaphore(f"{name}_{s}")
    E, KU, W2 = EXPERTS, K, 2 * HID
    with ExitStack() as ctx:
        ps = lambda s, shape: ctx.enter_context(nc.psum_tensor(f"{name}_{s}", shape, F32))
        local = buffers.place
        up_w, down_w, up_raw, down_raw, plan = buffers.up_w, buffers.down_w, buffers.up_raw, buffers.down_raw, buffers.plan
        xt = local("xt", [128, 2, K, BLOCK], F32R)
        gate = local("gate", [BLOCK, HID])
        hidden = local("hidden", [BLOCK, HK * 128])
        ht = local("ht", [128, 2, HK, BLOCK], F32R)
        y = local("y", [BLOCK, D])
        index = local("index", [128, SLOT_BLOCKS], I32)
        index_now = local("index_now", [128, 1], I32)
        waits = local("waits", [128, 2])
        zeros = local("zeros", [128, 256])
        ident = local("ident", [128, 128])
        square = local("square", [128, 128], I32)
        assert local.at <= 199040, local.at
        x = Map(nc, buffers.late_at, name)("x", [BLOCK, 2, D])
        gate_ps = ps("gate_ps", [128, HID])
        up_ps = ps("up_ps", [128, HID])
        y_ps = [ps(f"y_ps{j}", [128, H]) for j in range(2)]
        turned = [ps(f"turned{r}", [128, 4, BLOCK]) for r in range(2)]
        ht_ps = ps("ht_ps", [128, HK, BLOCK])

        once = sem("once")
        made = sem("made")
        ident_ready = sem("ident_ready")
        ht_cleared = sem("ht_cleared")
        raw_loaded = sem("raw_loaded")
        w_high = sem("w_high")
        w_ready = sem("w_ready")
        index_ready = sem("index_ready")
        gathered = sem("gathered")
        x_turned = sem("x_turned")
        xt_high = sem("xt_high")
        xt_ready = sem("xt_ready")
        gate_done = sem("gate_done")
        up_done = sem("up_done")
        once_dve = sem("once_dve")
        gate_ready = sem("gate_ready")
        hidden_ready = sem("hidden_ready")
        h_turned = sem("h_turned")
        ht_high = sem("ht_high")
        ht_ready = sem("ht_ready")
        down_ready = sem("down_ready")
        y_ready = sem("y_ready")
        y_stored = sem("y_stored")
        cleared = sem("cleared")

        block = ctx.enter_context(nc.Block())

        @block.sync
        def _(sp):
            with nc.allow_non_contiguous_dma(reason="slots of a block over the partitions; a small table"):
                sp.dma_start(index[:, :], table.rearrange("(b p) o -> p (b o)", p=128)).then_inc(once, 16)
            sp.wait_ge(gathered, 16)
            with sp.Fori(0, E - 1) as before:
                sp.wait_ge(w_ready, 3 * before + 3)
                buffers.load_raw(sp, gate_up_t, down_t, before + 1, raw_loaded)
            sp.wait_ge(once_dve, 2)
            total = sp.value_load(plan[0:1, AT_TOTAL:AT_TOTAL + 1], min_val=E, max_val=BLOCKS)
            with sp.Fori(total + 1, SLOT_BLOCKS) as i:
                sp.dma_start(results[bass.ds(i * BLOCK, BLOCK), :].rearrange("p (r n) -> p r n", n=256),
                             zeros[:, :].unsqueeze(1).broadcast_to([128, D // 256, 256])).then_inc(cleared, 16)
            sp.wait_ge(w_ready, 3 * E)
            sp.dma_start(buffers.base_rows[:, 0:buffers.early, :],
                         base[0:buffers.early * P, :].rearrange("(t p) n -> p t n", p=P)).then_inc(base_loaded, 16)

        @block.gpsimd
        def _(pool):
            pool.iota(square[:, :], pattern=[[1, 128]], base=0, channel_multiplier=-1).then_inc(made, 1)
            pool.memset(waits[:, 1:2], 0.0).then_inc(made, 1)
            pool.wait_ge(made, 2)
            pool.wait_ge(once, 16)
            total = pool.value_load(plan[0:1, AT_TOTAL:AT_TOTAL + 1], min_val=E, max_val=BLOCKS)
            with pool.Fori(0, (total + 2) // 2) as pair:
                for side in range(2):
                    i = pair * 2 + side
                    pool.wait_ge(x_turned, i)
                    pool.tensor_copy(index_now[:, :], index[:, bass.ds(i, 1)]).then_inc(index_ready, 1)
                    pool.wait_ge(index_ready, i + 1)
                    pool.tensor_tensor(waits[:, 0:1], waits[:, 1:2], waits[:, 1:2], ALU.add)
                    pool.indirect_dma_start(x[:, side, :], None, tokens, bass.IndirectOffsetOnAxis(index_now[:, :], 0)).then_inc(gathered, 16)
                    pool.wait_ge(gathered, 16 * i + 16)
            rest = pool.value_load(plan[0:1, AT_REST:AT_REST + 1], min_val=1, max_val=SLOT_BLOCKS)
            pool.wait_ge(cleared, rest * 16)
            pool.wait_ge(y_stored, 16 * total + 16)

        @block.scalar
        def _(act):
            def split(e, side, g):
                (k0, k1), d = GROUPS[g]
                act.wait_ge(raw_loaded, 48 * e)
                act.activation(up_w[:, side, 0, k0:k1, :], up_raw[:, k0:k1, :], ACT.Copy)
                act.activation(down_w[:, side, 0, d, :], down_raw[:, d, :], ACT.Copy).then_inc(w_high, 1)

            def xt_part(i):
                act.wait_ge(x_turned, i + 2)
                for r in range(2):
                    ins = act.activation(xt[:, 0, 4 * r:4 * r + 4, :], turned[r][:, :, :], ACT.Copy)
                ins.then_inc(xt_high, 1)

            def result(i):
                act.wait_ge(down_ready, i + 1)
                act.wait_ge(y_stored, 16 * i)
                for j in range(2):
                    ins = act.activation(y[:, j * H:(j + 1) * H], y_ps[j][:, :], ACT.Copy)
                ins.then_inc(y_ready, 1)
                act.wait_ge(y_ready, i + 1)
                act.dma_start(results[bass.ds(i * BLOCK, BLOCK), :], y[:, :]).then_inc(y_stored, 16)

            def one_block(i):
                act.wait_ge(gate_done, i + 1)
                act.wait_ge(hidden_ready, i)
                act.activation(gate[:, :], gate_ps[:, :], ACT.Silu).then_inc(gate_ready, 1)
                act.wait_ge(up_done, i + 1)
                xt_part(i + 1)
                result(i)
                act.wait_ge(h_turned, i + 1)
                act.activation(ht[:, 0, :, :], ht_ps[:, :, :], ACT.Copy).then_inc(ht_high, 1)

            def expert(e, side, last):
                mine = act.value_load(plan[0:1, bass.ds(AT_COUNT + e, 1)], min_val=1, max_val=T)
                with act.Fori(0, mine) as b:
                    one_block(act.snap(count))
                    act.reg_add(count, count, 1)
                    if not last:
                        with act.If(b == 0):
                            split(e + 1, 1 - side, 0)
                            split(e + 1, 1 - side, 1)
                        with act.If(b == 1):
                            split(e + 1, 1 - side, 2)
                if not last:
                    with act.If(mine <= 1):
                        split(e + 1, 1 - side, 2)

            xt_part(0)
            count = act.alloc_register(f"{name}_act_blocks")
            act.reg_mov(count, 0)
            with act.Fori(0, E // 2 - 1) as pair:
                for side in range(2):
                    expert(pair * 2 + side, side, False)
            expert(E - 2, 0, False)
            expert(E - 1, 1, True)
            total = act.snap(count)
            result(total)

        @block.vector
        def _(dve):
            def split(e, side, g):
                (k0, k1), d = GROUPS[g]
                dve.wait_ge(w_high, 3 * e + (g - 2))
                dve.tensor_tensor(up_w[:, side, 1, k0:k1, :], up_raw[:, k0:k1, :], up_w[:, side, 0, k0:k1, :].bitcast(F32), ALU.subtract)
                dve.tensor_tensor(down_w[:, side, 1, d, :], down_raw[:, d, :], down_w[:, side, 0, d, :].bitcast(F32), ALU.subtract).then_inc(w_ready, 1)

            def xt_part(i):
                dve.wait_ge(xt_high, i + 1)
                for r in range(2):
                    ins = dve.tensor_tensor(xt[:, 1, 4 * r:4 * r + 4, :], turned[r][:, :, :],
                                            xt[:, 0, 4 * r:4 * r + 4, :].bitcast(F32), ALU.subtract)
                ins.then_inc(xt_ready, 1)

            def one_block(i):
                dve.wait_ge(gate_ready, i + 1)
                dve.wait_ge(up_done, i + 1)
                dve.wait_ge(h_turned, i)
                dve.tensor_tensor(hidden[:, 0:HID], up_ps[:, :], gate[:, :], ALU.mult).then_inc(hidden_ready, 1)
                xt_part(i + 1)
                dve.wait_ge(ht_high, i + 1)
                dve.tensor_tensor(ht[:, 1, :, :], ht_ps[:, :, :], ht[:, 0, :, :].bitcast(F32), ALU.subtract).then_inc(ht_ready, 1)

            def expert(e, side, last):
                mine = dve.value_load(plan[0:1, bass.ds(AT_COUNT + e, 1)], min_val=1, max_val=T)
                with dve.Fori(0, mine) as b:
                    one_block(dve.snap(count))
                    dve.reg_add(count, count, 1)
                    if not last:
                        with dve.If(b == 0):
                            split(e + 1, 1 - side, 0)
                            split(e + 1, 1 - side, 1)
                        with dve.If(b == 1):
                            split(e + 1, 1 - side, 2)
                if not last:
                    with dve.If(mine <= 1):
                        split(e + 1, 1 - side, 2)

            dve.sem_inc(w_ready, 3)
            dve.memset(hidden[:, HID:HK * 128], 0.0).then_inc(once_dve, 1)
            dve.memset(zeros[:, :], 0.0).then_inc(once_dve, 1)
            dve.memset(ht[:, :, :, :].bitcast(F32), 0.0).then_inc(ht_ready, 1)
            dve.wait_ge(made, 1)
            dve.tensor_scalar(ident[:, :], square[:, :], 0.0, None, ALU.is_equal).then_inc(ident_ready, 1)
            xt_part(0)
            count = dve.alloc_register(f"{name}_dve_blocks")
            dve.reg_mov(count, 0)
            with dve.Fori(0, E // 2 - 1) as pair:
                for side in range(2):
                    expert(pair * 2 + side, side, False)
            expert(E - 2, 0, False)
            expert(E - 1, 1, True)

        @block.tensor
        def _(pe):
            def turn_x(i):
                pe.wait_ge(gathered, 16 * i + 16)

                def turn(side):
                    for k in range(K):
                        ins = pe.transpose(turned[k // 4][:, k % 4, :], x[:, side, k * 128:(k + 1) * 128], ident[:, :])
                    ins.then_inc(x_turned, 1)

                if isinstance(i, int):
                    turn(i & 1)
                else:
                    for side in range(2):
                        with pe.If((i & 1) == side):
                            turn(side)

            def up(i):
                begun = pe.value_load(plan[0:1, bass.ds(AT_EXPERT + i, 1)], min_val=1, max_val=E)
                side = pe.value_load(plan[0:1, bass.ds(AT_SIDE + 1 + i, 1)], min_val=0, max_val=1)
                pe.wait_ge(w_ready, begun * 3)
                pe.wait_ge(xt_ready, i + 1)
                pe.wait_ge(hidden_ready, i)
                for out, c0, done in ((gate_ps, 0, gate_done), (up_ps, HID, up_done)):
                    for k in range(K):
                        high, low = (up_w[:, bass.ds(side, 1), part, k, c0:c0 + HID].rearrange("p o n -> p (o n)") for part in range(2))
                        pe.matmul(out[:, :], xt[:, 0, k, :], high, start=k == 0, stop=False)
                        pe.matmul(out[:, :], xt[:, 0, k, :], low, start=False, stop=False)
                        ins = pe.matmul(out[:, :], xt[:, 1, k, :], high, start=False, stop=k == K - 1)
                    ins.then_inc(done, 1)

            def down(i):
                side = pe.value_load(plan[0:1, bass.ds(AT_SIDE + i, 1)], min_val=0, max_val=1)
                pe.wait_ge(ht_ready, i + 1)
                pe.wait_ge(y_ready, i)
                for j in range(2):
                    for k in range(HK):
                        high, low = (down_w[:, bass.ds(side, 1), part, k, j * H:(j + 1) * H].rearrange("p o n -> p (o n)") for part in range(2))
                        pe.matmul(y_ps[j][:, :], ht[:, 0, k, :], high, start=k == 0, stop=False)
                        pe.matmul(y_ps[j][:, :], ht[:, 0, k, :], low, start=False, stop=False)
                        ins = pe.matmul(y_ps[j][:, :], ht[:, 1, k, :], high, start=False, stop=k == HK - 1)
                ins.then_inc(down_ready, 1)

            def turn_h(i):
                pe.wait_ge(hidden_ready, i + 1)
                for k in range(HK):
                    ins = pe.transpose(ht_ps[:, k, :], hidden[:, k * 128:(k + 1) * 128], ident[:, :])
                ins.then_inc(h_turned, 1)

            pe.wait_ge(once_dve, 1)
            pe.wait_ge(ident_ready, 1)
            pe.sem_inc(x_turned, 1)
            turn_x(0)
            total = pe.value_load(plan[0:1, AT_TOTAL:AT_TOTAL + 1], min_val=E, max_val=BLOCKS)
            with pe.Fori(0, total) as i:
                up(i)
                turn_x(i + 1)
                down(i)
                turn_h(i)
            down(total)


def combine_phase(nc, name, buffers, base, results, alpha, out, base_loaded):
    sem = lambda s: nc.alloc_semaphore(f"{name}_{s}")
    early = buffers.early
    with ExitStack() as ctx:
        local = Map(nc, 0, name)
        row = [[local(f"row{t}_{j}", [P, D]) for j in range(TOP)] for t in range(T)]
        scale = local("scale", [P, 1])
        scaled = local("scaled", [P, T, TOP])
        x = buffers.base_rows
        once = sem("once")
        scaled_ready = sem("scaled_ready")
        rest_loaded = sem("rest_loaded")
        gathered = [[sem(f"gathered{t}_{j}") for j in range(TOP)] for t in range(T)]
        added = sem("added")
        stored = sem("stored")
        block = ctx.enter_context(nc.Block())

        @block.sync
        def _(sp):
            sp.dma_start(scale[:, :], alpha.broadcast_to([P, 1])).then_inc(once, 16)
            sp.dma_start(x[:, early:T, :], base[early * P:N, :].rearrange("(t p) n -> p t n", p=P)).then_inc(rest_loaded, 16)

        @block.scalar
        def _(act):
            for t in range(T):
                act.wait_ge(added, TOP * (t + 1))
                act.dma_start(out[t * P:(t + 1) * P, :], x[:, t, :]).then_inc(stored, 16)
            act.wait_ge(stored, 16 * T)

        @block.gpsimd
        def _(pool):
            for t in range(T):
                for j in range(TOP):
                    pool.indirect_dma_start(row[t][j][:, :], None, results,
                                            bass.IndirectOffsetOnAxis(buffers.slot[:, t, j:j + 1], 0),
                                            element_offset=BLOCK * D).then_inc(gathered[t][j], 16)

        @block.vector
        def _(dve):
            dve.wait_ge(once, 16)
            dve.tensor_scalar(scale[:, :], scale[:, :], -0.5, 2.0, ALU.max, ALU.min).then_inc(scaled_ready, 1)
            dve.wait_ge(scaled_ready, 1)
            dve.tensor_scalar(scaled[:, :, :], buffers.weight[:, :, :], scale[:, 0:1], None, ALU.mult).then_inc(scaled_ready, 1)
            dve.wait_ge(scaled_ready, 2)
            dve.wait_ge(base_loaded, 16)
            for t in range(T):
                if t == early:
                    dve.wait_ge(rest_loaded, 16)
                for j in range(TOP):
                    dve.wait_ge(gathered[t][j], 16)
                    if j:
                        dve.wait_ge(added, TOP * t + j)
                    dve.scalar_tensor_tensor(x[:, t, :], row[t][j][:, :], scaled[:, t, j:j + 1], x[:, t, :],
                                             ALU.mult, ALU.add).then_inc(added, 1)


def gnn_ffn_gnn_moe_kernel(nc, x, edges_src_cols, edges_dst_cols, edges_dst_chunks, w_self0, w_neigh0, bias0,
                           w_self1, w_neigh1, bias1, train1, train2, ffn_bias, att_w, att_a, norm_w, router_t,
                           gate_up_t, down_t, alpha, out):
    dram = lambda name, shape, dt=F32: nc.dram_tensor(name, shape, dt, kind="Internal").ap()
    counts_by_src = dram("counts_by_src", [T, P, T, P])
    counts_by_dst = dram("counts_by_dst", [T, P, T, P])
    deg_inv = dram("deg_inv", [P, T])
    w_ffn = dram("w_ffn", [D, D])
    xt0 = dram("xt0", [T, 128, 2, K, P])
    xt1 = dram("xt1", [T, 128, 2, K, P])
    h0 = dram("h0", [N, D])
    x1 = dram("x1", [N, D])
    x2 = dram("x2", [N, D])
    base = dram("base", [N, D])
    tokens = dram("tokens", [N, D])
    scores = dram("scores", [P, T, 2])
    logits = dram("logits", [P, T, EXPERTS])
    table = dram("table", [SLOT_BLOCKS * BLOCK, 1], I32)
    results = dram("results", [SLOT_BLOCKS * BLOCK, D])

    place = lambda name, shape, dt, at: nc.alloc_sbuf_tensor_at(name, shape, dt, offset=BASE + at)
    raw = place("raw", [128, K, D], F32, RAW_AT)
    wh = place("wh", [128, K, D], F32R, WH_AT)
    wl = place("wl", [128, K, D], F32R, WL_AT)
    gh = place("gh", [128, T, D], F32R, GH_AT)
    gl = place("gl", [128, T, D], F32R, GL_AT)

    raw_loaded = nc.alloc_semaphore("raw_loaded")
    base_loaded = nc.alloc_semaphore("base_loaded")

    def clear_semaphores(before):
        nc.clear_and_free_semaphores(nc.allocated_since(before))
        nc.all_engine_barrier()

    before = nc.snapshot_sems()
    graph = GraphBuffers(nc)
    prepare_phase(nc, "prepare", graph, edges_dst_chunks, edges_src_cols, edges_dst_cols, w_neigh0, raw, wh, wl)
    count_project_phase(nc, "neigh0", graph, x, xt0, wh, wl, gh, gl, counts_by_src, counts_by_dst, deg_inv)
    aggregate_phase(nc, "self0", xt0, counts_by_src, deg_inv, bias0, None, h0,
                    raw, wh, wl, gh, gl, raw_loaded, 1, w_neigh1, own_w=w_self0, unfold=(train1, train2, w_ffn))
    project_phase(nc, "neigh1", h0, xt1, raw, wh, wl, gh, gl, raw_loaded, 2, w_self1,
                  normalize=False, relu=True, result="split")
    aggregate_phase(nc, "self1", xt1, counts_by_src, deg_inv, bias1, x, x1,
                    raw, wh, wl, gh, gl, raw_loaded, 3, w_ffn)
    clear_semaphores(before)
    before = nc.snapshot_sems()
    project_phase(nc, "ffn", x1, None, raw, wh, wl, None, None, raw_loaded, 4, att_w,
                  normalize=True, relu=False, result="residual", bias=ffn_bias, out=x2)
    project_phase(nc, "att_h", x2, None, raw, wh, wl, gh, gl, raw_loaded, 5, None,
                  normalize=True, relu=False, result="scores", score_w=att_a, scores=scores)
    attention_phase(nc, "att", x2, counts_by_dst, scores, norm_w, router_t, gh, gl, base, tokens, logits)
    experts = ExpertBuffers(nc)
    route_phase(nc, "route", experts, logits, table, gate_up_t, down_t)
    clear_semaphores(before)
    expert_phase(nc, "experts", experts, tokens, table, gate_up_t, down_t, base, results, base_loaded)
    combine_phase(nc, "combine", experts, base, results, alpha, out, base_loaded)


_NAMES = ["x", "edges_src_cols", "edges_dst_cols", "edges_dst_chunks", "w_self0", "w_neigh0", "bias0",
          "w_self1", "w_neigh1", "bias1", "train1", "train2", "ffn_bias", "att_w", "att_a", "norm_w", "router_t",
          "gate_up_t", "down_t", "alpha"]


def _layout(inputs):
    a = {k: np.asarray(v) for k, v in inputs.items()}
    pad = np.full(CHUNKS * CHUNK - a["src"].shape[0], NONE, a["src"].dtype)
    src = np.concatenate([a["src"], pad])
    dst = np.concatenate([a["dst"], pad])
    cols = lambda e: e.reshape(TILES * CHUNKS, EDGE_TILE).T
    train1 = lambda g: np.repeat(g[0].transpose(2, 1, 0).reshape(32, 128), 16, axis=0)
    train2 = lambda g: np.tile(g[:, :, 0, :].transpose(2, 0, 1).reshape(16, 64), (8, 1))
    row = lambda v: v.reshape(1, -1)
    return dict(
        x=a["x"], edges_src_cols=cols(src), edges_dst_cols=cols(dst), edges_dst_chunks=dst.reshape(CHUNKS, CHUNK),
        w_self0=a["L0_gnn_W_self0"], w_neigh0=a["L0_gnn_W_neigh0"], bias0=row(a["L0_gnn_b0"]),
        w_self1=a["L0_gnn_W_self1"], w_neigh1=a["L0_gnn_W_neigh1"], bias1=row(a["L0_gnn_b1"]),
        train1=np.stack([train1(a["L0_ffn_G1_R"]), train1(a["L0_ffn_G1_I"])]),
        train2=np.stack([train2(a["L0_ffn_G2_R"]), train2(a["L0_ffn_G2_I"])]),
        ffn_bias=row(np.concatenate([a["L0_ffn_bias_real"], a["L0_ffn_bias_imag"]])),
        att_w=a["L1_gnn_W"], att_a=row(a["L1_gnn_a"]), norm_w=row(a["L1_ffn_norm_weight"]),
        router_t=a["L1_ffn_router_weight"].reshape(EXPERTS, K, 128).transpose(2, 1, 0).reshape(128, K * EXPERTS),
        gate_up_t=a["L1_ffn_gate_up_weight"].reshape(EXPERTS, 2 * HID, K, 128).transpose(0, 3, 2, 1).reshape(EXPERTS, 128, K * 2 * HID),
        down_t=a["L1_ffn_down_weight"].transpose(0, 2, 1),
        alpha=a["L1_ffn_residual_alpha"].reshape(1, 1))


def kernel(**inputs):
    import concourse.bacc as _bacc
    from concourse import mybir as _mybir
    from concourse.bass_utils import run_bass_kernel_spmd as _run

    nc = _bacc.Bacc("TRN2", target_bir_lowering=False, num_devices=1)
    data = _layout(inputs)
    arrays, args = {}, []
    for name in _NAMES:
        a = np.ascontiguousarray(data[name])
        arrays[f"in_{name}"] = a
        args.append(nc.dram_tensor(f"in_{name}", a.shape, _mybir.dt.from_np(a.dtype), kind="ExternalInput").ap())
    args.append(nc.dram_tensor("out_rows", (N, D), _mybir.dt.float32, kind="ExternalOutput").ap())
    gnn_ffn_gnn_moe_kernel(nc, *args)
    r = _run(nc, [arrays], core_ids=[0])
    return r.results[0]["out_rows"]
```

```python
import numpy as np
import concourse.bass as bass
from concourse import mybir
from contextlib import ExitStack

F32 = mybir.dt.float32
F32R = mybir.dt.float32r
ALU = mybir.AluOpType
ACT = mybir.ActivationFunctionType
AX = mybir.AxisListType
N, P, D = 1250, 125, 1024
T, K, H = N // P, D // 128, D // 2

BASE = 16512
W_BYTES = K * D * 4
G_BYTES = T * D * 4
RAW_AT = 0
WH_AT = RAW_AT + W_BYTES
WL_AT = WH_AT + W_BYTES
GH_AT = WL_AT + W_BYTES
GL_AT = GH_AT + G_BYTES
LOCAL_AT = GL_AT + G_BYTES
SBUF_END = 229344
HANDED_AT = SBUF_END - BASE - 5024


class Map:

    def __init__(self, nc, at, name):
        self.nc, self.at, self.name = nc, at, name

    def __call__(self, name, shape, dt=F32):
        size = 2 if dt == mybir.dt.float16 else 4
        for s in shape[1:]:
            size *= s
        t = self.nc.alloc_sbuf_tensor_at(f"{self.name}_{name}", shape, dt, offset=BASE + self.at)
        self.at += -(-size // 32) * 32
        return t


def node_rows(x, t):
    return x[bass.ds(t * P, P), :]


def load_counts(eng, counts, counts_by_src, done, t):
    eng.dma_start(counts[:, :, :].bitcast(F32),
                  counts_by_src[bass.ds(t, 1), :, :, :].rearrange("o s k d -> (o s) k d")).then_inc(done, 16)


def project_phase(nc, name, rows, xt_out, raw, wh, wl, gh, gl, raw_loaded, loads, next_w,
                  normalize, relu, result, bias=None, out=None, score_w=None, scores=None, counts_ahead=None):
    sem = lambda s: nc.alloc_semaphore(f"{name}_{s}")
    with ExitStack() as ctx:
        ps = lambda s, shape: ctx.enter_context(nc.psum_tensor(f"{name}_{s}", shape, F32))
        local = Map(nc, LOCAL_AT, name)
        xt = [local(f"xt{u}", [128, 2, K, P], F32R) for u in range(2)]
        if result == "residual":
            local = Map(nc, GH_AT, name)
            bias_row = local("bias_row", [P, D])
            biased = [local(f"biased{u}", [P, D]) for u in range(2)]
            xn = local("xn", [P, D])
            y = [local(f"y{u}", [P, D]) for u in range(2)]
        x = [local(f"x{u}", [P, D]) for u in range(2)]
        if result != "residual":
            xn = None
        ident = local("ident", [P, P])
        square = local("square", [P, P], mybir.dt.int32)
        power = local("power", [P, 1])
        eps = local("eps", [P, 1])
        waits = local("waits", [P, 1])
        stats = [local(f"stats{u}", [P, 12]) for u in range(2)]
        moments = [local(f"moments{u}", [P, 2]) for u in range(2)]
        rstd = [local(f"rstd{u}", [P, 1]) for u in range(2)]
        if result == "scores":
            score_parts = local("score_parts", [P, 2, 2, 2])
        acc = [[ps(f"acc{u}{j}", [128, 512]) for j in range(2)] for u in range(2)]
        turned = [ps(f"turned{r}", [128, 4, P]) for r in range(2)]

        x_loaded = [sem(f"x_loaded{u}") for u in range(2)]
        xt_high = sem("xt_high")
        xt_low = sem("xt_low")
        if xt_out is not None:
            xt_stored = [sem(f"xt_stored{u}") for u in range(2)]
        if normalize:
            stats_ready = sem("stats_ready")
            moments_ready = sem("moments_ready")
            rstd_ready = sem("rstd_ready")
            var_eps = sem("var_eps")
            xn_ready = sem("xn_ready")
        turned_ready = sem("turned_ready")
        acc_ready = sem("acc_ready")
        if result != "residual":
            acc_high = sem("acc_high")
            acc_free = sem("acc_free")
        w_high = sem("w_high")
        w_low = sem("w_low")
        made = sem("made")
        ident_ready = sem("ident_ready")
        if result != "split":
            extra = sem("extra")
        if result == "scores":
            scored = sem("scored")
            score_ready = sem("score_ready")
        if result == "residual":
            biased_ready = sem("biased_ready")
            y_ready = sem("y_ready")
            y_stored = [sem(f"y_stored{u}") for u in range(2)]

        def xn_of(u):
            return x[u] if xn is None else xn

        block = ctx.enter_context(nc.Block())

        @block.sync
        def _(sp):
            if bias is not None:
                sp.dma_start(bias_row[:, :], bias.broadcast_to([P, D])).then_inc(extra, 16)

            def load(t, u, pair):
                if pair is not None:
                    sp.wait_ge(turned_ready, t - 1)
                    if result == "residual":
                        sp.wait_ge(biased_ready, t - 1)
                sp.dma_start(x[u][:, :], node_rows(rows, t)).then_inc(x_loaded[u], 16)

            def store(t, u):
                if xt_out is not None:
                    sp.wait_ge(xt_low, t + 1)
                    sp.dma_start(xt_out[bass.ds(t, 1), :, :, :, :].rearrange("o p a k n -> (o p) a k n"),
                                 xt[u][:, :, :, :].bitcast(F32)).then_inc(xt_stored[u], 16)
                if result == "residual":
                    sp.wait_ge(y_ready, 2 * t + 2)
                    sp.dma_start(node_rows(out, t), y[u][:, :]).then_inc(y_stored[u], 16)

            load(0, 0, None)
            load(1, 1, None)
            if counts_ahead is not None:
                load_counts(sp, *counts_ahead, 0)
            with sp.Fori(0, T // 2 - 1) as pair:
                for u in range(2):
                    load(pair * 2 + (u + 2), u, pair)
                    store(pair * 2 + u, u)
            for t in (T - 2, T - 1):
                store(t, t % 2)
            if xt_out is not None:
                for u in range(2):
                    sp.wait_ge(xt_stored[u], 16 * (T // 2))
            if result == "residual":
                for u in range(2):
                    sp.wait_ge(y_stored[u], 16 * (T // 2))

        @block.gpsimd
        def _(pool):
            pool.iota(square[:, :], pattern=[[1, P]], base=0, channel_multiplier=-1).then_inc(made, 1)
            pool.memset(power[:, :], -0.5).then_inc(made, 1)
            pool.memset(eps[:, :], 1e-5).then_inc(made, 1)
            pool.wait_ge(made, 3)
            def tile(t, u, pair):
                if normalize:
                    pool.wait_ge(moments_ready, t + 1)
                    pool.tensor_tensor(rstd[u][:, :], moments[u][:, 1:2], eps[:, :], ALU.add).then_inc(var_eps, 1)
                    pool.wait_ge(var_eps, t + 1)
                    pool.tensor_tensor(rstd[u][:, :], rstd[u][:, :], power[:, :], ALU.pow).then_inc(rstd_ready, 1)
                if result == "residual":
                    pool.wait_ge(x_loaded[u], pair * 16 + 16)
                    if not (isinstance(pair, int) and pair == 0):
                        pool.wait_ge(y_ready, 2 * t - 2)
                    pool.tensor_tensor(biased[u][:, :], x[u][:, :], bias_row[:, :], ALU.add).then_inc(biased_ready, 1)

            if result == "residual":
                pool.wait_ge(extra, 16)
            if normalize or result == "residual":
                tile(0, 0, 0)
                tile(1, 1, 0)
                with pool.Fori(1, T // 2) as pair:
                    for u in range(2):
                        tile(pair * 2 + u, u, pair)

        @block.scalar
        def _(act):
            def turn(t, u, pair):
                act.wait_ge(turned_ready, t + 1)
                if not (isinstance(pair, int) and pair == 0):
                    act.wait_ge(acc_ready, 2 * t - 2)
                    if xt_out is not None:
                        act.wait_ge(xt_stored[u], 16 * pair)
                for r in range(2):
                    act.activation(xt[u][:, 0, 4 * r:4 * r + 4, :], turned[r][:, :, :],
                                         ACT.Relu if relu else ACT.Copy).then_inc(xt_high, 1)

            def result_of(t, u):
                for j in range(2):
                    if result == "residual":
                        continue
                    act.wait_ge(acc_ready, 2 * t + j + 1)
                    act.activation(gh[0:P, bass.ds(t, 1), j * H:(j + 1) * H].rearrange("p o n -> p (o n)"),
                                   acc[u][j][0:P, :], ACT.Copy).then_inc(acc_high, 1)

            act.wait_ge(raw_loaded, 16 * loads)
            for k in range(K):
                if k == K // 2:
                    turn(0, 0, 0)
                act.activation(wh[:, k, :], raw[:, k, :], ACT.Copy).then_inc(w_high, 1)
            turn(1, 1, 0)
            if next_w is not None:
                act.wait_ge(w_low, K)
                act.dma_start(raw[:, :, :], next_w.rearrange("(k p) n -> p k n", p=128)).then_inc(raw_loaded, 16)
            if result == "scores":
                act.wait_ge(w_low, K)
                act.dma_start(raw[0:P, 0:2, :].rearrange("p c n -> p (c n)"), score_w.broadcast_to([P, 2 * D])).then_inc(extra, 16)
            result_of(0, 0)
            with act.Fori(0, T // 2 - 1) as pair:
                for u in range(2):
                    turn(pair * 2 + (u + 2), u, pair + 1)
                    result_of(pair * 2 + (u + 1), 1 - u)
            result_of(T - 1, 1)

        @block.vector
        def _(dve):
            dve.wait_ge(made, 3)
            dve.tensor_scalar(ident[:, :], square[:, :], 0.0, None, ALU.is_equal).then_inc(ident_ready, 1)

            def norm(t, u, pair):
                stats_of(t, u, pair)
                apply(t, u)

            def stats_of(t, u, pair):
                dve.wait_ge(x_loaded[u], 16 * (pair + 1))
                if not normalize:
                    return
                for j in range(2):
                    dve.bn_stats(stats[u][:, 6 * j:6 * j + 6], x[u][:, j * H:(j + 1) * H]).then_inc(stats_ready, 1)
                dve.wait_ge(stats_ready, 2 * t + 2)
                dve.memset(waits[:, :], 0.0)
                dve.bn_aggr(moments[u][:, :], stats[u][:, :]).then_inc(moments_ready, 1)

            def apply(t, u):
                if not normalize:
                    return
                dve.wait_ge(rstd_ready, t + 1)
                if xn is not None:
                    dve.wait_ge(turned_ready, t)
                dve.tensor_scalar(xn_of(u)[:, :], x[u][:, :], moments[u][:, 0:1], rstd[u][:, 0:1],
                                  ALU.subtract, ALU.mult).then_inc(xn_ready, 1)

            def turn(t, u):
                for r in range(2):
                    dve.wait_ge(xt_high, 2 * t + r + 1)
                    low, high = xt[u][:, 1, 4 * r:4 * r + 4, :], xt[u][:, 0, 4 * r:4 * r + 4, :].bitcast(F32)
                    if relu:
                        ins = dve.scalar_tensor_tensor(low, turned[r][:, :, :], 0.0, high, ALU.max, ALU.subtract)
                    else:
                        ins = dve.tensor_tensor(low, turned[r][:, :, :], high, ALU.subtract)
                ins.then_inc(xt_low, 1)

            def result_of(t, u, pair):
                for j in range(2):
                    cols = slice(j * H, (j + 1) * H)
                    if result == "residual":
                        dve.wait_ge(acc_ready, 2 * t + j + 1)
                        if j == 0:
                            dve.wait_ge(biased_ready, t + 1)
                            dve.wait_ge(y_stored[u], 16 * pair)
                        dve.tensor_tensor(y[u][:, cols], acc[u][j][0:P, :], biased[u][:, cols], ALU.add).then_inc(y_ready, 1)
                    else:
                        dve.wait_ge(acc_high, 2 * t + j + 1)
                        if result == "scores":
                            for c in range(2):
                                dve.wait_ge(scored, 4 * t)
                                dve.tensor_tensor_reduce(raw[0:P, 2 + 2 * j + c, 0:H], acc[u][j][0:P, :], raw[0:P, c, cols],
                                                         1.0, 0.0, ALU.mult, ALU.add,
                                                         score_parts[:, u, c, j:j + 1]).then_inc(scored, 1)
                        high = gh[0:P, bass.ds(t, 1), cols].rearrange("p o n -> p (o n)")
                        low = gl[0:P, bass.ds(t, 1), cols].rearrange("p o n -> p (o n)")
                        dve.tensor_tensor(low, acc[u][j][0:P, :], high.bitcast(F32), ALU.subtract).then_inc(acc_free, 1)
                if result == "scores":
                    dve.wait_ge(scored, 4 * t + 4)
                    dve.tensor_tensor(scores[:, bass.ds(t, 1), :].rearrange("p o c -> p (o c)"), score_parts[:, u, :, 0],
                                      score_parts[:, u, :, 1], ALU.add).then_inc(score_ready, 1)

            def split(k):
                dve.wait_ge(w_high, k + 1)
                dve.tensor_tensor(wl[:, k, :], raw[:, k, :], wh[:, k, :].bitcast(F32), ALU.subtract).then_inc(w_low, 1)

            split(0)
            split(1)
            stats_of(0, 0, 0)
            split(2)
            apply(0, 0)
            split(3)
            turn(0, 0)
            split(4)
            stats_of(1, 1, 0)
            split(5)
            if xn is None:
                apply(1, 1)
            split(6)
            if xn is not None:
                apply(1, 1)
            split(7)
            turn(1, 1)
            if result == "scores":
                dve.wait_ge(extra, 16)
            with dve.Fori(0, T // 2 - 1) as pair:
                for u in range(2):
                    norm(pair * 2 + (u + 2), u, pair + 1)
                    result_of(pair * 2 + u, u, pair)
                    turn(pair * 2 + (u + 2), u)
            for t in (T - 2, T - 1):
                result_of(t, t % 2, T // 2 - 1)

        @block.tensor
        def _(pe):
            pe.wait_ge(ident_ready, 1)

            def turn(t, u, pair):
                if normalize:
                    pe.wait_ge(xn_ready, t + 1)
                else:
                    pe.wait_ge(x_loaded[u], 16 * (pair + 1))
                pe.wait_ge(xt_low, t)
                for k in range(K):
                    ins = pe.transpose(turned[k // 4][:, k % 4, :], xn_of(u)[:, k * 128:(k + 1) * 128], ident[:, :])
                    if k == K - 1:
                        ins.then_inc(turned_ready, 1)

            def first_products():
                pe.wait_ge(xt_low, 1)
                for k in range(K):
                    if k == K - 2:
                        turn(1, 1, 0)
                    pe.wait_ge(w_low, k + 1)
                    for j in range(2):
                        cols = slice(j * H, (j + 1) * H)
                        pe.matmul(acc[0][j][0:P, :], xt[0][:, 0, k, :], wh[:, k, cols], start=k == 0, stop=False)
                        pe.matmul(acc[0][j][0:P, :], xt[0][:, 0, k, :], wl[:, k, cols], start=False, stop=False)
                        ins = pe.matmul(acc[0][j][0:P, :], xt[0][:, 1, k, :], wh[:, k, cols], start=False, stop=k == K - 1)
                        if k == K - 1:
                            ins.then_inc(acc_ready, 1)

            def products(t, u, j, first):
                if not first:
                    pe.wait_ge(y_ready if result == "residual" else acc_free, 2 * t + j - 3)
                if j == 0:
                    pe.wait_ge(xt_low, t + 1)
                for k in range(K):
                    cols = slice(j * H, (j + 1) * H)
                    pe.matmul(acc[u][j][0:P, :], xt[u][:, 0, k, :], wh[:, k, cols], start=k == 0, stop=False)
                    pe.matmul(acc[u][j][0:P, :], xt[u][:, 0, k, :], wl[:, k, cols], start=False, stop=False)
                    ins = pe.matmul(acc[u][j][0:P, :], xt[u][:, 1, k, :], wh[:, k, cols], start=False, stop=k == K - 1)
                ins.then_inc(acc_ready, 1)

            turn(0, 0, 0)
            first_products()
            products(1, 1, 0, True)
            turn(2, 0, 1)
            products(1, 1, 1, True)
            with pe.Fori(1, T // 2 - 1) as pair:
                for u in range(2):
                    t = pair * 2 + u
                    products(t, u, 0, False)
                    turn(t + 1, 1 - u, pair + u)
                    products(t, u, 1, False)
            products(T - 2, 0, 0, False)
            turn(T - 1, 1, T // 2 - 1)
            products(T - 2, 0, 1, False)
            products(T - 1, 1, 0, False)
            products(T - 1, 1, 1, False)


def aggregate_phase(nc, name, xt_in, counts, counts_loaded, counts_by_src, deg_inv, bias, residual, out, raw, wh, wl, gh, gl,
                    raw_loaded, loads, next_w, own_w=None, unfold=None):
    sem = lambda s: nc.alloc_semaphore(f"{name}_{s}")
    with ExitStack() as ctx:
        ps = lambda s, shape: ctx.enter_context(nc.psum_tensor(f"{name}_{s}", shape, F32))
        local = Map(nc, LOCAL_AT, name)
        xt = local("xt", [128, 2, K, P], F32R)
        bias_row = local("bias_row", [P, D])
        x = local("x", [P, D]) if residual is not None else None
        mean = [local(f"mean{j}", [P, H]) for j in range(2)]
        y = local("y", [P, D])
        dinv = local("dinv", [P, T])
        if unfold is not None:
            C, B, E = 4, 32, 16
            KT = H // 128
            zero, taken = local("zero", [128, 1]), local("taken", [128, 1])
            local = Map(nc, RAW_AT, f"{name}_unfold")
            first = local("first", [128, 2, KT, C, B])
            second = local("second", [128, 2, C, E])
            terms = local("terms", [128, C, B, E])
            w_part = [local(f"w{i}", [128, H]) for i in range(2)]
            minus = local("minus", [128, H])
            assert local.at <= WH_AT
            zeroed = sem("zeroed")
            trains_loaded = sem("trains_loaded")
            unfold_step = sem("unfold_step")
            w_stored = sem("w_stored")
        own = [[ps(f"own{u}{j}", [128, 512]) for j in range(2)] for u in range(2)]
        agg = [[ps(f"agg{u}{j}", [128, 512]) for j in range(2)] for u in range(2)]
        if own_w is not None:
            own_loaded = [sem(f"own_loaded{i}") for i in range(2)]
        once = sem("once")
        xt_loaded = sem("xt_loaded")
        x_loaded = sem("x_loaded")
        own_ready = sem("own_ready")
        agg_ready = sem("agg_ready")
        mean_scaled = sem("mean_scaled")
        x_biased = sem("x_biased")
        mean_ready = sem("mean_ready")
        y_ready = sem("y_ready")
        y_stored = sem("y_stored")
        w_high = sem("w_high")
        w_low = sem("w_low")

        block = ctx.enter_context(nc.Block())

        @block.sync
        def _(sp):
            def loads_of(t, first):
                if not first:
                    sp.wait_ge(agg_ready, 2 * t)
                    load_counts(sp, counts, counts_by_src, counts_loaded, t)
                if not first:
                    sp.wait_ge(own_ready, 2 * t)
                sp.dma_start(xt[:, :, :, :].bitcast(F32),
                             xt_in[bass.ds(t, 1), :, :, :, :].rearrange("o p a k n -> (o p) a k n")).then_inc(xt_loaded, 16)
                if residual is not None:
                    if not first:
                        sp.wait_ge(mean_ready, 2 * t)
                    sp.dma_start(x[:, :], node_rows(residual, t)).then_inc(x_loaded, 16)

            def store(t):
                sp.wait_ge(y_ready, 2 * t + 2)
                sp.dma_start(node_rows(out, t), y[:, :]).then_inc(y_stored, 16)

            loads_of(0, True)
            with sp.Fori(1, T - 1) as t:
                loads_of(t, False)
                store(t - 1)
            loads_of(T - 1, False)
            if unfold is not None:
                sp.wait_ge(w_stored, 64 * KT)
                if next_w is not None:
                    sp.dma_start(raw[:, :, :], next_w.rearrange("(k p) n -> p k n", p=128)).then_inc(raw_loaded, 16)
            store(T - 2)
            store(T - 1)
            sp.wait_ge(y_stored, 16 * T)

        @block.gpsimd
        def _(pool):
            pool.dma_start(bias_row[:, :], bias.broadcast_to([P, D])).then_inc(once, 16)
            pool.dma_start(dinv[:, :], deg_inv).then_inc(once, 16)
            pool.wait_ge(once, 32)

            def tile(t):
                for j in range(2):
                    cols = slice(j * H, (j + 1) * H)
                    if residual is not None:
                        if j == 0:
                            pool.wait_ge(x_loaded, 16 * t + 16)
                            pool.tensor_tensor(x[:, :], x[:, :], bias_row[:, :], ALU.add).then_inc(x_biased, 1)
                            pool.wait_ge(x_biased, t + 1)
                        pool.wait_ge(mean_scaled, 2 * t + j + 1)
                        pool.tensor_tensor(mean[j][:, :], mean[j][:, :], x[:, cols], ALU.add).then_inc(mean_ready, 1)
                    else:
                        pool.wait_ge(mean_scaled, 2 * t + j + 1)
                        pool.tensor_tensor(mean[j][:, :], mean[j][:, :], bias_row[:, cols], ALU.add).then_inc(mean_ready, 1)

            def unfold_tile(k):
                n = [0]

                def then(ins):
                    n[0] += 1
                    ins.then_inc(unfold_step, 1)
                    pool.wait_ge(unfold_step, 7 * k + n[0])

                pool.wait_ge(w_stored, 64 * k)
                for part in range(2):
                    if part:
                        pool.wait_ge(unfold_step, 7 * k + 3)
                    then(pool.tensor_tensor(terms[:, :, :, :],
                                            first[:, part, bass.ds(k, 1), :, :].rearrange("p o c b -> p (o c) b").unsqueeze(3).broadcast_to([128, C, B, E]),
                                            second[:, part, :, :].unsqueeze(2).broadcast_to([128, C, B, E]), ALU.mult))
                    then(pool.tensor_tensor(terms[:, 0:2, :, :], terms[:, 0:2, :, :], terms[:, 2:4, :, :], ALU.add))
                    then(pool.tensor_tensor(w_part[part][:, :], terms[:, 0, :, :].rearrange("p b e -> p (b e)"),
                                            terms[:, 1, :, :].rearrange("p b e -> p (b e)"), ALU.add))
                then(pool.tensor_tensor(minus[:, :], zero[:, :].broadcast_to([128, H]), w_part[1][:, :], ALU.subtract))
                pool.tensor_tensor(taken[:, :], zero[:, :], zero[:, :], ALU.add)
                for src, i, j in ((w_part[0], 0, 0), (w_part[0], 1, 1), (w_part[1], 0, 1), (minus, 1, 0)):
                    pool.dma_start(unfold[2][bass.ds(k * 128 + i * H, 128), j * H:(j + 1) * H], src[:, :]).then_inc(w_stored, 16)

            if unfold is None:
                with pool.Fori(0, T) as t:
                    tile(t)
            else:
                pool.wait_ge(w_low, K)
                for part in range(2):
                    pool.dma_start(first[:, part, :, :, :].rearrange("p k c b -> p k (c b)"),
                                   unfold[0][part].rearrange("(k p) n -> p k n", p=128)).then_inc(trains_loaded, 16)
                    pool.dma_start(second[:, part, :, :].rearrange("p c e -> p (c e)"), unfold[1][part]).then_inc(trains_loaded, 16)
                pool.memset(zero[:, :], 0.0).then_inc(zeroed, 1)
                pool.wait_ge(zeroed, 1)
                pool.wait_ge(trains_loaded, 64)
                with pool.Fori(0, KT) as pair:
                    tile(pair * 2)
                    tile(pair * 2 + 1)
                    unfold_tile(pair)
                for t in range(2 * KT, T):
                    tile(t)

        @block.scalar
        def _(act):
            if own_w is not None:
                for i in range(2):
                    ks = slice(i * K // 2, (i + 1) * K // 2)
                    act.dma_start(raw[:, ks, :], own_w.rearrange("(k p) n -> p k n", p=128)[:, ks, :]).then_inc(own_loaded[i], 16)
            else:
                act.wait_ge(raw_loaded, 16 * loads)
            for k in range(K):
                if own_w is not None and k % (K // 2) == 0:
                    act.wait_ge(own_loaded[k // (K // 2)], 16)
                act.activation(wh[:, k, :], raw[:, k, :], ACT.Copy).then_inc(w_high, 1)
            act.wait_ge(once, 32)
            if next_w is not None and unfold is None:
                act.wait_ge(w_low, K)
                act.dma_start(raw[:, :, :], next_w.rearrange("(k p) n -> p k n", p=128)).then_inc(raw_loaded, 16)
            with act.Fori(0, T // 2) as pair:
                for u in range(2):
                    t = pair * 2 + u
                    act.wait_ge(y_ready, 2 * t)
                    act.wait_ge(agg_ready, 2 * t + 2)
                    for j in range(2):
                        act.activation(mean[j][:, :], agg[u][j][0:P, :], ACT.Copy,
                                       scale=dinv[:, bass.ds(t, 1)]).then_inc(mean_scaled, 1)

        @block.vector
        def _(dve):
            for k in range(K):
                dve.wait_ge(w_high, k + 1)
                dve.tensor_tensor(wl[:, k, :], raw[:, k, :], wh[:, k, :].bitcast(F32), ALU.subtract).then_inc(w_low, 1)
            with dve.Fori(0, T // 2) as pair:
                for u in range(2):
                    t = pair * 2 + u
                    for j in range(2):
                        dve.wait_ge(mean_ready, 2 * t + j + 1)
                        if j == 0:
                            dve.wait_ge(own_ready, 2 * t + 2)
                            dve.wait_ge(y_stored, 16 * t)
                        dve.tensor_tensor(y[:, j * H:(j + 1) * H], own[u][j][0:P, :], mean[j][:, :], ALU.add).then_inc(y_ready, 1)

        @block.tensor
        def _(pe):
            def products(t, u, first, split):
                pe.wait_ge(counts_loaded, 16 * t + 16)
                for j in range(2):
                    cols = slice(j * H, (j + 1) * H)
                    if not first:
                        pe.wait_ge(y_ready, 2 * t + j - 3)
                    for k in range(T):
                        pe.matmul(agg[u][j][0:P, :], counts[:, k, :], gh[0:P, k, cols], start=k == 0, stop=False)
                        ins = pe.matmul(agg[u][j][0:P, :], counts[:, k, :], gl[0:P, k, cols], start=False, stop=k == T - 1)
                    ins.then_inc(agg_ready, 1)
                pe.wait_ge(xt_loaded, 16 * t + 16)
                if split:
                    for k in range(K):
                        pe.wait_ge(w_low, k + 1)
                        for j in range(2):
                            cols = slice(j * H, (j + 1) * H)
                            pe.matmul(own[u][j][0:P, :], xt[:, 0, k, :], wh[:, k, cols], start=k == 0, stop=False)
                            pe.matmul(own[u][j][0:P, :], xt[:, 0, k, :], wl[:, k, cols], start=False, stop=False)
                            ins = pe.matmul(own[u][j][0:P, :], xt[:, 1, k, :], wh[:, k, cols], start=False, stop=k == K - 1)
                            if k == K - 1:
                                ins.then_inc(own_ready, 1)
                    return
                for j in range(2):
                    cols = slice(j * H, (j + 1) * H)
                    for k in range(K):
                        pe.matmul(own[u][j][0:P, :], xt[:, 0, k, :], wh[:, k, cols], start=k == 0, stop=False)
                        pe.matmul(own[u][j][0:P, :], xt[:, 0, k, :], wl[:, k, cols], start=False, stop=False)
                        ins = pe.matmul(own[u][j][0:P, :], xt[:, 1, k, :], wh[:, k, cols], start=False, stop=k == K - 1)
                    ins.then_inc(own_ready, 1)

            products(0, 0, True, True)
            products(1, 1, True, False)
            with pe.Fori(1, T // 2) as pair:
                for u in range(2):
                    products(pair * 2 + u, u, False, False)


F16 = mybir.dt.float16
I32 = mybir.dt.int32
EDGE_TILE = 128
TILES = 4
CHUNK = TILES * EDGE_TILE
EDGES = 21250
CHUNKS = -(-EDGES // CHUNK)
NONE = 2047


class GraphBuffers:

    def __init__(self, nc):
        place = Map(nc, RAW_AT, "graph")
        self.place = place
        self.node = place("node", [128, N], F16)
        self.src = place("src", [128, TILES * CHUNKS])
        self.dst = place("dst", [128, TILES * CHUNKS])
        self.bounds = place("bounds", [1, 2, T], I32)
        self.raw = Map(nc, GL_AT + 2 * D * 4, "graph")("raw", [128, K, D])
        self.raw_in = [nc.alloc_semaphore(f"graph_raw_in{i}") for i in range(2)]


def prepare_phase(nc, name, graph, edges_dst_chunks, edges_src_cols, edges_dst_cols, first_w):
    sem = lambda s: nc.alloc_semaphore(f"{name}_{s}")
    with ExitStack() as ctx:
        local = Map(nc, GH_AT, name)
        chunks_i = local("chunks_i", [CHUNKS, CHUNK], I32)
        src_i = local("src_i", [128, TILES * CHUNKS], I32)
        dst_i = local("dst_i", [128, TILES * CHUNKS], I32)
        chunks_f = local("chunks_f", [CHUNKS, CHUNK])
        node_i = local("node_i", [128, N], I32)
        square = local("square", [128, 128], I32)
        ident = local("ident", [128, 128])
        block_i = local("block_i", [1, T, CHUNKS], I32)
        block_at = local("block_at", [1, T, CHUNKS])
        chunk_i = local("chunk_i", [1, T, CHUNKS], I32)
        chunk_at = local("chunk_at", [1, T, CHUNKS])
        least = local("least", [CHUNKS, 1])
        most = local("most", [CHUNKS, 1])
        rows = local("rows", [1, 2, CHUNKS])
        local = Map(nc, LOCAL_AT, name)
        work = [local(f"work{i}", [1, T, CHUNKS]) for i in range(4)]
        bounds = local("bounds", [1, 2, T])
        rows_ps = ctx.enter_context(nc.psum_tensor(f"{name}_rows_ps", [128, 512], F32))

        chunks_loaded = sem("chunks_loaded")
        cols_loaded = sem("cols_loaded")
        made = sem("made")
        step = sem("step")
        rows_up = sem("rows_up")
        bounds_made = sem("bounds_made")
        block = ctx.enter_context(nc.Block())

        @block.sync
        def _(sp):
            sp.dma_start(chunks_i[:, :], edges_dst_chunks).then_inc(chunks_loaded, 16)
            sp.dma_start(src_i[:, :], edges_src_cols).then_inc(cols_loaded, 16)
            sp.dma_start(dst_i[:, :], edges_dst_cols).then_inc(cols_loaded, 16)

        @block.gpsimd
        def _(pool):
            pool.iota(block_i[:, :, :], pattern=[[P, T], [0, CHUNKS]], base=0, channel_multiplier=0).then_inc(made, 1)
            pool.iota(chunk_i[:, :, :], pattern=[[0, T], [1, CHUNKS]], base=0, channel_multiplier=0).then_inc(made, 1)
            pool.iota(square[:, :], pattern=[[1, 128]], base=0, channel_multiplier=-1).then_inc(made, 1)
            pool.iota(node_i[:, :], pattern=[[1, N]], base=0, channel_multiplier=0).then_inc(made, 1)

        @block.scalar
        def _(act):
            act.wait_ge(chunks_loaded, 16)
            act.wait_ge(cols_loaded, 32)
            halves = first_w.rearrange("(k p) n -> p k n", p=128)
            for i in range(2):
                ks = slice(i * K // 2, (i + 1) * K // 2)
                act.dma_start(graph.raw[:, ks, :], halves[:, ks, :]).then_inc(graph.raw_in[i], 16)

        @block.tensor
        def _(pe):
            pe.wait_ge(step, 6)
            pe.matmul(rows_ps[0:1, 0:CHUNKS], least[:, :], ident[0:CHUNKS, 0:CHUNKS], start=True, stop=True)
            pe.matmul(rows_ps[0:1, CHUNKS:2 * CHUNKS], most[:, :], ident[0:CHUNKS, 0:CHUNKS],
                      start=True, stop=True).then_inc(rows_up, 1)

        @block.vector
        def _(dve):
            n = [0]

            def then(ins, wait=True):
                n[0] += 1
                ins.then_inc(step, 1)
                if wait:
                    dve.wait_ge(step, n[0])

            dve.wait_ge(made, 3)
            then(dve.tensor_scalar(ident[:, :], square[:, :], 0.0, None, ALU.is_equal), False)
            then(dve.tensor_copy(block_at[:, :, :], block_i[:, :, :]), False)
            then(dve.tensor_copy(chunk_at[:, :, :], chunk_i[:, :, :]), False)
            dve.wait_ge(chunks_loaded, 16)
            then(dve.tensor_copy(chunks_f[:, :], chunks_i[:, :]))
            then(dve.tensor_reduce(least[:, :], chunks_f[:, :], AX.X, ALU.min), False)
            then(dve.tensor_reduce(most[:, :], chunks_f[:, :], AX.X, ALU.max), False)
            dve.wait_ge(rows_up, 1)
            then(dve.tensor_copy(rows[:, :, :], rows_ps[0:1, 0:2 * CHUNKS].rearrange("p (a c) -> p a c", a=2)), False)
            low = rows[:, 0:1, :].broadcast_to([1, T, CHUNKS])
            high = rows[:, 1:2, :].broadcast_to([1, T, CHUNKS])
            then(dve.tensor_scalar(work[0][:, :, :], block_at[:, :, :], float(P), None, ALU.add))
            then(dve.tensor_tensor(work[1][:, :, :], low, work[0][:, :, :], ALU.is_lt), False)
            then(dve.tensor_tensor(work[2][:, :, :], high, block_at[:, :, :], ALU.is_ge))
            then(dve.tensor_tensor(work[3][:, :, :], work[1][:, :, :], work[2][:, :, :], ALU.mult))
            then(dve.tensor_scalar(work[0][:, :, :], chunk_at[:, :, :], float(CHUNKS - 1), None, ALU.subtract), False)
            then(dve.tensor_scalar(work[1][:, :, :], chunk_at[:, :, :], 1.0, None, ALU.add))
            then(dve.tensor_tensor(work[2][:, :, :], work[0][:, :, :], work[3][:, :, :], ALU.mult))
            then(dve.tensor_tensor(work[0][:, :, :], work[1][:, :, :], work[3][:, :, :], ALU.mult), False)
            then(dve.tensor_reduce(bounds[:, 0, :], work[2][:, :, :], AX.X, ALU.min))
            then(dve.tensor_reduce(bounds[:, 1, :], work[0][:, :, :], AX.X, ALU.max), False)
            then(dve.tensor_scalar(bounds[:, 0, :], bounds[:, 0, :], float(CHUNKS - 1), None, ALU.add))
            then(dve.tensor_scalar(work[0][:, 0, 0:T], bounds[:, 0, :], 1.0, None, ALU.add))
            then(dve.tensor_tensor(bounds[:, 1, :], bounds[:, 1, :], work[0][:, 0, 0:T], ALU.max))
            dve.wait_ge(cols_loaded, 32)
            dve.tensor_copy(graph.src[:, :], src_i[:, :])
            dve.tensor_copy(graph.dst[:, :], dst_i[:, :])
            dve.wait_ge(made, 4)
            dve.tensor_copy(graph.bounds[:, :, :], bounds[:, :, :])
            dve.tensor_copy(graph.node[:, :], node_i[:, :])


def count_project_phase(nc, name, graph, rows, xt_out, wh, wl, gh, gl, counts_by_src, counts_by_dst, deg_inv,
                        counts_ahead):
    sem = lambda s: nc.alloc_semaphore(f"{name}_{s}")
    BANKS = [(0, 418), (418, 416), (834, 416)]
    ROUNDS = [(0, 4), (4, 4), (8, 2)]
    with ExitStack() as ctx:
        ps = lambda s, shape: ctx.enter_context(nc.psum_tensor(f"{name}_{s}", shape, F32))
        local = graph.place
        zeros = local("zeros", [128, 128], F16)
        hot_src = [local(f"hot_src{i}", [128, N], F16) for i in range(TILES)]
        hot_dst = [local(f"hot_dst{i}", [128, P], F16) for i in range(TILES)]
        by_dst = [local(f"by_dst{i}", [P, N]) for i in range(2)]
        by_src = local("by_src", [P, T, P], F32R)
        deg = local("deg", [P, T])
        deg_parts = [local(f"deg_parts{i}", [P, 3]) for i in range(2)]
        deg_two = [local(f"deg_two{i}", [P, 1]) for i in range(2)]
        assert local.at <= WH_AT
        local = Map(nc, LOCAL_AT, name)
        xt = [local(f"xt{u}", [128, 2, K, P], F32R) for u in range(2)]
        x = [local(f"x{u}", [P, D]) for u in range(2)]
        ident = local("ident", [P, P])
        square = local("square", [P, P], I32)
        power, eps, waits = (local(s, [P, 1]) for s in ("power", "eps", "waits"))
        stats = [local(f"stats{u}", [P, 12]) for u in range(2)]
        moments = [local(f"moments{u}", [P, 2]) for u in range(2)]
        rstd = [local(f"rstd{u}", [P, 1]) for u in range(2)]
        assert local.at <= HANDED_AT, local.at
        counted = ps("counted", [128, 3, 512])
        acc = [ps(f"acc{j}", [128, 512]) for j in range(2)]
        turned = [ps(f"turned{r}", [128, 4, P]) for r in range(2)]
        count_turned = ps("count_turned", [128, 512])

        made = sem("made")
        consts = sem("consts")
        x_loaded = [sem(f"x_loaded{u}") for u in range(2)]
        stats_ready = sem("stats_ready")
        moments_ready = sem("moments_ready")
        var_eps = sem("var_eps")
        rstd_ready = sem("rstd_ready")
        xn_ready = sem("xn_ready")
        turned_ready = sem("turned_ready")
        xt_high = sem("xt_high")
        xt_low = sem("xt_low")
        xt_stored = [sem(f"xt_stored{u}") for u in range(2)]
        acc_ready = sem("acc_ready")
        acc_high = sem("acc_high")
        acc_free = sem("acc_free")
        hot_ready = sem("hot_ready")
        hot_free = sem("hot_free")
        counted_ready = sem("counted_ready")
        by_dst_ready = sem("by_dst_ready")
        round_ready = sem("round_ready")
        by_src_ready = sem("by_src_ready")
        dst_stored = [sem(f"dst_stored{i}") for i in range(2)]
        src_stored = sem("src_stored")
        deg_ready = sem("deg_ready")
        deg_step = sem("deg_step")
        w_high = sem("w_high")
        w_low = sem("w_low")
        deg_stored = sem("deg_stored")

        fixed = lambda t: isinstance(t, int)

        def tiles(eng, step):
            for t in range(2):
                step(t, t % 2, t // 2)
            with eng.Fori(0, (T - 4) // 2) as i:
                step(i * 2 + 2, 0, i + 1)
                step(i * 2 + 3, 1, i + 1)
            for t in range(T - 2, T):
                step(t, t % 2, t // 2)

        block = ctx.enter_context(nc.Block())

        @block.sync
        def _(sp):
            def load_x(t, u):
                sp.dma_start(x[u][:, :], node_rows(rows, t)).then_inc(x_loaded[u], 16)

            def store_by_src(t):
                sp.wait_ge(by_src_ready, 3 * t + 3)
                sp.dma_start(counts_by_src[bass.ds(t, 1), :, :, :].rearrange("o s k d -> (o s) k d"),
                             by_src[:, :, :].bitcast(F32)).then_inc(src_stored, 16)

            def step(t, u, q):
                if not (fixed(t) and t == 0):
                    store_by_src(t - 1)
                sp.wait_ge(xt_low, t + 1)
                sp.dma_start(xt_out[bass.ds(t, 1), :, :, :, :].rearrange("o p a k n -> (o p) a k n"),
                             xt[u][:, :, :, :].bitcast(F32)).then_inc(xt_stored[u], 16)
                if not fixed(t) or t + 2 < T:
                    sp.wait_ge(turned_ready, t + 1)
                    load_x(t + 2, u)
                sp.wait_ge(by_dst_ready, t + 1)
                sp.dma_start(counts_by_dst[:, :, bass.ds(t, 1), :].rearrange("t d o s -> d (t o) s"),
                             by_dst[u][:, :].rearrange("d (t s) -> d t s", s=P)).then_inc(dst_stored[u], 16)

            load_x(0, 0)
            load_x(1, 1)
            tiles(sp, step)
            sp.wait_ge(src_stored, 16 * (T - 1))
            load_counts(sp, *counts_ahead, 0)
            store_by_src(T - 1)
            sp.wait_ge(deg_ready, T + 1)
            sp.dma_start(deg_inv, deg[:, :]).then_inc(deg_stored, 16)
            for u in range(2):
                sp.wait_ge(dst_stored[u], 16 * (T // 2))
                sp.wait_ge(xt_stored[u], 16 * (T // 2))
            sp.wait_ge(src_stored, 16 * T)
            sp.wait_ge(deg_stored, 16)

        @block.gpsimd
        def _(pool):
            pool.iota(square[:, :], pattern=[[1, P]], base=0, channel_multiplier=-1).then_inc(made, 1)
            pool.memset(power[:, :], -0.5).then_inc(made, 1)
            pool.memset(eps[:, :], 1e-5).then_inc(made, 1)
            pool.wait_ge(made, 3)

            def step(t, u, q):
                pool.wait_ge(moments_ready, t + 1)
                pool.tensor_tensor(rstd[u][:, :], moments[u][:, 1:2], eps[:, :], ALU.add).then_inc(var_eps, 1)
                pool.wait_ge(var_eps, t + 1)
                pool.tensor_tensor(rstd[u][:, :], rstd[u][:, :], power[:, :], ALU.pow).then_inc(rstd_ready, 1)
                if fixed(t) and t == 1:
                    for k in range(K):
                        pool.wait_ge(w_high, k + 1)
                        pool.tensor_tensor(wl[:, k, :], graph.raw[:, k, :], wh[:, k, :].bitcast(F32), ALU.subtract).then_inc(w_low, 1)
                    degree(0, 0)
                if not (fixed(t) and t < 2):
                    degree(t - 1, 1 - u)

            def degree(t, u):
                pool.wait_ge(by_dst_ready, t + 1)
                pool.tensor_tensor(deg_two[u][:, :], deg_parts[u][:, 0:1], deg_parts[u][:, 1:2], ALU.add).then_inc(deg_step, 1)
                pool.wait_ge(deg_step, t + 1)
                pool.tensor_tensor(deg[:, bass.ds(t, 1)], deg_two[u][:, :], deg_parts[u][:, 2:3], ALU.add).then_inc(deg_ready, 1)

            tiles(pool, step)
            degree(T - 1, 1)

        @block.scalar
        def _(act):
            def turn(t, u, q):
                act.wait_ge(turned_ready, t + 1)
                if not (fixed(t) and t < 2):
                    act.wait_ge(acc_ready, 2 * t - 2)
                    act.wait_ge(xt_stored[u], 16 * q)
                for r in range(2):
                    act.activation(xt[u][:, 0, 4 * r:4 * r + 4, :], turned[r][:, :, :], ACT.Copy).then_inc(xt_high, 1)

            def round_of(t, r):
                k0, kn = ROUNDS[r]
                act.wait_ge(round_ready, 3 * t + r + 1)
                if r == 0 and not (fixed(t) and t == 0):
                    act.wait_ge(src_stored, 16 * t)
                act.activation(by_src[:, k0:k0 + kn, :], count_turned[0:P, 0:kn * P].rearrange("s (k d) -> s k d", d=P),
                               ACT.Copy).then_inc(by_src_ready, 1)

            def high(t, j):
                act.wait_ge(acc_ready, 2 * t + j + 1)
                act.activation(gh[0:P, bass.ds(t, 1), j * H:(j + 1) * H].rearrange("p o n -> p (o n)"),
                               acc[j][0:P, :], ACT.Copy).then_inc(acc_high, 1)

            def step(t, u, q):
                act.wait_ge(counted_ready, t + 1)
                if not (fixed(t) and t < 2):
                    act.wait_ge(dst_stored[u], 16 * q)
                    act.wait_ge(deg_ready, t - 1)
                for j, (at, n) in enumerate(BANKS):
                    ins = act.activation(by_dst[u][:, at:at + n], counted[0:P, j, 0:n], ACT.Copy, accum_out=deg_parts[u][:, j:j + 1])
                ins.then_inc(by_dst_ready, 1)
                if not fixed(t) or t + 1 < T:
                    turn(t + 1, 1 - u, q + u)
                round_of(t, 0)
                high(t, 0)
                round_of(t, 1)
                high(t, 1)
                round_of(t, 2)

            for k in range(K):
                if k % (K // 2) == 0:
                    act.wait_ge(graph.raw_in[k // (K // 2)], 16)
                if k == K // 2:
                    turn(0, 0, 0)
                act.activation(wh[:, k, :], graph.raw[:, k, :], ACT.Copy).then_inc(w_high, 1)
            tiles(act, step)

        @block.vector
        def _(dve):
            dve.wait_ge(made, 3)
            dve.tensor_scalar(ident[:, :], square[:, :], 0.0, None, ALU.is_equal).then_inc(consts, 1)
            dve.memset(zeros[:, :], 0.0).then_inc(consts, 1)
            done = dve.alloc_register(f"{name}_hot_made")
            dve.reg_mov(done, 0)

            def norm(t, u, q):
                stats_of(t, u, q)
                apply(t, u)

            def stats_of(t, u, q):
                dve.wait_ge(x_loaded[u], 16 * (q + 1))
                for j in range(2):
                    dve.bn_stats(stats[u][:, 6 * j:6 * j + 6], x[u][:, j * H:(j + 1) * H]).then_inc(stats_ready, 1)
                dve.wait_ge(stats_ready, 2 * t + 2)
                dve.memset(waits[:, :], 0.0)
                dve.bn_aggr(moments[u][:, :], stats[u][:, :]).then_inc(moments_ready, 1)

            def apply(t, u):
                dve.wait_ge(rstd_ready, t + 1)
                dve.tensor_scalar(x[u][:, :], x[u][:, :], moments[u][:, 0:1], rstd[u][:, 0:1],
                                  ALU.subtract, ALU.mult).then_inc(xn_ready, 1)

            def turn(t, u):
                for r in range(2):
                    dve.wait_ge(xt_high, 2 * t + r + 1)
                    ins = dve.tensor_tensor(xt[u][:, 1, 4 * r:4 * r + 4, :], turned[r][:, :, :],
                                            xt[u][:, 0, 4 * r:4 * r + 4, :].bitcast(F32), ALU.subtract)
                ins.then_inc(xt_low, 1)

            def low(t, j):
                dve.wait_ge(acc_high, 2 * t + j + 1)
                part = lambda g: g[0:P, bass.ds(t, 1), j * H:(j + 1) * H].rearrange("p o n -> p (o n)")
                dve.tensor_tensor(part(gl), acc[j][0:P, :], part(gh).bitcast(F32), ALU.subtract).then_inc(acc_free, 1)

            def hots(t):
                first = dve.value_load(graph.bounds[0:1, 0, bass.ds(t, 1)], min_val=0, max_val=CHUNKS - 1)
                last = dve.value_load(graph.bounds[0:1, 1, bass.ds(t, 1)], min_val=1, max_val=CHUNKS)
                with dve.Fori(first, last) as c:
                    for h in range(TILES):
                        dve.wait_ge(hot_free, dve.snap(done) + h)
                        dve.tensor_scalar(hot_dst[h][:, :], graph.node[:, bass.ds(t * P, P)],
                                          graph.dst[:, bass.ds(c * TILES + h, 1)], None, ALU.is_equal)
                        dve.tensor_scalar(hot_src[h][:, :], graph.node[:, :],
                                          graph.src[:, bass.ds(c * TILES + h, 1)], None, ALU.is_equal).then_inc(hot_ready, 1)
                    dve.reg_add(done, done, TILES)

            def rest(t, u):
                low(t, 0)
                low(t, 1)

            def step(t, u, q):
                hots(t)
                if fixed(t) and t == 0:
                    turn(0, 0)
                else:
                    rest(t - 1, 1 - u)
                if not fixed(t) or t + 1 < T:
                    turn(t + 1, 1 - u)
                if not fixed(t) or t + 2 < T:
                    norm(t + 2, u, q + 1)

            for t in range(2):
                stats_of(t, t, 0)
            for t in range(2):
                apply(t, t)
            tiles(dve, step)
            rest(T - 1, 1)
            dve.wait_ge(deg_ready, T)
            dve.tensor_scalar(deg[:, :], deg[:, :], 1.0, None, ALU.max).then_inc(consts, 1)
            dve.wait_ge(consts, 3)
            dve.reciprocal(deg[:, :], deg[:, :]).then_inc(deg_ready, 1)

        @block.tensor
        def _(pe):
            pe.wait_ge(consts, 2)
            pe.sem_inc(hot_free, TILES - 1)
            done = pe.alloc_register(f"{name}_hot_used")
            pe.reg_mov(done, 0)

            def turn(t, u):
                pe.wait_ge(xn_ready, t + 1)
                pe.wait_ge(xt_low, t)
                for k in range(K):
                    ins = pe.transpose(turned[k // 4][:, k % 4, :], x[u][:, k * 128:(k + 1) * 128], ident[:, :])
                ins.then_inc(turned_ready, 1)

            def count(t):
                first = pe.value_load(graph.bounds[0:1, 0, bass.ds(t, 1)], min_val=0, max_val=CHUNKS - 1)
                last = pe.value_load(graph.bounds[0:1, 1, bass.ds(t, 1)], min_val=1, max_val=CHUNKS)
                if not (fixed(t) and t == 0):
                    pe.wait_ge(by_dst_ready, t)
                for j, (at, n) in enumerate(BANKS):
                    pe.matmul(counted[:, j, 0:n], zeros[:, :], graph.node[:, 0:n], start=True, stop=False)
                with pe.Fori(first, last) as c:
                    for h in range(TILES):
                        pe.wait_ge(hot_ready, pe.snap(done) + (h + 1))
                        for j, (at, n) in enumerate(BANKS):
                            mm = pe.matmul(counted[0:P, j, 0:n], hot_dst[h][:, :], hot_src[h][:, at:at + n],
                                           start=False, stop=False)
                        mm.then_inc(hot_free, 1)
                    pe.reg_add(done, done, TILES)
                for j, (at, n) in enumerate(BANKS):
                    mm = pe.matmul(counted[:, j, 0:n], zeros[:, :], graph.node[:, 0:n], start=False, stop=True)
                mm.then_inc(counted_ready, 1)

            def round_of(t, u, r):
                if r == 0:
                    pe.wait_ge(by_dst_ready, t + 1)
                if not (fixed(t) and t == 0 and r == 0):
                    pe.wait_ge(by_src_ready, 3 * t + r)
                k0, kn = ROUNDS[r]
                for k in range(k0, k0 + kn):
                    mm = pe.transpose(count_turned[0:P, (k - k0) * P:(k - k0 + 1) * P],
                                      by_dst[u][:, k * P:(k + 1) * P], ident[:, :])
                mm.then_inc(round_ready, 1)

            def products(t, u, j):
                if not (fixed(t) and t == 0):
                    pe.wait_ge(acc_free, 2 * t + j - 1)
                pe.wait_ge(xt_low, t + 1)
                cols = slice(j * H, (j + 1) * H)
                for k in range(K):
                    if fixed(t) and t == 0 and j == 0:
                        pe.wait_ge(w_low, k + 1)
                    pe.matmul(acc[j][0:P, :], xt[u][:, 0, k, :], wh[:, k, cols], start=k == 0, stop=False)
                    pe.matmul(acc[j][0:P, :], xt[u][:, 0, k, :], wl[:, k, cols], start=False, stop=False)
                    ins = pe.matmul(acc[j][0:P, :], xt[u][:, 1, k, :], wh[:, k, cols], start=False, stop=k == K - 1)
                ins.then_inc(acc_ready, 1)

            def step(t, u, q):
                count(t)
                if not fixed(t) or t + 1 < T:
                    turn(t + 1, 1 - u)
                round_of(t, u, 0)
                products(t, u, 0)
                round_of(t, u, 1)
                products(t, u, 1)
                round_of(t, u, 2)

            turn(0, 0)
            tiles(pe, step)


def attention_phase(nc, name, rows, counts_by_dst, scores, norm_w, router_t, gh, gl, base, tokens, logits):
    sem = lambda s: nc.alloc_semaphore(f"{name}_{s}")
    EXPERTS = 8
    LARGEST = 3.4028234e38
    with ExitStack() as ctx:
        ps = lambda s, shape: ctx.enter_context(nc.psum_tensor(f"{name}_{s}", shape, F32))
        local = Map(nc, RAW_AT, name)
        counts = [local(f"counts{u}", [P, T, P]) for u in range(2)]
        z = [local(f"z{u}", [P, T, P]) for u in range(2)]
        e = local("e", [P, T, P])
        weight = local("weight", [P, T, P])
        ph = [local(f"ph{u}", [P, T, P], F32R) for u in range(2)]
        pl = [local(f"pl{u}", [P, T, P], F32R) for u in range(2)]
        al_row = local("al_row", [P, T, P])
        x = [local(f"x{u}", [P, D]) for u in range(2)]
        low = local("low", [P, D])
        nw_row = local("nw_row", [P, D])
        h = [local(f"h{u}", [P, D]) for u in range(2)]
        assert local.at <= GH_AT, local.at
        local = Map(nc, LOCAL_AT, name)
        y = [local(f"y{u}", [P, D]) for u in range(2)]
        token = [local(f"token{u}", [P, D]) for u in range(2)]
        token_t = local("token_t", [128, K, P])
        ident = local("ident", [P, P])
        square = local("square", [P, P], mybir.dt.int32)
        router = local("router", [128, K, EXPERTS])
        sc = scores
        ones = local("ones", [P, 2])
        part_sum = [local(f"part_sum{u}", [P, P]) for u in range(2)]
        small = lambda s: [local(f"{s}{u}", [P, 1]) for u in range(2)]
        total, rtotal, rstd, rrms, meansq = small("total"), small("rtotal"), small("rstd"), small("rrms"), small("meansq")
        stats = [local(f"stats{u}", [P, 12]) for u in range(2)]
        moments = [local(f"moments{u}", [P, 2]) for u in range(2)]
        power, eps, eps_rms, waits = (local(s, [P, 1]) for s in ("power", "eps", "eps_rms", "waits"))
        logit_rows = local("logit_rows", [P, T, EXPERTS])
        assert local.at <= HANDED_AT, local.at
        acc = [[ps(f"acc{u}{j}", [128, 512]) for j in range(2)] for u in range(2)]
        turned = [ps(f"turned{r}", [128, 4, P]) for r in range(2)]
        sums = ps("sums", [128, 2])
        logit_ps = ps("logit_ps", [128, EXPERTS])

        once = sem("once")
        part_sum_ready = sem("part_sum_ready")
        made = sem("made")
        consts = sem("consts")
        row_ready = sem("row_ready")
        al_ready = sem("al_ready")
        counts_loaded = [sem(f"counts_loaded{u}") for u in range(2)]
        x_loaded = [sem(f"x_loaded{u}") for u in range(2)]
        z_ready = sem("z_ready")
        leaky_ready = sem("leaky_ready")
        e_ready = sem("e_ready")
        weight_ready = sem("weight_ready")
        ph_ready = sem("ph_ready")
        pl_ready = sem("pl_ready")
        acc_ready = sem("acc_ready")
        sums_ready = sem("sums_ready")
        total_ready = sem("total_ready")
        rtotal_ready = sem("rtotal_ready")
        h_ready = sem("h_ready")
        low_ready = sem("low_ready")
        exp_ready = sem("exp_ready")
        elu_ready = sem("elu_ready")
        x3_ready = sem("x3_ready")
        stats_ready = sem("stats_ready")
        moments_ready = sem("moments_ready")
        pool_step = sem("pool_step")
        rstd_ready = sem("rstd_ready")
        y_ready = sem("y_ready")
        meansq_ready = sem("meansq_ready")
        rrms_ready = sem("rrms_ready")
        token_ready = sem("token_ready")
        base_ready = sem("base_ready")
        turned_ready = sem("turned_ready")
        token_t_ready = sem("token_t_ready")
        logit_ready = sem("logit_ready")
        logit_read = sem("logit_read")
        base_stored = [sem(f"base_stored{u}") for u in range(2)]
        token_stored = [sem(f"token_stored{u}") for u in range(2)]

        def tiles(eng, step):
            for t in range(3):
                step(t, t % 2, t // 2)
            with eng.Fori(0, (T - 6) // 2) as i:
                step(i * 2 + 3, 1, i + 1)
                step(i * 2 + 4, 0, i + 2)
            for t in range(T - 3, T):
                step(t, t % 2, t // 2)

        fixed = lambda t: isinstance(t, int)
        block = ctx.enter_context(nc.Block())

        @block.sync
        def _(sp):
            sp.dma_start(nw_row[:, :], norm_w.broadcast_to([P, D])).then_inc(once, 16)
            sp.dma_start(router[:, :, :], router_t.rearrange("p (k e) -> p k e", e=EXPERTS)).then_inc(once, 16)

            def load_counts(t, u):
                sp.dma_start(counts[u][:, :, :], counts_by_dst[bass.ds(t, 1), :, :, :].rearrange("o d k s -> (o d) k s")).then_inc(counts_loaded[u], 16)

            def load_x(t, u):
                sp.dma_start(x[u][:, :], node_rows(rows, t)).then_inc(x_loaded[u], 16)

            def store_token(t, u):
                sp.wait_ge(token_ready, t + 1)
                sp.dma_start(node_rows(tokens, t), token[u][:, :]).then_inc(token_stored[u], 16)

            def step(t, u, q):
                more = not fixed(t) or t + 2 < T
                if not fixed(t) or t + 3 < T:
                    sp.wait_ge(weight_ready, t + 2)
                    load_counts(t + 3, 1 - u)
                if not (fixed(t) and t == 0):
                    store_token(t - 1, 1 - u)
                sp.wait_ge(base_ready, t + 1)
                sp.dma_start(node_rows(base, t), x[u][:, :]).then_inc(base_stored[u], 16)
                if more:
                    sp.wait_ge(base_stored[u], 16 * q + 16)
                    load_x(t + 2, u)

            for t in range(2):
                load_counts(t, t)
                load_x(t, t)
            sp.wait_ge(weight_ready, 1)
            load_counts(2, 0)
            tiles(sp, step)
            store_token(T - 1, (T - 1) % 2)
            for u in range(2):
                sp.wait_ge(token_stored[u], 16 * (T // 2))
                sp.wait_ge(base_stored[u], 16 * (T // 2))
            sp.wait_ge(logit_read, T)
            sp.dma_start(logits, logit_rows[:, :, :]).then_inc(once, 16)
            sp.wait_ge(once, 48)

        @block.gpsimd
        def _(pool):
            pool.iota(square[:, :], pattern=[[1, P]], base=0, channel_multiplier=-1).then_inc(made, 1)
            pool.memset(power[:, :], -0.5).then_inc(made, 1)
            pool.memset(eps[:, :], 1e-5).then_inc(made, 1)
            pool.memset(eps_rms[:, :], 1e-6).then_inc(made, 1)
            pool.memset(ones[:, :], 1.0).then_inc(made, 1)
            pool.wait_ge(made, 5)
            pool.wait_ge(al_ready, 3)

            def edge_z(t, u):
                if not (fixed(t) and t < 2):
                    pool.wait_ge(leaky_ready, t - 1)
                pool.tensor_tensor(z[u][:, :, :], al_row[:, bass.ds(t, 1), :].broadcast_to([P, T, P]),
                                   sc[:, :, 1:2].broadcast_to([P, T, P]), ALU.add).then_inc(z_ready, 1)

            def step(t, u, q):
                pool.wait_ge(moments_ready, t + 1)
                pool.tensor_tensor(rstd[u][:, :], moments[u][:, 1:2], eps[:, :], ALU.add).then_inc(pool_step, 1)
                pool.wait_ge(pool_step, 2 * t + 1)
                pool.tensor_tensor(rstd[u][:, :], rstd[u][:, :], power[:, :], ALU.pow).then_inc(rstd_ready, 1)
                if not fixed(t) or t + 3 < T:
                    edge_z(t + 3, 1 - u)
                pool.wait_ge(meansq_ready, t + 1)
                pool.tensor_tensor(rrms[u][:, :], meansq[u][:, :], eps_rms[:, :], ALU.add).then_inc(pool_step, 1)
                pool.wait_ge(pool_step, 2 * t + 2)
                pool.tensor_tensor(rrms[u][:, :], rrms[u][:, :], power[:, :], ALU.pow).then_inc(rrms_ready, 1)
                pool.tensor_tensor(x[u][:, :], x[u][:, :], y[u][:, :], ALU.add).then_inc(base_ready, 1)

            for t in range(3):
                edge_z(t, t % 2)
            tiles(pool, step)

        @block.scalar
        def _(act):
            act.wait_ge(row_ready, 1)
            for r, (k0, kn) in enumerate([(0, 4), (4, 4), (8, 2)]):
                act.activation(al_row[:, k0:k0 + kn, :],
                               acc[r // 2][r % 2][0:P, 0:kn * P].rearrange("p (k n) -> p k n", n=P), ACT.Copy).then_inc(al_ready, 1)

            def edge_exp(t):
                act.wait_ge(leaky_ready, t + 1)
                act.activation(e[:, :, :], e[:, :, :], ACT.Exp, scale=-1.0).then_inc(e_ready, 1)

            def edge_high(t, u):
                act.wait_ge(weight_ready, t + 1)
                act.activation(ph[u][:, :, :], weight[:, :, :], ACT.Copy).then_inc(ph_ready, 1)

            def turn(t):
                act.wait_ge(turned_ready, t + 1)
                act.wait_ge(logit_ready, t)
                for r in range(2):
                    ins = act.activation(token_t[:, 4 * r:4 * r + 4, :], turned[r][:, :, :], ACT.Copy)
                ins.then_inc(token_t_ready, 1)

            def logit(t):
                act.wait_ge(logit_ready, t + 1)
                act.activation(logit_rows[:, bass.ds(t, 1), :].rearrange("p o n -> p (o n)"),
                               logit_ps[0:P, :], ACT.Copy).then_inc(logit_read, 1)

            def step(t, u, q):
                ahead = not fixed(t) or t + 2 < T
                if ahead:
                    edge_exp(t + 2)
                act.wait_ge(acc_ready, 2 * t + 2)
                act.wait_ge(rtotal_ready, t + 1)
                for j in range(2):
                    act.activation(h[u][:, j * H:(j + 1) * H], acc[u][j][0:P, :], ACT.Copy, scale=rtotal[u][:, 0:1]).then_inc(h_ready, 1)
                if ahead:
                    edge_high(t + 2, u)
                act.wait_ge(low_ready, t + 1)
                act.activation(low[:, :], low[:, :], ACT.Exp).then_inc(exp_ready, 1)
                if not (fixed(t) and t < 3):
                    logit(t - 3)
                if not (fixed(t) and t < 2):
                    turn(t - 2)
                act.wait_ge(y_ready, t + 1)
                act.activation(low[:, :], y[u][:, :], ACT.Square, scale=D ** -0.5, accum_out=meansq[u][:, 0:1]).then_inc(meansq_ready, 1)

            for t in range(2):
                edge_exp(t)
                edge_high(t, t)
            tiles(act, step)
            logit(T - 3)
            for t in (T - 2, T - 1):
                turn(t)
                logit(t)

        @block.vector
        def _(dve):
            dve.wait_ge(made, 5)
            dve.tensor_scalar(ident[:, :], square[:, :], 0.0, None, ALU.is_equal).then_inc(consts, 1)

            def edge_leaky(t, u):
                dve.wait_ge(z_ready, t + 1)
                dve.wait_ge(weight_ready, t)
                dve.scalar_tensor_tensor(e[:, :, :], z[u][:, :, :], 0.1, z[u][:, :, :], ALU.mult, ALU.max).then_inc(leaky_ready, 1)

            def edge_weight(t, u, q):
                dve.wait_ge(e_ready, t + 1)
                dve.wait_ge(counts_loaded[u], 16 * q + 16)
                dve.wait_ge(part_sum_ready, t)
                dve.scalar_tensor_tensor(weight[:, :, :], e[:, :, :], LARGEST, counts[u][:, :, :], ALU.min, ALU.mult).then_inc(weight_ready, 1)

            def edge_low(t, u):
                dve.wait_ge(ph_ready, t + 1)
                dve.tensor_tensor(pl[u][:, :, :], weight[:, :, :], ph[u][:, :, :].bitcast(F32), ALU.subtract).then_inc(pl_ready, 1)
                dve.tensor_reduce(part_sum[u][:, :], weight[:, :, :].rearrange("p k s -> p s k"), AX.X, ALU.add).then_inc(part_sum_ready, 1)

            def make_token(t, u, q):
                dve.wait_ge(rrms_ready, t + 1)
                if not (fixed(t) and t < 2):
                    dve.wait_ge(token_stored[u], 16 * q)
                    dve.wait_ge(turned_ready, t - 1)
                dve.scalar_tensor_tensor(token[u][:, :], y[u][:, :], rrms[u][:, 0:1], nw_row[:, :], ALU.mult, ALU.mult).then_inc(token_ready, 1)

            def step(t, u, q):
                ahead = not fixed(t) or t + 2 < T
                if ahead:
                    edge_leaky(t + 2, u)
                dve.wait_ge(sums_ready, t + 1)
                dve.tensor_scalar(total[u][:, :], sums[0:P, 0:1], 1e-5, None, ALU.add).then_inc(total_ready, 1)
                dve.wait_ge(total_ready, t + 1)
                dve.reciprocal(rtotal[u][:, :], total[u][:, :]).then_inc(rtotal_ready, 1)
                if ahead:
                    edge_weight(t + 2, u, q + 1)
                dve.wait_ge(h_ready, 2 * t + 2)
                dve.wait_ge(meansq_ready, t)
                dve.tensor_scalar(low[:, :], h[u][:, :], 0.0, None, ALU.min).then_inc(low_ready, 1)
                if ahead:
                    edge_low(t + 2, u)
                dve.wait_ge(exp_ready, t + 1)
                dve.scalar_tensor_tensor(h[u][:, :], h[u][:, :], 0.0, low[:, :], ALU.max, ALU.add).then_inc(elu_ready, 1)
                dve.wait_ge(elu_ready, t + 1)
                dve.wait_ge(x_loaded[u], 16 * q + 16)
                dve.scalar_tensor_tensor(x[u][:, :], h[u][:, :], -1.0, x[u][:, :], ALU.add, ALU.add).then_inc(x3_ready, 1)
                dve.wait_ge(x3_ready, t + 1)
                for j in range(2):
                    dve.bn_stats(stats[u][:, 6 * j:6 * j + 6], x[u][:, j * H:(j + 1) * H]).then_inc(stats_ready, 1)
                dve.wait_ge(stats_ready, 2 * t + 2)
                dve.memset(waits[:, :], 0.0)
                dve.bn_aggr(moments[u][:, :], stats[u][:, :]).then_inc(moments_ready, 1)
                if not (fixed(t) and t == 0):
                    make_token(t - 1, 1 - u, q - 1 + u)
                dve.wait_ge(rstd_ready, t + 1)
                if not (fixed(t) and t < 2):
                    dve.wait_ge(base_ready, t - 1)
                dve.tensor_scalar(y[u][:, :], x[u][:, :], moments[u][:, 0:1], rstd[u][:, 0:1], ALU.subtract, ALU.mult).then_inc(y_ready, 1)

            for t in range(2):
                edge_leaky(t, t)
                edge_weight(t, t, 0)
                edge_low(t, t)
            dve.wait_ge(once, 32)
            tiles(dve, step)
            make_token(T - 1, (T - 1) % 2, (T - 1) // 2)

        @block.tensor
        def _(pe):
            pe.wait_ge(consts, 1)
            for t in range(T):
                r = t // 4
                ins = pe.matmul(acc[r // 2][r % 2][0:P, (t % 4) * P:(t % 4 + 1) * P],
                                sc[:, t, 0:1].broadcast_to([P, P]), ident[:, :], start=True, stop=True)
            ins.then_inc(row_ready, 1)
            pe.wait_ge(al_ready, 3)

            def half(t, u, j):
                if j == 0:
                    pe.wait_ge(pl_ready, t + 1)
                if not (fixed(t) and t < 2):
                    pe.wait_ge(h_ready, 2 * t + j - 3)
                cols = slice(j * H, (j + 1) * H)
                for k in range(T):
                    pe.matmul(acc[u][j][0:P, :], ph[u][:, k, :], gh[0:P, k, cols], start=k == 0, stop=False)
                    pe.matmul(acc[u][j][0:P, :], ph[u][:, k, :], gl[0:P, k, cols], start=False, stop=False)
                    ins = pe.matmul(acc[u][j][0:P, :], pl[u][:, k, :], gh[0:P, k, cols], start=False, stop=k == T - 1)
                ins.then_inc(acc_ready, 1)

            def sum_of(t, u):
                pe.wait_ge(part_sum_ready, t + 1)
                pe.wait_ge(total_ready, t)
                pe.matmul(sums[0:P, :], part_sum[u][:, :], ones[:, :], start=True, stop=True).then_inc(sums_ready, 1)

            def turn(t, u):
                pe.wait_ge(token_ready, t + 1)
                pe.wait_ge(token_t_ready, t)
                for k in range(K):
                    ins = pe.transpose(turned[k // 4][:, k % 4, :], token[u][:, k * 128:(k + 1) * 128], ident[:, :])
                ins.then_inc(turned_ready, 1)

            def route(t):
                pe.wait_ge(token_t_ready, t + 1)
                pe.wait_ge(logit_read, t)
                for k in range(K):
                    ins = pe.matmul(logit_ps[0:P, :], token_t[:, k, :], router[:, k, :], start=k == 0, stop=k == K - 1)
                ins.then_inc(logit_ready, 1)

            def step(t, u, q):
                half(t, u, 0)
                sum_of(t, u)
                if not (fixed(t) and t < 3):
                    turn(t - 3, 1 - u)
                half(t, u, 1)
                if not (fixed(t) and t < 3):
                    route(t - 3)

            tiles(pe, step)
            for t in range(T - 3, T):
                turn(t, t % 2)
                route(t)


U32 = mybir.dt.uint32
EXPERTS, TOP, HID = 8, 2, 352
BLOCK = 128
BLOCKS = (TOP * N + EXPERTS * (BLOCK - 1) + EXPERTS) // BLOCK
SLOT_BLOCKS = BLOCKS + 2
HK = 3
HROWS = [128, 128, HID - 256]


AT_EXPERT = 0
AT_SIDE = AT_EXPERT + BLOCKS
AT_COUNT = AT_SIDE + BLOCKS + 1
AT_TOTAL = AT_COUNT + EXPERTS
AT_REST = AT_TOTAL + 1
PLAN = AT_REST + 1


class ExpertBuffers:

    def __init__(self, nc):
        place = Map(nc, 0, "expert")
        self.up_w = place("up_w", [128, 2, 2, K, 2 * HID], F32R)
        self.down_w = place("down_w", [128, 2, 2, HK, D], F32R)
        raw_at = place.at
        self.up_raw = place("up_raw", [128, K, 2 * HID])
        self.down_raw = place("down_raw", [128, HK, D])
        self.early = (place.at - raw_at) // (4 * D)
        self.base_rows = Map(nc, raw_at, "expert")("base_rows", [P, T, D])
        self.place = place
        place = Map(nc, 199040, "expert")
        self.slot = place("slot", [P, T, TOP], I32)
        self.weight = place("weight", [P, T, TOP])
        self.plan = place("plan", [1, PLAN], I32)
        self.index = place("index", [128, SLOT_BLOCKS], I32)
        self.late_at = place.at

    def load_raw(self, eng, gate_up_t, down_t, e, done):
        eng.dma_start(self.up_raw[:, :, :], gate_up_t[bass.ds(e, 1), :, :].rearrange("o p (k n) -> (o p) k n", n=2 * HID)).then_inc(done, 16)
        eng.dma_start(self.down_raw[:, 0:2, :], down_t[bass.ds(e, 1), 0:256, :].rearrange("o (k p) n -> (o p) k n", p=128)).then_inc(done, 16)
        eng.dma_start(self.down_raw[0:HROWS[2], 2, :], down_t[bass.ds(e, 1), 256:HID, :].rearrange("o p n -> (o p) n")).then_inc(done, 16)


PIECES = [((0, 3), ()), ((3, 6), ()), ((6, 8), (0,)), (None, (1, 2))]


def route_phase(nc, name, buffers, logits, gate_up_t, down_t):
    sem = lambda s: nc.alloc_semaphore(f"{name}_{s}")
    E = EXPERTS
    with ExitStack() as ctx:
        ps = lambda s, shape: ctx.enter_context(nc.psum_tensor(f"{name}_{s}", shape, F32))
        local = Map(nc, buffers.place.at, name)
        weight, slot_i, plan_i = buffers.weight, buffers.slot, buffers.plan
        lg = local("lg", [P, T, E])
        top = local("top", [P, T, E])
        top_at = local("top_at", [P, T, E], U32)
        peak = local("peak", [P, T, 1])
        total = local("total", [P, T, 1])
        pick = local("pick", [P, T, TOP])
        wsum = local("wsum", [P, T, 1])
        expert_i = local("expert_i", [P, T, E], I32)
        expert = local("expert", [P, T, E])
        hot = [local(f"hot{j}", [P, T, E]) for j in range(TOP)]
        both = local("both", [P, T, E])
        node_i = local("node_i", [P, T], I32)
        node_two = local("node_two", [P, T, TOP])
        square = local("square", [P, P], I32)
        below = local("below", [P, P])
        ones = local("ones", [P, P])
        place = local("place", [P, T, E])
        count = local("count", [P, T, E])
        start = local("start", [P, T + 1, E])
        steps_i = local("steps_i", [P, E, T - 1], I32)
        steps = local("steps", [P, E, T - 1])
        over = local("over", [P, E, T - 1])
        blocks = local("blocks", [P, E])
        first = local("first", [P, E + 1])
        offset = local("offset", [P, E])
        at = [local(f"at{j}", [P, T, E]) for j in range(TOP)]
        slot = local("slot", [P, T, TOP])
        block_i = local("block_i", [1, BLOCKS, E], I32)
        block_f = local("block_f", [1, BLOCKS, E])
        begun = local("begun", [1, BLOCKS, E])
        sign_i = local("sign_i", [1, E // 2, 2], I32)
        sign = local("sign", [1, E])
        signed = local("signed", [1, BLOCKS, E])
        plan = local("plan", [1, PLAN])
        first_slot_i = local("first_slot_i", [P, SLOT_BLOCKS + 1], I32)
        first_slot = local("first_slot", [P, SLOT_BLOCKS + 1])
        reached = local("reached", [P, T * TOP, SLOT_BLOCKS + 1])
        past = local("past", [P, T * TOP])
        in_block = local("in_block", [P, T * TOP])
        token_block = local("token_block", [P, T * TOP, SLOT_BLOCKS], F16)
        at_place = local("at_place", [P, T * TOP, 128], F16)
        place_no_i = local("place_no_i", [P, 128], I32)
        place_no = local("place_no", [P, 128])
        assert local.at <= 199040, local.at
        place_ps = ps("place_ps", [128, T * E])
        count_ps = ps("count_ps", [128, T * E])
        index_ps = ps("index_ps", [128, SLOT_BLOCKS])

        loaded = sem("loaded")
        made = sem("made")
        step = sem("step")
        expd = sem("expd")
        peak_ready = sem("peak_ready")
        both_ready = sem("both_ready")
        placed = sem("placed")
        map_ready = sem("map_ready")
        mapped = sem("mapped")
        raw_loaded = sem("raw_loaded")
        down_cleared = sem("down_cleared")
        w_high = sem("w_high")

        def split_low(eng, pieces):
            for p in pieces:
                ups, downs = PIECES[p]
                eng.wait_ge(w_high, p + 1)
                if ups:
                    ks = slice(*ups)
                    eng.tensor_tensor(buffers.up_w[:, 0, 1, ks, :], buffers.up_raw[:, ks, :],
                                      buffers.up_w[:, 0, 0, ks, :].bitcast(F32), ALU.subtract)
                for d in downs:
                    eng.tensor_tensor(buffers.down_w[:, 0, 1, d, :], buffers.down_raw[:, d, :],
                                      buffers.down_w[:, 0, 0, d, :].bitcast(F32), ALU.subtract)

        block = ctx.enter_context(nc.Block())

        @block.sync
        def _(sp):
            sp.dma_start(lg[:, :, :], logits).then_inc(loaded, 16)
            buffers.load_raw(sp, gate_up_t, down_t, 0, raw_loaded)

        @block.gpsimd
        def _(pool):
            pool.iota(first_slot_i[:, :], pattern=[[BLOCK, SLOT_BLOCKS + 1]], base=0, channel_multiplier=0).then_inc(made, 1)
            pool.iota(expert_i[:, :, :], pattern=[[0, T], [1, E]], base=0, channel_multiplier=0).then_inc(made, 1)
            pool.iota(node_i[:, :], pattern=[[P, T]], base=0, channel_multiplier=1).then_inc(made, 1)
            pool.iota(square[:, :], pattern=[[1, P]], base=0, channel_multiplier=-1).then_inc(made, 1)
            pool.iota(steps_i[:, :, :], pattern=[[0, E], [BLOCK, T - 1]], base=BLOCK, channel_multiplier=0).then_inc(made, 1)
            pool.iota(block_i[:, :, :], pattern=[[1, BLOCKS], [0, E]], base=0, channel_multiplier=0).then_inc(made, 1)
            pool.iota(sign_i[:, :, :], pattern=[[0, E // 2], [2, 2]], base=-1, channel_multiplier=0).then_inc(made, 1)
            pool.memset(ones[:, :], 1.0).then_inc(made, 1)
            pool.iota(place_no_i[:, :], pattern=[[1, 128]], base=0, channel_multiplier=0).then_inc(made, 1)
            split_low(pool, (0, 1, 3))

        @block.scalar
        def _(act):
            act.wait_ge(peak_ready, 1)
            act.activation(lg[:, :, :], lg[:, :, :], ACT.Exp).then_inc(expd, 1)
            act.wait_ge(raw_loaded, 48)
            act.wait_ge(down_cleared, 1)
            for ups, downs in PIECES:
                if ups:
                    ins = act.activation(buffers.up_w[:, 0, 0, slice(*ups), :], buffers.up_raw[:, slice(*ups), :], ACT.Copy)
                for d in downs:
                    ins = act.activation(buffers.down_w[:, 0, 0, d, :], buffers.down_raw[:, d, :], ACT.Copy)
                ins.then_inc(w_high, 1)

        @block.tensor
        def _(pe):
            pe.wait_ge(both_ready, 1)
            rhs = both[:, :, :].rearrange("p t e -> p (t e)")
            pe.matmul(place_ps[0:P, :], below[:, :], rhs, start=True, stop=True).then_inc(placed, 1)
            pe.matmul(count_ps[0:P, :], ones[:, :], rhs, start=True, stop=True).then_inc(placed, 1)
            pe.wait_ge(map_ready, 1)
            for i in range(T * TOP):
                ins = pe.matmul(index_ps[:, :], at_place[:, i, :], token_block[:, i, :], start=i == 0, stop=i == T * TOP - 1)
            ins.then_inc(mapped, 1)

        @block.vector
        def _(dve):
            n = [0]

            def then(ins, wait=True):
                n[0] += 1
                ins.then_inc(step, 1)
                if wait:
                    dve.wait_ge(step, n[0])

            dve.memset(buffers.down_raw[96:128, 2, :], 0.0).then_inc(down_cleared, 1)
            dve.wait_ge(made, 9)
            dve.wait_ge(loaded, 16)
            tte = lambda ap: ap.broadcast_to([P, T, E])
            then(dve.tensor_copy(first_slot[:, :], first_slot_i[:, :]), False)
            then(dve.tensor_copy(place_no[:, :], place_no_i[:, :]), False)
            for j in range(TOP):
                then(dve.tensor_copy(node_two[:, :, j], node_i[:, :]), False)
            then(dve.tensor_reduce(peak[:, :, 0], lg[:, :, :], AX.X, ALU.max))
            dve.tensor_tensor(lg[:, :, :], lg[:, :, :], tte(peak[:, :, :]), ALU.subtract).then_inc(peak_ready, 1)
            dve.wait_ge(expd, 1)
            then(dve.tensor_reduce(total[:, :, 0], lg[:, :, :], AX.X, ALU.add))
            then(dve.reciprocal(total[:, :, :], total[:, :, :]))
            then(dve.tensor_tensor(lg[:, :, :], lg[:, :, :], tte(total[:, :, :]), ALU.mult))
            for t in range(T):
                then(dve.max(top[:, t, :], lg[:, t, :]), t == T - 1)
            for t in range(T):
                then(dve.max_index(top_at[:, t, :], top[:, t, :], lg[:, t, :]), t == T - 1)
            then(dve.tensor_tensor(wsum[:, :, :], top[:, :, 0:1], top[:, :, 1:2], ALU.add))
            then(dve.reciprocal(wsum[:, :, :], wsum[:, :, :]))
            then(dve.tensor_tensor(weight[:, :, :], top[:, :, 0:TOP], wsum[:, :, :].broadcast_to([P, T, TOP]), ALU.mult))
            then(dve.tensor_copy(pick[:, :, :], top_at[:, :, 0:TOP]))
            then(dve.tensor_copy(expert[:, :, :], expert_i[:, :, :]))
            for j in range(TOP):
                then(dve.tensor_tensor(hot[j][:, :, :], expert[:, :, :], tte(pick[:, :, j:j + 1]), ALU.is_equal))
            then(dve.tensor_scalar(below[:, :], square[:, :], 0.0, None, ALU.is_gt))
            dve.tensor_tensor(both[:, :, :], hot[0][:, :, :], hot[1][:, :, :], ALU.add).then_inc(both_ready, 1)
            then(dve.tensor_copy(steps[:, :, :], steps_i[:, :, :]), False)
            then(dve.memset(start[:, 0, :], 0.0))
            dve.wait_ge(placed, 2)
            then(dve.tensor_copy(place[:, :, :], place_ps[0:P, :].rearrange("p (t e) -> p t e", e=E)), False)
            then(dve.tensor_copy(count[:, :, :], count_ps[0:P, :].rearrange("p (t e) -> p t e", e=E)))
            for t in range(T):
                then(dve.tensor_tensor(start[:, t + 1, :], start[:, t, :], count[:, t, :], ALU.add))
            then(dve.tensor_tensor(place[:, :, :], place[:, :, :], start[:, 0:T, :], ALU.add), False)
            then(dve.tensor_tensor(over[:, :, :], start[:, T, :].unsqueeze(2).broadcast_to([P, E, T - 1]), steps[:, :, :], ALU.is_gt))
            then(dve.tensor_reduce(blocks[:, :], over[:, :, :], AX.X, ALU.add))
            then(dve.tensor_scalar(blocks[:, :], blocks[:, :], 1.0, None, ALU.add))
            then(dve.memset(first[:, 0:1], 0.0))
            for e in range(E):
                then(dve.tensor_tensor(first[:, e + 1:e + 2], first[:, e:e + 1], blocks[:, e:e + 1], ALU.add))
            then(dve.tensor_scalar(offset[:, :], first[:, 0:E], float(BLOCK), None, ALU.mult))
            then(dve.tensor_tensor(place[:, :, :], place[:, :, :], offset[:, :].unsqueeze(1).broadcast_to([P, T, E]), ALU.add))
            for j in range(TOP):
                then(dve.tensor_tensor(at[j][:, :, :], place[:, :, :], hot[j][:, :, :], ALU.mult), j == TOP - 1)
            for j in range(TOP):
                then(dve.tensor_reduce(slot[:, :, j], at[j][:, :, :], AX.X, ALU.add), j == TOP - 1)
            then(dve.tensor_copy(slot_i[:, :, :], slot[:, :, :]), False)
            S = [P, T * TOP, SLOT_BLOCKS + 1]
            flat = slot[:, :, :].rearrange("p t j -> p (t j)")
            then(dve.tensor_tensor(reached[:, :, :], flat.unsqueeze(2).broadcast_to(S), first_slot[:, :].unsqueeze(1).broadcast_to(S), ALU.is_ge))
            then(dve.tensor_reduce(past[:, :], reached[:, :, :], AX.X, ALU.add))
            then(dve.tensor_scalar(past[:, :], past[:, :], -float(BLOCK), float(BLOCK), ALU.mult, ALU.add))
            then(dve.tensor_tensor(in_block[:, :], flat, past[:, :], ALU.add))
            then(dve.tensor_tensor(at_place[:, :, :], in_block[:, :].unsqueeze(2).broadcast_to([P, T * TOP, 128]),
                                   place_no[:, :].unsqueeze(1).broadcast_to([P, T * TOP, 128]), ALU.is_equal), False)
            then(dve.tensor_tensor(reached[:, :, 0:SLOT_BLOCKS], reached[:, :, 0:SLOT_BLOCKS], reached[:, :, 1:], ALU.subtract))
            dve.tensor_tensor(token_block[:, :, :], reached[:, :, 0:SLOT_BLOCKS],
                              node_two[:, :, :].rearrange("p t j -> p (t j)").unsqueeze(2).broadcast_to([P, T * TOP, SLOT_BLOCKS]),
                              ALU.mult).then_inc(map_ready, 1)
            then(dve.tensor_copy(block_f[:, :, :], block_i[:, :, :]))
            then(dve.tensor_tensor(begun[:, :, :], block_f[:, :, :], first[0:1, 0:E].unsqueeze(1).broadcast_to([1, BLOCKS, E]), ALU.is_ge))
            then(dve.memset(plan[:, :], 0.0))
            then(dve.tensor_reduce(plan[:, AT_EXPERT:AT_EXPERT + BLOCKS], begun[:, :, :], AX.X, ALU.add))
            then(dve.tensor_copy(sign[:, :], sign_i[:, :, :].rearrange("p a b -> p (a b)")))
            then(dve.memset(sign[:, 0:1], 0.0))
            then(dve.tensor_tensor(signed[:, :, :], begun[:, :, :], sign[:, :].unsqueeze(1).broadcast_to([1, BLOCKS, E]), ALU.mult))
            then(dve.tensor_reduce(plan[:, AT_SIDE + 1:AT_SIDE + 1 + BLOCKS], signed[:, :, :], AX.X, ALU.add))
            then(dve.tensor_copy(plan[:, AT_COUNT:AT_COUNT + E], blocks[0:1, :]))
            then(dve.tensor_copy(plan[:, AT_TOTAL:AT_TOTAL + 1], first[0:1, E:E + 1]))
            then(dve.tensor_scalar(plan[:, AT_REST:AT_REST + 1], first[0:1, E:E + 1], -1.0, float(SLOT_BLOCKS - 1), ALU.mult, ALU.add))
            then(dve.tensor_copy(plan_i[:, :], plan[:, :]), False)
            dve.wait_ge(mapped, 1)
            then(dve.tensor_copy(buffers.index[:, :], index_ps[:, :]), False)
            split_low(dve, (2,))


def expert_phase(nc, name, buffers, tokens, gate_up_t, down_t, base, results, base_loaded):
    sem = lambda s: nc.alloc_semaphore(f"{name}_{s}")
    E, KU, W2 = EXPERTS, K, 2 * HID
    with ExitStack() as ctx:
        ps = lambda s, shape: ctx.enter_context(nc.psum_tensor(f"{name}_{s}", shape, F32))
        local = buffers.place
        up_w, down_w, up_raw, down_raw, plan = buffers.up_w, buffers.down_w, buffers.up_raw, buffers.down_raw, buffers.plan
        xt = local("xt", [128, 2, K, BLOCK], F32R)
        gate = local("gate", [BLOCK, HID])
        hidden = local("hidden", [BLOCK, HK * 128])
        ht = local("ht", [128, 2, HK, BLOCK], F32R)
        y = local("y", [BLOCK, D])
        index = buffers.index
        index_now = local("index_now", [128, 1], I32)
        waits = local("waits", [128, 2])
        zeros = local("zeros", [128, 256])
        ident = local("ident", [128, 128])
        square = local("square", [128, 128], I32)
        assert local.at <= 199040, local.at
        x = Map(nc, buffers.late_at, name)("x", [BLOCK, 2, D])
        gate_ps = ps("gate_ps", [128, HID])
        up_ps = ps("up_ps", [128, HID])
        y_ps = [ps(f"y_ps{j}", [128, H]) for j in range(2)]
        turned = [ps(f"turned{r}", [128, 4, BLOCK]) for r in range(2)]
        ht_ps = ps("ht_ps", [128, HK, BLOCK])

        made = sem("made")
        ident_ready = sem("ident_ready")
        ht_cleared = sem("ht_cleared")
        raw_loaded = sem("raw_loaded")
        w_high = sem("w_high")
        w_ready = sem("w_ready")
        index_ready = sem("index_ready")
        gathered = sem("gathered")
        x_turned = sem("x_turned")
        xt_high = sem("xt_high")
        xt_ready = sem("xt_ready")
        gate_done = sem("gate_done")
        up_done = sem("up_done")
        once_dve = sem("once_dve")
        gate_ready = sem("gate_ready")
        hidden_ready = sem("hidden_ready")
        h_turned = sem("h_turned")
        ht_high = sem("ht_high")
        ht_ready = sem("ht_ready")
        down_ready = sem("down_ready")
        y_ready = sem("y_ready")
        y_stored = sem("y_stored")
        cleared = sem("cleared")

        block = ctx.enter_context(nc.Block())

        @block.sync
        def _(sp):
            sp.wait_ge(gathered, 16)
            with sp.Fori(0, E - 1) as before:
                sp.wait_ge(w_ready, 4 * before + 4)
                buffers.load_raw(sp, gate_up_t, down_t, before + 1, raw_loaded)
            sp.wait_ge(once_dve, 2)
            total = sp.value_load(plan[0:1, AT_TOTAL:AT_TOTAL + 1], min_val=E, max_val=BLOCKS)
            with sp.Fori(total + 1, SLOT_BLOCKS) as i:
                sp.dma_start(results[bass.ds(i * BLOCK, BLOCK), :].rearrange("p (r n) -> p r n", n=256),
                             zeros[:, :].unsqueeze(1).broadcast_to([128, D // 256, 256])).then_inc(cleared, 16)
            sp.wait_ge(w_ready, 4 * E)
            sp.dma_start(buffers.base_rows[:, 0:buffers.early, :],
                         base[0:buffers.early * P, :].rearrange("(t p) n -> p t n", p=P)).then_inc(base_loaded, 16)

        @block.gpsimd
        def _(pool):
            pool.iota(square[:, :], pattern=[[1, 128]], base=0, channel_multiplier=-1).then_inc(made, 1)
            pool.memset(waits[:, 1:2], 0.0).then_inc(made, 1)
            pool.wait_ge(made, 2)
            total = pool.value_load(plan[0:1, AT_TOTAL:AT_TOTAL + 1], min_val=E, max_val=BLOCKS)
            with pool.Fori(0, (total + 2) // 2) as pair:
                for side in range(2):
                    i = pair * 2 + side
                    pool.wait_ge(x_turned, i)
                    pool.tensor_copy(index_now[:, :], index[:, bass.ds(i, 1)]).then_inc(index_ready, 1)
                    pool.wait_ge(index_ready, i + 1)
                    pool.tensor_tensor(waits[:, 0:1], waits[:, 1:2], waits[:, 1:2], ALU.add)
                    pool.indirect_dma_start(x[:, side, :], None, tokens, bass.IndirectOffsetOnAxis(index_now[:, :], 0)).then_inc(gathered, 16)
                    pool.wait_ge(gathered, 16 * i + 16)
            rest = pool.value_load(plan[0:1, AT_REST:AT_REST + 1], min_val=1, max_val=SLOT_BLOCKS)
            pool.wait_ge(cleared, rest * 16)
            pool.wait_ge(y_stored, 16 * total + 16)

        @block.scalar
        def _(act):
            def split(e, side, p):
                ups, downs = PIECES[p]
                act.wait_ge(raw_loaded, 48 * e)
                if ups:
                    ins = act.activation(up_w[:, side, 0, slice(*ups), :], up_raw[:, slice(*ups), :], ACT.Copy)
                for d in downs:
                    ins = act.activation(down_w[:, side, 0, d, :], down_raw[:, d, :], ACT.Copy)
                ins.then_inc(w_high, 1)

            def xt_part(i):
                act.wait_ge(x_turned, i + 2)
                for r in range(2):
                    ins = act.activation(xt[:, 0, 4 * r:4 * r + 4, :], turned[r][:, :, :], ACT.Copy)
                ins.then_inc(xt_high, 1)

            def result(i):
                act.wait_ge(down_ready, i + 1)
                act.wait_ge(y_stored, 16 * i)
                for j in range(2):
                    ins = act.activation(y[:, j * H:(j + 1) * H], y_ps[j][:, :], ACT.Copy)
                ins.then_inc(y_ready, 1)
                act.wait_ge(y_ready, i + 1)
                act.dma_start(results[bass.ds(i * BLOCK, BLOCK), :], y[:, :]).then_inc(y_stored, 16)

            def one_block(i, spare):
                act.wait_ge(gate_done, i + 1)
                act.wait_ge(hidden_ready, i)
                act.activation(gate[:, :], gate_ps[:, :], ACT.Silu).then_inc(gate_ready, 1)
                spare(0)
                act.wait_ge(up_done, i + 1)
                xt_part(i + 1)
                spare(1)
                result(i)
                act.wait_ge(h_turned, i + 1)
                act.activation(ht[:, 0, :, :], ht_ps[:, :, :], ACT.Copy).then_inc(ht_high, 1)
                spare(2)

            def expert(e, side, last):
                mine = act.value_load(plan[0:1, bass.ds(AT_COUNT + e, 1)], min_val=1, max_val=T)
                with act.Fori(0, mine) as b:
                    def spare(n):
                        if not last:
                            with act.If(b == 0):
                                split(e + 1, 1 - side, n)
                            if n == 0:
                                with act.If(b == 1):
                                    split(e + 1, 1 - side, 3)

                    one_block(act.snap(count), spare)
                    act.reg_add(count, count, 1)
                if not last:
                    with act.If(mine <= 1):
                        split(e + 1, 1 - side, 3)

            xt_part(0)
            count = act.alloc_register(f"{name}_act_blocks")
            act.reg_mov(count, 0)
            with act.Fori(0, E // 2 - 1) as pair:
                for side in range(2):
                    expert(pair * 2 + side, side, False)
            expert(E - 2, 0, False)
            expert(E - 1, 1, True)
            total = act.snap(count)
            result(total)

        @block.vector
        def _(dve):
            def split(e, side, p):
                ups, downs = PIECES[p]
                dve.wait_ge(w_high, 4 * e + (p - 3))
                if ups:
                    ks = slice(*ups)
                    ins = dve.tensor_tensor(up_w[:, side, 1, ks, :], up_raw[:, ks, :], up_w[:, side, 0, ks, :].bitcast(F32), ALU.subtract)
                for d in downs:
                    ins = dve.tensor_tensor(down_w[:, side, 1, d, :], down_raw[:, d, :], down_w[:, side, 0, d, :].bitcast(F32), ALU.subtract)
                ins.then_inc(w_ready, 1)

            def xt_part(i):
                dve.wait_ge(xt_high, i + 1)
                for r in range(2):
                    ins = dve.tensor_tensor(xt[:, 1, 4 * r:4 * r + 4, :], turned[r][:, :, :],
                                            xt[:, 0, 4 * r:4 * r + 4, :].bitcast(F32), ALU.subtract)
                ins.then_inc(xt_ready, 1)

            def one_block(i, spare):
                dve.wait_ge(gate_ready, i + 1)
                dve.wait_ge(up_done, i + 1)
                dve.wait_ge(h_turned, i)
                dve.tensor_tensor(hidden[:, 0:HID], up_ps[:, :], gate[:, :], ALU.mult).then_inc(hidden_ready, 1)
                spare(0)
                xt_part(i + 1)
                spare(1)
                dve.wait_ge(ht_high, i + 1)
                dve.tensor_tensor(ht[:, 1, :, :], ht_ps[:, :, :], ht[:, 0, :, :].bitcast(F32), ALU.subtract).then_inc(ht_ready, 1)
                spare(2)

            def expert(e, side, last):
                mine = dve.value_load(plan[0:1, bass.ds(AT_COUNT + e, 1)], min_val=1, max_val=T)
                with dve.Fori(0, mine) as b:
                    def spare(n):
                        if not last:
                            with dve.If(b == 0):
                                split(e + 1, 1 - side, n)
                            if n == 0:
                                with dve.If(b == 1):
                                    split(e + 1, 1 - side, 3)

                    one_block(dve.snap(count), spare)
                    dve.reg_add(count, count, 1)
                if not last:
                    with dve.If(mine <= 1):
                        split(e + 1, 1 - side, 3)

            dve.sem_inc(w_ready, 4)
            dve.memset(hidden[:, HID:HK * 128], 0.0).then_inc(once_dve, 1)
            dve.memset(zeros[:, :], 0.0).then_inc(once_dve, 1)
            dve.memset(ht[:, :, :, :].bitcast(F32), 0.0).then_inc(ht_ready, 1)
            dve.wait_ge(made, 1)
            dve.tensor_scalar(ident[:, :], square[:, :], 0.0, None, ALU.is_equal).then_inc(ident_ready, 1)
            xt_part(0)
            count = dve.alloc_register(f"{name}_dve_blocks")
            dve.reg_mov(count, 0)
            with dve.Fori(0, E // 2 - 1) as pair:
                for side in range(2):
                    expert(pair * 2 + side, side, False)
            expert(E - 2, 0, False)
            expert(E - 1, 1, True)

        @block.tensor
        def _(pe):
            def turn_x(i):
                pe.wait_ge(gathered, 16 * i + 16)

                def turn(side):
                    for k in range(K):
                        ins = pe.transpose(turned[k // 4][:, k % 4, :], x[:, side, k * 128:(k + 1) * 128], ident[:, :])
                    ins.then_inc(x_turned, 1)

                if isinstance(i, int):
                    turn(i & 1)
                else:
                    for side in range(2):
                        with pe.If((i & 1) == side):
                            turn(side)

            def up(i):
                begun = pe.value_load(plan[0:1, bass.ds(AT_EXPERT + i, 1)], min_val=1, max_val=E)
                side = pe.value_load(plan[0:1, bass.ds(AT_SIDE + 1 + i, 1)], min_val=0, max_val=1)
                pe.wait_ge(w_ready, begun * 4)
                pe.wait_ge(xt_ready, i + 1)
                pe.wait_ge(hidden_ready, i)
                for out, c0, done in ((gate_ps, 0, gate_done), (up_ps, HID, up_done)):
                    for k in range(K):
                        high, low = (up_w[:, bass.ds(side, 1), part, k, c0:c0 + HID].rearrange("p o n -> p (o n)") for part in range(2))
                        pe.matmul(out[:, :], xt[:, 0, k, :], high, start=k == 0, stop=False)
                        pe.matmul(out[:, :], xt[:, 0, k, :], low, start=False, stop=False)
                        ins = pe.matmul(out[:, :], xt[:, 1, k, :], high, start=False, stop=k == K - 1)
                    ins.then_inc(done, 1)

            def down(i):
                side = pe.value_load(plan[0:1, bass.ds(AT_SIDE + i, 1)], min_val=0, max_val=1)
                pe.wait_ge(ht_ready, i + 1)
                pe.wait_ge(y_ready, i)
                for j in range(2):
                    for k in range(HK):
                        high, low = (down_w[:, bass.ds(side, 1), part, k, j * H:(j + 1) * H].rearrange("p o n -> p (o n)") for part in range(2))
                        pe.matmul(y_ps[j][:, :], ht[:, 0, k, :], high, start=k == 0, stop=False)
                        pe.matmul(y_ps[j][:, :], ht[:, 0, k, :], low, start=False, stop=False)
                        ins = pe.matmul(y_ps[j][:, :], ht[:, 1, k, :], high, start=False, stop=k == HK - 1)
                ins.then_inc(down_ready, 1)

            def turn_h(i):
                pe.wait_ge(hidden_ready, i + 1)
                for k in range(HK):
                    ins = pe.transpose(ht_ps[:, k, :], hidden[:, k * 128:(k + 1) * 128], ident[:, :])
                ins.then_inc(h_turned, 1)

            pe.wait_ge(once_dve, 1)
            pe.wait_ge(ident_ready, 1)
            pe.sem_inc(x_turned, 1)
            turn_x(0)
            total = pe.value_load(plan[0:1, AT_TOTAL:AT_TOTAL + 1], min_val=E, max_val=BLOCKS)
            with pe.Fori(0, total) as i:
                up(i)
                turn_x(i + 1)
                down(i)
                turn_h(i)
            down(total)


def combine_phase(nc, name, buffers, base, results, alpha, out, base_loaded):
    sem = lambda s: nc.alloc_semaphore(f"{name}_{s}")
    early = buffers.early
    with ExitStack() as ctx:
        local = Map(nc, 0, name)
        row = [[local(f"row{t}_{j}", [P, D]) for j in range(TOP)] for t in range(T)]
        scale = local("scale", [P, 1])
        scaled = local("scaled", [P, T, TOP])
        x = buffers.base_rows
        once = sem("once")
        scaled_ready = sem("scaled_ready")
        rest_loaded = sem("rest_loaded")
        gathered = [[sem(f"gathered{t}_{j}") for j in range(TOP)] for t in range(T)]
        added = sem("added")
        stored = sem("stored")
        block = ctx.enter_context(nc.Block())

        @block.sync
        def _(sp):
            sp.dma_start(scale[:, :], alpha.broadcast_to([P, 1])).then_inc(once, 16)
            sp.dma_start(x[:, early:T, :], base[early * P:N, :].rearrange("(t p) n -> p t n", p=P)).then_inc(rest_loaded, 16)

        @block.scalar
        def _(act):
            for t in range(T):
                act.wait_ge(added, TOP * (t + 1))
                act.dma_start(out[t * P:(t + 1) * P, :], x[:, t, :]).then_inc(stored, 16)
            act.wait_ge(stored, 16 * T)

        @block.gpsimd
        def _(pool):
            for t in range(T):
                for j in range(TOP):
                    pool.indirect_dma_start(row[t][j][:, :], None, results,
                                            bass.IndirectOffsetOnAxis(buffers.slot[:, t, j:j + 1], 0),
                                            element_offset=BLOCK * D).then_inc(gathered[t][j], 16)

        @block.vector
        def _(dve):
            dve.wait_ge(once, 16)
            dve.tensor_scalar(scale[:, :], scale[:, :], -0.5, 2.0, ALU.max, ALU.min).then_inc(scaled_ready, 1)
            dve.wait_ge(scaled_ready, 1)
            dve.tensor_scalar(scaled[:, :, :], buffers.weight[:, :, :], scale[:, 0:1], None, ALU.mult).then_inc(scaled_ready, 1)
            dve.wait_ge(scaled_ready, 2)
            dve.wait_ge(base_loaded, 16)
            for t in range(T):
                if t == early:
                    dve.wait_ge(rest_loaded, 16)
                for j in range(TOP):
                    dve.wait_ge(gathered[t][j], 16)
                    if j:
                        dve.wait_ge(added, TOP * t + j)
                    dve.scalar_tensor_tensor(x[:, t, :], row[t][j][:, :], scaled[:, t, j:j + 1], x[:, t, :],
                                             ALU.mult, ALU.add).then_inc(added, 1)


def gnn_ffn_gnn_moe_kernel(nc, x, edges_src_cols, edges_dst_cols, edges_dst_chunks, w_self0, w_neigh0, bias0,
                           w_self1, w_neigh1, bias1, train1, train2, ffn_bias, att_w, att_a, norm_w, router_t,
                           gate_up_t, down_t, alpha, out):
    dram = lambda name, shape, dt=F32: nc.dram_tensor(name, shape, dt, kind="Internal").ap()
    counts_by_src = dram("counts_by_src", [T, P, T, P])
    counts_by_dst = dram("counts_by_dst", [T, P, T, P])
    deg_inv = dram("deg_inv", [P, T])
    w_ffn = dram("w_ffn", [D, D])
    xt0 = dram("xt0", [T, 128, 2, K, P])
    xt1 = dram("xt1", [T, 128, 2, K, P])
    h0 = dram("h0", [N, D])
    x1 = dram("x1", [N, D])
    x2 = dram("x2", [N, D])
    base = dram("base", [N, D])
    tokens = dram("tokens", [N, D])
    logits = dram("logits", [P, T, EXPERTS])
    results = dram("results", [SLOT_BLOCKS * BLOCK, D])

    place = lambda name, shape, dt, at: nc.alloc_sbuf_tensor_at(name, shape, dt, offset=BASE + at)
    raw = place("raw", [128, K, D], F32, RAW_AT)
    wh = place("wh", [128, K, D], F32R, WH_AT)
    wl = place("wl", [128, K, D], F32R, WL_AT)
    gh = place("gh", [128, T, D], F32R, GH_AT)
    gl = place("gl", [128, T, D], F32R, GL_AT)

    counts = place("counts", [P, T, P], F32R, HANDED_AT)
    scores = place("scores", [P, T, 2], F32, HANDED_AT)
    raw_loaded = nc.alloc_semaphore("raw_loaded")
    counts_loaded = [nc.alloc_semaphore(f"counts_loaded{i}") for i in range(2)]
    base_loaded = nc.alloc_semaphore("base_loaded")

    def clear_semaphores(before):
        nc.clear_and_free_semaphores(nc.allocated_since(before))
        nc.all_engine_barrier()

    before = nc.snapshot_sems()
    graph = GraphBuffers(nc)
    prepare_phase(nc, "prepare", graph, edges_dst_chunks, edges_src_cols, edges_dst_cols, w_neigh0)
    count_project_phase(nc, "neigh0", graph, x, xt0, wh, wl, gh, gl, counts_by_src, counts_by_dst, deg_inv,
                        (counts, counts_by_src, counts_loaded[0]))
    aggregate_phase(nc, "self0", xt0, counts, counts_loaded[0], counts_by_src, deg_inv, bias0, None, h0,
                    raw, wh, wl, gh, gl, raw_loaded, 0, w_neigh1, own_w=w_self0, unfold=(train1, train2, w_ffn))
    project_phase(nc, "neigh1", h0, xt1, raw, wh, wl, gh, gl, raw_loaded, 1, w_self1,
                  normalize=False, relu=True, result="split", counts_ahead=(counts, counts_by_src, counts_loaded[1]))
    aggregate_phase(nc, "self1", xt1, counts, counts_loaded[1], counts_by_src, deg_inv, bias1, x, x1,
                    raw, wh, wl, gh, gl, raw_loaded, 2, w_ffn)
    clear_semaphores(before)
    before = nc.snapshot_sems()
    project_phase(nc, "ffn", x1, None, raw, wh, wl, None, None, raw_loaded, 3, att_w,
                  normalize=True, relu=False, result="residual", bias=ffn_bias, out=x2)
    project_phase(nc, "att_h", x2, None, raw, wh, wl, gh, gl, raw_loaded, 4, None,
                  normalize=True, relu=False, result="scores", score_w=att_a, scores=scores)
    attention_phase(nc, "att", x2, counts_by_dst, scores, norm_w, router_t, gh, gl, base, tokens, logits)
    experts = ExpertBuffers(nc)
    route_phase(nc, "route", experts, logits, gate_up_t, down_t)
    clear_semaphores(before)
    expert_phase(nc, "experts", experts, tokens, gate_up_t, down_t, base, results, base_loaded)
    combine_phase(nc, "combine", experts, base, results, alpha, out, base_loaded)


_NAMES = ["x", "edges_src_cols", "edges_dst_cols", "edges_dst_chunks", "w_self0", "w_neigh0", "bias0",
          "w_self1", "w_neigh1", "bias1", "train1", "train2", "ffn_bias", "att_w", "att_a", "norm_w", "router_t",
          "gate_up_t", "down_t", "alpha"]


def _layout(inputs):
    a = {k: np.asarray(v) for k, v in inputs.items()}
    pad = np.full(CHUNKS * CHUNK - a["src"].shape[0], NONE, a["src"].dtype)
    src = np.concatenate([a["src"], pad])
    dst = np.concatenate([a["dst"], pad])
    cols = lambda e: e.reshape(TILES * CHUNKS, EDGE_TILE).T
    train1 = lambda g: np.repeat(g[0].transpose(2, 1, 0).reshape(32, 128), 16, axis=0)
    train2 = lambda g: np.tile(g[:, :, 0, :].transpose(2, 0, 1).reshape(16, 64), (8, 1))
    row = lambda v: v.reshape(1, -1)
    return dict(
        x=a["x"], edges_src_cols=cols(src), edges_dst_cols=cols(dst), edges_dst_chunks=dst.reshape(CHUNKS, CHUNK),
        w_self0=a["L0_gnn_W_self0"], w_neigh0=a["L0_gnn_W_neigh0"], bias0=row(a["L0_gnn_b0"]),
        w_self1=a["L0_gnn_W_self1"], w_neigh1=a["L0_gnn_W_neigh1"], bias1=row(a["L0_gnn_b1"]),
        train1=np.stack([train1(a["L0_ffn_G1_R"]), train1(a["L0_ffn_G1_I"])]),
        train2=np.stack([train2(a["L0_ffn_G2_R"]), train2(a["L0_ffn_G2_I"])]),
        ffn_bias=row(np.concatenate([a["L0_ffn_bias_real"], a["L0_ffn_bias_imag"]])),
        att_w=a["L1_gnn_W"], att_a=row(a["L1_gnn_a"]), norm_w=row(a["L1_ffn_norm_weight"]),
        router_t=a["L1_ffn_router_weight"].reshape(EXPERTS, K, 128).transpose(2, 1, 0).reshape(128, K * EXPERTS),
        gate_up_t=a["L1_ffn_gate_up_weight"].reshape(EXPERTS, 2 * HID, K, 128).transpose(0, 3, 2, 1).reshape(EXPERTS, 128, K * 2 * HID),
        down_t=a["L1_ffn_down_weight"].transpose(0, 2, 1),
        alpha=a["L1_ffn_residual_alpha"].reshape(1, 1))


def kernel(**inputs):
    import concourse.bacc as _bacc
    from concourse import mybir as _mybir
    from concourse.bass_utils import run_bass_kernel_spmd as _run

    nc = _bacc.Bacc("TRN2", target_bir_lowering=False, num_devices=1)
    data = _layout(inputs)
    arrays, args = {}, []
    for name in _NAMES:
        a = np.ascontiguousarray(data[name])
        arrays[f"in_{name}"] = a
        args.append(nc.dram_tensor(f"in_{name}", a.shape, _mybir.dt.from_np(a.dtype), kind="ExternalInput").ap())
    args.append(nc.dram_tensor("out_rows", (N, D), _mybir.dt.float32, kind="ExternalOutput").ap())
    gnn_ffn_gnn_moe_kernel(nc, *args)
    r = _run(nc, [arrays], core_ids=[0])
    return r.results[0]["out_rows"]
```
